# Optimizing a Trainium2 kernel written in Bass

```python
import numpy as np
import jax
import jax.numpy as jnp

def _softmax(x, axis=-1):
    return jax.nn.softmax(x, axis=axis)

def _gelu(x):
    return jax.nn.gelu(x, approximate=True)

def _silu(x):
    return jax.nn.silu(x)

def _sigmoid(x):
    return jax.nn.sigmoid(x)

def _layernorm(x, axis=-1, eps=1e-05):
    m = jnp.mean(x, axis=axis, keepdims=True)
    v = jnp.var(x, axis=axis, keepdims=True)
    return (x - m) / jnp.sqrt(v + eps)

def _scatter_add(tgt, idx, src, axis=0):
    return tgt.at[idx].add(src)

def _segment_sum(src, seg, n):
    return jax.ops.segment_sum(src, seg, n)
kernel_name = 'mk_adj_resnorm_d4_adj_r2_3e146f'

def setup_inputs(seed: int=0):
    np.random.seed(seed)
    _w = jnp.asarray

    def _rec_inputs():
        import jax
        import jax.numpy as jnp
        _gk = jax.random.key(seed)
        x = 7.22e-05 + 1 * jax.random.normal(jax.random.fold_in(_gk, 1), (32, 256, 256), jnp.float32)
        _a = jax.random.bernoulli(jax.random.fold_in(_gk, 2), 0.0078125, (256, 256))
        _a = jnp.logical_or(_a, jnp.swapaxes(_a, -1, -2))
        _a = jnp.logical_or(_a, jnp.eye(256, dtype=bool))
        adj = _a.astype(jnp.int32)
        return (x, adj)
    x, adj = _rec_inputs()

    def _L0_gnn_setup():
        import jax, jax.numpy as jnp
        import numpy as np
        LEAKY_ALPHA = 0.01
        NEG_INF = -1000000000.0
        LN_EPS = 1e-05

        def _gat_heads(x, adj, W, a):
            O = W.shape[-1]
            Wh = jnp.einsum('bnf,hfo->bhno', x, W)
            f1 = jnp.einsum('bhno,ho->bhn', Wh, a[:, :O])
            f2 = jnp.einsum('bhno,ho->bhn', Wh, a[:, O:])
            e = f1[:, :, :, None] + f2[:, :, None, :]
            e = jnp.where(e > 0, e, LEAKY_ALPHA * e)
            e = jnp.where(adj[None, None] > 0, e, NEG_INF)
            attn = jax.nn.softmax(e, axis=-1)
            return jnp.einsum('bhnm,bhmo->bhno', attn, Wh)
        key = jax.random.key(seed)
        ks = jax.random.split(key, 10)
        B, N, F_in, F_hid, H, F_out, D_ff = (8, 1024, 256, 256, 4, 256, 256)
        s = 0.05
        return {'enc_inputs': jax.random.normal(ks[0], (B, N, F_in), jnp.float32), 'adj': jax.random.randint(ks[1], (N, N), 0, 2, jnp.int32), 'W_heads': jax.random.normal(ks[2], (H, F_in, F_hid), jnp.float32) * s, 'a_heads': jax.random.normal(ks[3], (H, 2 * F_hid), jnp.float32) * s, 'W_out': jax.random.normal(ks[4], (H * F_hid, F_out), jnp.float32) * s, 'a_out': jax.random.normal(ks[5], (2 * F_out,), jnp.float32) * s, 'w1': jax.random.normal(ks[6], (F_out, D_ff), jnp.float32) * s, 'b1': jnp.zeros((D_ff,), jnp.float32), 'w2': jax.random.normal(ks[7], (D_ff, F_out), jnp.float32) * s, 'b2': jnp.zeros((F_out,), jnp.float32), 'ln_gamma': jnp.ones((F_out,), jnp.float32), 'ln_beta': jnp.zeros((F_out,), jnp.float32)}
    _L0_gnn_all = _L0_gnn_setup()
    _L0_gnn_in = {k: v for k, v in _L0_gnn_all.items() if k in ('W_heads', 'a_heads', 'W_out', 'a_out', 'w1', 'b1', 'w2', 'b2', 'ln_gamma', 'ln_beta')}
    del _L0_gnn_all

    def _L1_gnn_setup():
        import jax, jax.numpy as jnp
        import numpy as np
        B, K, DIN, DOUT = (32, 64, 256, 256)
        key = jax.random.key(seed)
        k1, k2, k3, k4 = jax.random.split(key, 4)
        x = jax.random.normal(k1, (B, K, DIN), dtype=jnp.float32)
        adj = jax.random.randint(k2, (K, K), 0, 2, dtype=jnp.int32)
        W = jax.random.normal(k3, (DOUT, 2 * DIN), dtype=jnp.float32) * 0.02
        b = jax.random.normal(k4, (DOUT,), dtype=jnp.float32) * 0.02
        return {'x': x, 'adj': adj, 'W': W, 'b': b}
    _L1_gnn_all = _L1_gnn_setup()
    _L1_gnn_in = {k: v for k, v in _L1_gnn_all.items() if k in ('W', 'b')}
    del _L1_gnn_all

    def _L2_gnn_setup():
        import jax, jax.numpy as jnp
        import numpy as np
        D_MODEL = 256
        NUM_HEADS = 8
        D_HEAD = D_MODEL // NUM_HEADS
        B, N = (4, 1024)
        key = jax.random.key(seed)
        ks = jax.random.split(key, 10)
        s = 1.0 / np.sqrt(D_MODEL)
        inp = {'h': jax.random.normal(ks[0], (B, N, D_MODEL), dtype=jnp.float32), 'adj': jax.random.randint(ks[1], (N, N), 0, 2, dtype=jnp.int32), 'Wq': jax.random.uniform(ks[2], (D_MODEL, D_MODEL), jnp.float32, -s, s), 'bq': jax.random.uniform(ks[3], (D_MODEL,), jnp.float32, -s, s), 'Wk': jax.random.uniform(ks[4], (D_MODEL, D_MODEL), jnp.float32, -s, s), 'bk': jax.random.uniform(ks[5], (D_MODEL,), jnp.float32, -s, s), 'Wv': jax.random.uniform(ks[6], (D_MODEL, D_MODEL), jnp.float32, -s, s), 'bv': jax.random.uniform(ks[7], (D_MODEL,), jnp.float32, -s, s), 'Wo': jax.random.uniform(ks[8], (D_MODEL, D_MODEL), jnp.float32, -s, s), 'bo': jax.random.uniform(ks[9], (D_MODEL,), jnp.float32, -s, s)}
        return inp
    _L2_gnn_all = _L2_gnn_setup()
    _L2_gnn_in = {k: v for k, v in _L2_gnn_all.items() if k in ('Wq', 'bq', 'Wk', 'bk', 'Wv', 'bv', 'Wo', 'bo')}
    del _L2_gnn_all

    def _L3_gnn_setup():
        import jax, jax.numpy as jnp
        import numpy as np
        B, K, DIN, DOUT = (32, 64, 256, 256)
        key = jax.random.key(seed)
        k1, k2, k3, k4 = jax.random.split(key, 4)
        x = jax.random.normal(k1, (B, K, DIN), dtype=jnp.float32)
        adj = jax.random.randint(k2, (K, K), 0, 2, dtype=jnp.int32)
        W = jax.random.normal(k3, (DOUT, 2 * DIN), dtype=jnp.float32) * 0.02
        b = jax.random.normal(k4, (DOUT,), dtype=jnp.float32) * 0.02
        return {'x': x, 'adj': adj, 'W': W, 'b': b}
    _L3_gnn_all = _L3_gnn_setup()
    _L3_gnn_in = {k: v for k, v in _L3_gnn_all.items() if k in ('W', 'b')}
    del _L3_gnn_all
    return {'x': x, 'adj': adj, 'L0_gnn_W_heads': _L0_gnn_in['W_heads'], 'L0_gnn_a_heads': _L0_gnn_in['a_heads'], 'L0_gnn_W_out': _L0_gnn_in['W_out'], 'L0_gnn_a_out': _L0_gnn_in['a_out'], 'L0_gnn_w1': _L0_gnn_in['w1'], 'L0_gnn_b1': _L0_gnn_in['b1'], 'L0_gnn_w2': _L0_gnn_in['w2'], 'L0_gnn_b2': _L0_gnn_in['b2'], 'L0_gnn_ln_gamma': _L0_gnn_in['ln_gamma'], 'L0_gnn_ln_beta': _L0_gnn_in['ln_beta'], 'L1_gnn_W': _L1_gnn_in['W'], 'L1_gnn_b': _L1_gnn_in['b'], 'L2_gnn_Wq': _L2_gnn_in['Wq'], 'L2_gnn_bq': _L2_gnn_in['bq'], 'L2_gnn_Wk': _L2_gnn_in['Wk'], 'L2_gnn_bk': _L2_gnn_in['bk'], 'L2_gnn_Wv': _L2_gnn_in['Wv'], 'L2_gnn_bv': _L2_gnn_in['bv'], 'L2_gnn_Wo': _L2_gnn_in['Wo'], 'L2_gnn_bo': _L2_gnn_in['bo'], 'L3_gnn_W': _L3_gnn_in['W'], 'L3_gnn_b': _L3_gnn_in['b']}

def reference(x, adj, L0_gnn_W_heads, L0_gnn_a_heads, L0_gnn_W_out, L0_gnn_a_out, L0_gnn_w1, L0_gnn_b1, L0_gnn_w2, L0_gnn_b2, L0_gnn_ln_gamma, L0_gnn_ln_beta, L1_gnn_W, L1_gnn_b, L2_gnn_Wq, L2_gnn_bq, L2_gnn_Wk, L2_gnn_bk, L2_gnn_Wv, L2_gnn_bv, L2_gnn_Wo, L2_gnn_bo, L3_gnn_W, L3_gnn_b):
    import jax
    import jax.numpy as jnp

    def _L0_gnn_ref(enc_inputs, adj, W_heads, a_heads, W_out, a_out, w1, b1, w2, b2, ln_gamma, ln_beta):
        import jax, jax.numpy as jnp
        import numpy as np
        LEAKY_ALPHA = 0.01
        NEG_INF = -1000000000.0
        LN_EPS = 1e-05

        def _gat_heads(x, adj, W, a):
            O = W.shape[-1]
            Wh = jnp.einsum('bnf,hfo->bhno', x, W)
            f1 = jnp.einsum('bhno,ho->bhn', Wh, a[:, :O])
            f2 = jnp.einsum('bhno,ho->bhn', Wh, a[:, O:])
            e = f1[:, :, :, None] + f2[:, :, None, :]
            e = jnp.where(e > 0, e, LEAKY_ALPHA * e)
            e = jnp.where(adj[None, None] > 0, e, NEG_INF)
            attn = jax.nn.softmax(e, axis=-1)
            return jnp.einsum('bhnm,bhmo->bhno', attn, Wh)
        B, N, _ = enc_inputs.shape
        h = jax.nn.elu(_gat_heads(enc_inputs, adj, W_heads, a_heads))
        h = jnp.transpose(h, (0, 2, 1, 3)).reshape(B, N, -1)
        out = _gat_heads(h, adj, W_out[None], a_out[None])[:, 0]
        out = jax.nn.elu(out)
        ffn = jnp.maximum(out @ w1 + b1, 0.0) @ w2 + b2
        y = ffn + out
        mu = jnp.mean(y, axis=-1, keepdims=True)
        var = jnp.var(y, axis=-1, keepdims=True)
        return (y - mu) / jnp.sqrt(var + LN_EPS) * ln_gamma + ln_beta

    def _L1_gnn_ref(x, adj, W, b):
        import jax, jax.numpy as jnp
        import numpy as np
        B, K, DIN, DOUT = (32, 64, 256, 256)
        Din = x.shape[-1]
        Wi, Wj = (W[:, :Din], W[:, Din:])
        mi = jnp.einsum('bkd,od->bko', x, Wi)
        mj = jnp.einsum('bkd,od->bko', x, Wj)
        a = adj.astype(x.dtype)
        deg = a.sum(axis=1)
        out = deg[None, :, None] * (mi + b) + jnp.einsum('ij,bjo->bio', a, mj)
        return out

    def _L2_gnn_ref(h, adj, Wq, bq, Wk, bk, Wv, bv, Wo, bo):
        import jax, jax.numpy as jnp
        import numpy as np
        D_MODEL = 256
        NUM_HEADS = 8
        D_HEAD = D_MODEL // NUM_HEADS
        B, N = (4, 1024)
        b, n, _ = h.shape

        def split_heads(x):
            return x.reshape(b, n, NUM_HEADS, D_HEAD).transpose(0, 2, 1, 3)
        q = split_heads(h @ Wq.T + bq)
        k = split_heads(h @ Wk.T + bk)
        v = split_heads(h @ Wv.T + bv)
        scale = 1.0 / np.sqrt(D_HEAD)
        scores = jnp.einsum('bhqd,bhkd->bhqk', q, k) * scale
        mask = (adj == 0)[None, None, :, :]
        scores = jnp.where(mask, -jnp.inf, scores)
        attn = jax.nn.softmax(scores, axis=-1)
        out = jnp.einsum('bhqk,bhkd->bhqd', attn, v)
        out = out.transpose(0, 2, 1, 3).reshape(b, n, D_MODEL)
        return out @ Wo.T + bo

    def _L3_gnn_ref(x, adj, W, b):
        import jax, jax.numpy as jnp
        import numpy as np
        B, K, DIN, DOUT = (32, 64, 256, 256)
        Din = x.shape[-1]
        Wi, Wj = (W[:, :Din], W[:, Din:])
        mi = jnp.einsum('bkd,od->bko', x, Wi)
        mj = jnp.einsum('bkd,od->bko', x, Wj)
        a = adj.astype(x.dtype)
        deg = a.sum(axis=1)
        out = deg[None, :, None] * (mi + b) + jnp.einsum('ij,bjo->bio', a, mj)
        return out
    x = _layernorm(x + _L0_gnn_ref(x, adj, L0_gnn_W_heads, L0_gnn_a_heads, L0_gnn_W_out, L0_gnn_a_out, L0_gnn_w1, L0_gnn_b1, L0_gnn_w2, L0_gnn_b2, L0_gnn_ln_gamma, L0_gnn_ln_beta), axis=-1)
    x = _layernorm(x + _L1_gnn_ref(x, adj, L1_gnn_W, L1_gnn_b), axis=-1)
    x = _layernorm(x + _L2_gnn_ref(x, adj, L2_gnn_Wq, L2_gnn_bq, L2_gnn_Wk, L2_gnn_bk, L2_gnn_Wv, L2_gnn_bv, L2_gnn_Wo, L2_gnn_bo), axis=-1)
    x = _layernorm(x + _L3_gnn_ref(x, adj, L3_gnn_W, L3_gnn_b), axis=-1)
    return x

_drawn_inputs = setup_inputs


def setup_inputs(seed=0):
    import zlib

    import numpy as np

    out = dict(_drawn_inputs(seed))
    spreads = {'L0_gnn_b1': (0.0, 0.1),
     'L0_gnn_b2': (0.0, 0.1),
     'L0_gnn_ln_gamma': (1.0, 0.2),
     'L0_gnn_ln_beta': (0.0, 0.1)}
    factors = {'L2_gnn_bq': 39.446, 'L2_gnn_bk': 64.0, 'L2_gnn_bv': 2.961}
    for name, (base, spread) in spreads.items():
        noise = np.random.default_rng([zlib.crc32(name.encode()), seed]).standard_normal(out[name].shape)
        drawn = base * np.exp(spread * noise) if base else spread * noise
        out[name] = jnp.asarray(drawn.astype(out[name].dtype))
    for name, factor in factors.items():
        out[name] = (out[name] * factor).astype(out[name].dtype)
    return out
```

```python
from contextlib import ExitStack

import numpy as np

import concourse.bass as bass
from concourse import mybir

P = 128
F32 = mybir.dt.float32
F32R = mybir.dt.float32r
I32 = mybir.dt.int32
ALU = mybir.AluOpType
ACT = mybir.ActivationFunctionType
AX = mybir.AxisListType

GAT_MASK = -1e11
ATT_MASK = -1e30
SLOPE = 0.01
EPS = 1e-5

TILES_1 = ["wh00", "wh01", "wh10", "wh11", "f",
           "e0", "t0", "e1", "av0", "t1", "e2", "av1", "t2", "e3", "av2", "t3", "av3"]
TILES_2 = ["wh0", "wh1", "f", "e", "t", "av", "hid", "y", "xt", "m0", "m1", "a"]
TILES_3 = ["xt", "q", "k", "v", "s0", "s1", "s2", "t0", "s3", "s4", "t1", "s5", "t2", "s6", "t3", "t4",
           "s7", "t5", "o0", "t6", "t7", "o1", "o", "x3t", "m0", "m1", "a"]


class Banks:

    def __init__(self, ctx, nc, name, tiles, n):
        self.tiles, self.n = tiles, n
        self.bank = [ctx.enter_context(nc.psum_tensor(f"{name}_bank{r}", [P, 512], F32)) for r in range(n)]
        self.full = [ctx.enter_context(nc.semaphore(f"{name}_full{r}")) for r in range(n)]
        self.read = [ctx.enter_context(nc.semaphore(f"{name}_read{r}")) for r in range(n)]

    def ring(self, tile):
        i = self.tiles.index(tile)
        r = i % self.n
        return r, len(range(r, i, self.n)), len(range(r, len(self.tiles), self.n))

    def ap(self, tile):
        return self.bank[self.ring(tile)[0]]

    def half(self, tile):
        return self.ap(tile)[:].rearrange("p (t n) -> p t n", t=2)

    def filled(self, tile, b):
        r, use, per = self.ring(tile)
        return self.full[r], b * per + (use + 1)

    def was_read(self, tile, b):
        r, use, per = self.ring(tile)
        return self.read[r], b * per + (use + 1)

    def vacant(self, tile, b):
        r, use, per = self.ring(tile)
        return self.read[r], b * per + use

    def wait_read(self, eng, b, *tiles, into):
        r, use, _ = self.ring(into)
        counts = {r: use}
        for tile in tiles:
            r, use, _ = self.ring(tile)
            counts[r] = max(counts.get(r, 0), use + 1)
        for r, count in counts.items():
            wait(eng, (self.read[r], b * len(range(r, len(self.tiles), self.n)) + count))


def wait(eng, sem_value):
    sem, value = sem_value
    if not isinstance(value, int) or value > 0:
        eng.wait_ge(sem, value)


def build(nc, x, xt, adj, adjt, w_heads, a_heads, w_out, a_out, w1, b1, w2, b2, gamma, beta,
          l1_wt, l1_b, wq_t, bq, wk_t, bk, wv_t, bv, wo_t, bo, l3_wt, l3_b, ident_d, select_d, out):
    B, N, D = x.shape
    H = w_heads.shape[0]
    HM, DH = 8, 32
    PT3 = 6
    T = N // P
    K = D // P
    KH = H * D // P
    assert T == 2 and K == 2 and D == HM * DH and B >= 4
    SCALE = float(np.float32(1.0) / np.sqrt(np.float32(DH)))

    with ExitStack() as ctx:
        def sb(name, shape, dt=F32):
            return ctx.enter_context(nc.sbuf_tensor(name, shape, dt))

        def sem(name):
            return ctx.enter_context(nc.semaphore(name))

        wh_h, wh_l = sb("wh_h", [P, K, H * D], F32R), sb("wh_l", [P, K, H * D], F32R)
        wa_h, wa_l = sb("wa_h", [P, K, P], F32R), sb("wa_l", [P, K, P], F32R)
        l1_h, l1_l = sb("l1_h", [P, K, 2 * D], F32R), sb("l1_l", [P, K, 2 * D], F32R)
        l3_h, l3_l = sb("l3_h", [P, K, 2 * D], F32R), sb("l3_l", [P, K, 2 * D], F32R)
        qkv_h, qkv_l = sb("qkv_h", [P, 3, K, D], F32R), sb("qkv_l", [P, 3, K, D], F32R)
        wout = sb("wout", [P, KH, D + 4])
        w1_s, w2_s, wo_s = sb("w1_s", [P, K, D]), sb("w2_s", [P, K, D]), sb("wo_s", [P, K, D])
        ident = sb("ident_s", [P, P])
        select = sb("select_s", [P, 4])
        adjt_r = sb("adjt_r", [P, T, N], F32R)
        gat_mask, att_mask = sb("gat_mask", [P, T, N]), sb("att_mask", [P, T, N])
        deg = sb("deg", [P, T])
        rows = sb("rows", [P, 7, D])
        GAMMA, BETA, B2, BO, BV, L1B, L3B = range(7)
        l1_db, l3_db = sb("l1_db", [P, T, D]), sb("l3_db", [P, T, D])
        b1_c, bq_c, bk_c = sb("b1_c", [P, K]), sb("bq_c", [P, K]), sb("bk_c", [P, K])
        minus_half = sb("minus_half", [P, T])

        xt_s = sb("xt_s", [P, K, N])
        xt_h, xt_l = sb("xt_h", [P, K, N], F32R), sb("xt_l", [P, K, N], F32R)
        feats = sb("feats", [P, T, H * D])
        f_hi, f_tmp, f_sel = sb("f_hi", [P, N], F32R), sb("f_tmp", [P, N]), sb("f_sel", [P, N])
        g_query, g_key = sb("g_query", [P, N], F32R), sb("g_key", [P, N], F32R)
        e1, p1, pt1 = sb("e1", [P, 2, T, N]), sb("p1", [P, 2, T, N]), sb("pt1", [P, 2, T, N])
        max1, neg1, nmax1 = sb("max1", [P, 2, T]), sb("neg1", [P, 2, T]), sb("nmax1", [P, 2, T])
        sum1, inv1 = sb("sum1", [P, 2, T]), sb("inv1", [P, 2, T])
        elu1 = sb("elu1", [P, 2, K, N])
        heads_t = sb("heads_t", [P, KH, N])
        x_s = sb("x_s", [P, T, D])
        feats2 = sb("feats2", [P, T, D + 4])
        f2_hi, f2_tmp, f2_sel = sb("f2_hi", [4, N], F32R), sb("f2_tmp", [4, N]), sb("f2_sel", [4, N])
        g2_query, g2_key = sb("g2_query", [4, N], F32R), sb("g2_key", [4, N], F32R)
        e2, p2, pt2 = sb("e2", [P, T, N]), sb("p2", [P, T, N]), sb("pt2", [P, T, N])
        max2, neg2, nmax2 = sb("max2", [P, T]), sb("neg2", [P, T]), sb("nmax2", [P, T])
        sum2, inv2 = sb("sum2", [P, T]), sb("inv2", [P, T])
        elu2, out2_t, hid = sb("elu2", [P, K, N]), sb("out2_t", [P, K, N]), sb("hid", [P, K, N])
        y, x1, x2 = sb("y", [P, T, D]), sb("x1", [P, T, D]), sb("x2", [P, T, D])
        x1b = sb("x1b", [P, T, D])
        x1t_h, x1t_l = sb("x1t_h", [P, K, N], F32R), sb("x1t_l", [P, K, N], F32R)
        mj1_h, mj1_l = sb("mj1_h", [P, T, D], F32R), sb("mj1_l", [P, T, D], F32R)
        x2b = sb("x2b", [P, T, D])
        x2t_h, x2t_l = sb("x2t_h", [P, K, N], F32R), sb("x2t_l", [P, K, N], F32R)
        q_t, k_t, v_s = sb("q_t", [P, K, N]), sb("k_t", [P, K, N]), sb("v_s", [P, T, D])
        e3, p3, pt3 = sb("e3", [P, 2, T, N]), sb("p3", [P, 2, T, N]), sb("pt3", [P, PT3, T, N])
        max3, nmax3 = sb("max3", [P, 2, T]), sb("nmax3", [P, 2, T])
        sum3, inv3 = sb("sum3", [P, 2, T]), sb("inv3", [P, 2, T])
        att_t, x3, x3b = sb("att_t", [P, K, N]), sb("x3", [P, T, D]), sb("x3b", [P, T, D])
        x3t_h, x3t_l = sb("x3t_h", [P, K, N], F32R), sb("x3t_l", [P, K, N], F32R)
        mj3_h, mj3_l = sb("mj3_h", [P, T, D], F32R), sb("mj3_l", [P, T, D], F32R)
        x4 = sb("x4", [P, T, D])
        stats, mean_var = sb("stats", [P, 5, T, 6]), sb("mean_var", [P, 5, T, 2])
        var_eps, rstd = sb("var_eps", [P, 5, T]), sb("rstd", [P, 5, T])

        carrier = sb("carrier", [1, 1])

        stage_wh = pt3[:, 0:4].rearrange("p a t n -> p (a t n)").rearrange("p (k n) -> p k n", k=K)
        stage_l1 = pt3[:, 4:6].rearrange("p a t n -> p (a t n)").rearrange("p (k n) -> p k n", k=K)
        stage_l3 = p3[:].rearrange("p a t n -> p (a t n)").rearrange("p (k n) -> p k n", k=K)
        stage_qkv = heads_t[:, 0:3 * K].rearrange("p (w k) n -> p w k n", w=3)
        stage_ah = feats[:].rearrange("p t n -> p (t n)").rearrange("p (h two n) -> p h two n", h=H, two=2)
        stage_ao = e2[:]
        adj_i, adjt_i, adj_f = y[:].bitcast(I32), x1[:].bitcast(I32), x2[:]
        wa = f_sel[:].rearrange("p (k n) -> p k n", k=K)
        junk = e1[:].rearrange("p a t n -> p (a t) n")

        bank1 = Banks(ctx, nc, "s1", TILES_1, 3)
        bank2 = Banks(ctx, nc, "s2", TILES_2, 2)
        bank3 = Banks(ctx, nc, "s3", TILES_3, 3)

        loaded_stage, loaded_adj, loaded_rest = sem("loaded_stage"), sem("loaded_adj"), sem("loaded_rest")
        split_hi, wa_ready, wout_ready = sem("split_hi"), sem("wa_ready"), sem("wout_ready")
        setup_step, setup_act, setup_dve = sem("setup_step"), sem("setup_act"), sem("setup_dve")
        xt_loaded, xt_hi_ready, xt_lo_ready = sem("xt_loaded"), sem("xt_hi_ready"), sem("xt_lo_ready")
        g_ready, logits1_ready, exp1_done = sem("g_ready"), sem("logits1_ready"), sem("exp1_done")
        inv1_ready, probs1_ready, elu1_exp = sem("inv1_ready"), sem("probs1_ready"), sem("elu1_exp")
        x_loaded, xb_ready = sem("x_loaded"), sem("xb_ready")
        g2_ready, logits2_ready, exp2_done = sem("g2_ready"), sem("logits2_ready"), sem("exp2_done")
        inv2_ready, probs2_ready, elu2_exp = sem("inv2_ready"), sem("probs2_ready"), sem("elu2_exp")
        yn_ready, res1_ready = sem("yn_ready"), sem("res1_ready")
        x1_ready, x1b_ready, x1t_hi, mj1_hi, x2_ready = (sem("x1_ready"), sem("x1b_ready"), sem("x1t_hi"),
                                                          sem("mj1_hi"), sem("x2_ready"))
        x2b_ready, x2t_hi, logits3_ready = sem("x2b_ready"), sem("x2t_hi"), sem("logits3_ready")
        exp3_done, inv3_ready, probs3_ready = sem("exp3_done"), sem("inv3_ready"), sem("probs3_ready")
        x3_ready, x3b_ready, x3t_hi, mj3_hi, x4_ready = (sem("x3_ready"), sem("x3b_ready"), sem("x3t_hi"),
                                                          sem("mj3_hi"), sem("x4_ready"))
        stored = sem("stored")
        var_ready = [sem(f"var_ready{i}") for i in range(5)]
        rstd_ready = [sem(f"rstd_ready{i}") for i in range(5)]
        dve_step = [sem(f"dve_step{i}") for i in (1, 2, 3)]
        pool_step = sem("pool_step")
        DVE_STEPS = (9, 9, 4)

        block = ctx.enter_context(nc.Block())

        def pipeline(eng, iteration):
            iteration(0, None, None)
            iteration(1, 0, None)
            iteration(2, 1, 0)
            with eng.Fori(3, B) as i:
                iteration(i, i - 1, i - 2)
            iteration(None, B - 1, B - 2)
            iteration(None, None, B - 1)

        def on(b, step, *args):
            if b is not None:
                step(b, *args)

        def rows_of(dram, b):
            return dram[bass.ds(b, 1)].rearrange("b (t p) n -> p (b t) n", p=P)

        @block.sync
        def _(sp):
            tiled = "(k p) n -> p k n"
            for dst, src in ((stage_wh.rearrange("p k (h n) -> p k h n", h=H),
                              w_heads.rearrange("h (k p) n -> p k h n", p=P)),
                             (stage_l1[:, :, 0:D], l1_wt[0:D].rearrange(tiled, p=P)),
                             (stage_l1[:, :, D:], l1_wt[D:].rearrange(tiled, p=P)),
                             (stage_l3[:, :, 0:D], l3_wt[0:D].rearrange(tiled, p=P)),
                             (stage_l3[:, :, D:], l3_wt[D:].rearrange(tiled, p=P)),
                             (stage_qkv[:, 0], wq_t.rearrange(tiled, p=P)),
                             (stage_qkv[:, 1], wk_t.rearrange(tiled, p=P)),
                             (stage_qkv[:, 2], wv_t.rearrange(tiled, p=P)),
                             (wout[:, :, 0:D], w_out.rearrange(tiled, p=P))):
                if len(dst.shape) == 4:
                    for k in range(K):
                        sp.dma_start(dst[:, k], src[:, k]).then_inc(loaded_stage, 16)
                else:
                    sp.dma_start(dst, src).then_inc(loaded_stage, 16)

            def load_xt(b):
                wait(sp, (xt_lo_ready, b))
                sp.dma_start(xt_s[:], rows_of(xt, b)).then_inc(xt_loaded, 16)

            def load_x(b):
                wait(sp, (res1_ready, b))
                sp.dma_start(x_s[:], rows_of(x, b)).then_inc(x_loaded, 16)

            def store(b):
                sp.wait_ge(x4_ready, b + 1)
                sp.dma_start(rows_of(out, b), x4[:]).then_inc(stored, 16)

            load_xt(0)
            load_xt(1)
            load_x(0)
            load_xt(2)
            load_x(1)
            with sp.Fori(3, B) as i:
                load_xt(i)
                load_x(i - 1)
                store(i - 3)
            load_x(B - 1)
            for b in range(B - 3, B):
                store(b)
            sp.wait_ge(stored, 16 * B)

        N_STAGE = 10
        N_ADJ = 2
        N_REST = 3 + 2 + 9 + 7 + 3

        @block.gpsimd
        def _(pool):
            nc.gpsimd.memset(minus_half[:], -0.5).then_inc(pool_step, 1)
            pool.wait_ge(pool_step, 1)
            pool.wait_ge(loaded_rest, 16 * N_REST)
            pool.wait_ge(setup_dve, 1)

            def both(row):
                return rows[:, row, :].unsqueeze(1).broadcast_to([P, T, D])

            def spread(small):
                return small.unsqueeze(2).broadcast_to([P, T, N])

            def normalise(probs, inv, ready, done):
                wait(pool, ready)
                nc.gpsimd.tensor_tensor(probs, probs, spread(inv), ALU.mult).then_inc(done, 1)

            def probs_1(b, h):
                normalise(p1[:, h % 2], inv1[:, h % 2], (inv1_ready, b * H + h + 1), probs1_ready)

            def probs_2(b):
                normalise(p2[:], inv2[:], (inv2_ready, b + 1), probs2_ready)

            def probs_3(b, h):
                normalise(p3[:, h % 2], inv3[:, h % 2], (inv3_ready, b * HM + h + 1), probs3_ready)

            def inverse_root(b, i):
                pool.wait_ge(var_ready[i], b + 1)
                nc.gpsimd.tensor_tensor(rstd[:, i], var_eps[:, i], minus_half[:], ALU.pow).then_inc(rstd_ready[i], 1)

            def add_beta(b):
                pool.wait_ge(x_loaded, 16 * (b + 1))
                nc.gpsimd.tensor_tensor(x_s[:], x_s[:], both(BETA), ALU.add).then_inc(xb_ready, 1)

            def residual_1(b):
                pool.wait_ge(yn_ready, b + 1)
                wait(pool, bank2.filled("xt", b - 1))
                wait(pool, (x1b_ready, b))
                nc.gpsimd.tensor_tensor(x1[:], y[:], both(GAMMA), ALU.mult).then_inc(pool_step, 1)
                pool.wait_ge(pool_step, b + 2)
                pool.wait_ge(xb_ready, b + 1)
                nc.gpsimd.tensor_tensor(x1[:], x1[:], x_s[:], ALU.add).then_inc(res1_ready, 1)

            def add_const(b, dst, src, src_ready, const, dst_free, done):
                pool.wait_ge(src_ready, b + 1)
                wait(pool, dst_free)
                nc.gpsimd.tensor_tensor(dst, src, const, ALU.add).then_inc(done, 1)

            def x1_const(b):
                add_const(b, x1b[:], x1[:], x1_ready, l1_db[:], bank2.was_read("m1", b - 1), x1b_ready)

            def x2_const(b):
                add_const(b, x2b[:], x2[:], x2_ready, both(BO), bank3.was_read("o", b - 1), x2b_ready)

            def x3_const(b):
                add_const(b, x3b[:], x3[:], x3_ready, l3_db[:], bank3.was_read("m1", b - 1), x3b_ready)

            def iteration(b1, b2, b3):
                on(b2, add_beta)
                on(b3, x2_const)
                on(b3, probs_3, 0)
                on(b3, probs_3, 1)
                on(b2, probs_2)
                on(b3, probs_3, 2)
                on(b1, probs_1, 0)
                on(b3, probs_3, 3)
                on(b3, probs_3, 4)
                on(b3, probs_3, 5)
                on(b3, probs_3, 6)
                on(b1, probs_1, 1)
                on(b2, inverse_root, 0)
                on(b2, residual_1)
                on(b3, probs_3, 7)
                on(b2, inverse_root, 1)
                on(b1, probs_1, 2)
                on(b2, x1_const)
                on(b3, inverse_root, 3)
                on(b3, x3_const)
                on(b1, probs_1, 3)
                on(b2, inverse_root, 2)
                on(b3, inverse_root, 4)

            pipeline(pool, iteration)

        @block.scalar
        def _(act):
            tiled = "(k p) n -> p k n"
            act.dma_start(adj_i, adj.rearrange("(t p) n -> p t n", p=P)).then_inc(loaded_adj, 16)
            act.dma_start(adjt_i, adjt.rearrange("(t p) n -> p t n", p=P)).then_inc(loaded_adj, 16)
            for dst, src in ((w1_s, w1), (w2_s, w2), (wo_s, wo_t)):
                act.dma_start(dst[:], src.rearrange(tiled, p=P)).then_inc(loaded_rest, 16)
            act.dma_start(ident[:], ident_d).then_inc(loaded_rest, 16)
            act.dma_start(select[:], select_d).then_inc(loaded_rest, 16)
            for h in range(H):
                for half in range(2):
                    act.dma_start(stage_ah[:, h, half], a_heads[h:h + 1, half * D:(half + 1) * D]
                                  .broadcast_to([P, D])).then_inc(loaded_rest, 16)
            act.dma_start(stage_ao, a_out.rearrange("(o t n) -> o t n", o=1, t=2)
                          .broadcast_to([P, 2, D])).then_inc(loaded_rest, 16)
            for r, src in enumerate((gamma, beta, b2, bo, bv, l1_b, l3_b)):
                act.dma_start(rows[:, r], src.rearrange("(o n) -> o n", o=1).broadcast_to([P, D])).then_inc(loaded_rest, 16)
            for dst, src in ((b1_c, b1), (bq_c, bq), (bk_c, bk)):
                act.dma_start(dst[:], src).then_inc(loaded_rest, 16)

            act.wait_ge(loaded_stage, 16 * N_STAGE)
            for dst, src in ((wh_h[:], stage_wh), (l1_h[:], stage_l1), (l3_h[:], stage_l3), (qkv_h[:], stage_qkv)):
                nc.scalar.activation(dst, src, ACT.Copy).then_inc(split_hi, 1)
            act.wait_ge(wa_ready, 1)
            nc.scalar.activation(wa_h[:], wa, ACT.Copy).then_inc(split_hi, 1)
            act.wait_ge(loaded_adj, 16 * N_ADJ)
            nc.scalar.activation(adjt_r[:], adjt_i, ACT.Copy).then_inc(setup_act, 1)
            act.wait_ge(loaded_rest, 16 * N_REST)
            act.wait_ge(setup_dve, 3)

            def xt_upper(b):
                act.wait_ge(xt_loaded, 16 * (b + 1))
                wait(act, bank1.filled("f", b - 1))
                nc.scalar.activation(xt_h[:], xt_s[:], ACT.Copy).then_inc(xt_hi_ready, 1)

            def feats_copy(b, t, half):
                tile = f"wh{t}{half}"
                wait(act, bank1.filled(tile, b))
                if (t, half) == (0, 0):
                    wait(act, bank1.filled("av3", b - 1))
                nc.scalar.activation(feats[:, t, half * 512:(half + 1) * 512], bank1.ap(tile)[:], ACT.Copy)\
                    .then_inc(bank1.was_read(tile, b)[0], 1)

            def coeff_parts(b, bank, tile, n, hi, tmp, used):
                wait(act, bank.filled(tile, b))
                wait(act, (used, b))
                nc.scalar.activation(hi[:], bank.ap(tile)[0:n, 0:N], ACT.Copy)
                nc.scalar.activation(tmp[:], bank.ap(tile)[0:n, 0:N], ACT.Copy, scale=select[0:n, 0:1])\
                    .then_inc(bank.was_read(tile, b)[0], 1)

            def softmax_exp(e, probs, nmax, sums, scale, done):
                for t in range(T):
                    last = nc.scalar.activation(probs[:, t], e[:, t], ACT.Exp, bias=nmax[:, t:t + 1], scale=scale,
                                                accum_out=sums[:, t:t + 1])
                last.then_inc(done, 1)

            def exp_1(b, h):
                act.wait_ge(logits1_ready, b * H + h + 1)
                wait(act, bank1.filled(f"t{h - 2}", b) if h >= 2 else bank1.filled(f"t{h + 2}", b - 1))
                softmax_exp(e1[:, h % 2], p1[:, h % 2], nmax1[:, h % 2], sum1[:, h % 2], 1.0, exp1_done)

            def exp_2(b):
                act.wait_ge(logits2_ready, b + 1)
                wait(act, bank2.filled("t", b - 1))
                softmax_exp(e2[:], p2[:], nmax2[:], sum2[:], 1.0, exp2_done)

            def exp_3(b, h):
                act.wait_ge(logits3_ready, b * HM + h + 1)
                wait(act, bank3.filled(f"t{h - 2}", b) if h >= 2 else bank3.filled(f"t{h + 6}", b - 1))
                softmax_exp(e3[:, h % 2], p3[:, h % 2], nmax3[:, h % 2], sum3[:, h % 2], SCALE, exp3_done)

            def copy_out(b, bank, tile, dst, dst_free):
                wait(act, bank.filled(tile, b))
                wait(act, dst_free)
                nc.scalar.activation(dst, bank.half(tile), ACT.Copy).then_inc(bank.was_read(tile, b)[0], 1)

            def probs_t_1(b, h):
                copy_out(b, bank1, f"t{h}", pt1[:, h % 2],
                         bank1.filled(f"av{h - 2}", b) if h >= 2 else bank1.filled(f"av{h + 2}", b - 1))

            def probs_t_2(b):
                copy_out(b, bank2, "t", pt2[:], bank2.filled("av", b - 1))

            def probs_t_3(b, h):
                copy_out(b, bank3, f"t{h}", pt3[:, h % PT3],
                         bank3.filled("o0", b) if h >= PT3 else bank3.filled("o1", b - 1))

            def elu_exp_1(b, h):
                wait(act, bank1.filled(f"av{h}", b))
                wait(act, bank1.was_read(f"av{h - 2}", b) if h >= 2 else bank1.was_read(f"av{h + 2}", b - 1))
                nc.scalar.activation(elu1[:, h % 2], bank1.half(f"av{h}"), ACT.Exp).then_inc(elu1_exp, 1)

            def elu_exp_2(b):
                wait(act, bank2.filled("av", b))
                wait(act, bank2.was_read("av", b - 1))
                nc.scalar.activation(elu2[:], bank2.half("av"), ACT.Exp).then_inc(elu2_exp, 1)

            def feats2_copy(b, t):
                wait(act, bank2.filled(f"wh{t}", b))
                wait(act, bank2.filled("av", b - 1))
                nc.scalar.activation(feats2[:, t], bank2.ap(f"wh{t}")[:, 0:D + 4], ACT.Copy)\
                    .then_inc(bank2.was_read(f"wh{t}", b)[0], 1)

            def hidden(b):
                wait(act, bank2.filled("hid", b))
                wait(act, bank2.filled("y", b - 1))
                for m in range(K):
                    last = nc.scalar.activation(hid[:, m], bank2.half("hid")[:, m], ACT.Relu, bias=b1_c[:, m:m + 1])
                last.then_inc(bank2.was_read("hid", b)[0], 1)

            def upper(b, bank, tile, dst, used, done):
                wait(act, bank.filled(tile, b))
                wait(act, used)
                nc.scalar.activation(dst, bank.half(tile), ACT.Copy).then_inc(done, 1)

            def mj_upper(b, bank, t, dst, done):
                wait(act, bank.filled(f"m{t}", b))
                wait(act, bank.filled("a", b - 1))
                nc.scalar.activation(dst[:, t], bank.ap(f"m{t}")[:, D:], ACT.Copy).then_inc(done, 1)

            def project_copy(b, tile, dst, bias):
                wait(act, bank3.filled(tile, b))
                wait(act, bank3.filled("s7", b - 1))
                for m in range(K):
                    last = nc.scalar.activation(dst[:, m], bank3.half(tile)[:, m], ACT.Identity, bias=bias[:, m:m + 1])
                last.then_inc(bank3.was_read(tile, b)[0], 1)

            def att_copy(b, g):
                wait(act, bank3.filled(f"o{g}", b))
                wait(act, bank3.filled("o", b - 1))
                nc.scalar.activation(att_t[:, g], bank3.ap(f"o{g}")[:, 0:N], ACT.Copy).then_inc(bank3.was_read(f"o{g}", b)[0], 1)

            def iteration(b1, b2, b3):
                on(b2, feats2_copy, 0)
                on(b3, upper, bank3, "xt", x2t_h[:], bank3.filled("v", b3 - 1) if b3 is not None else None, x2t_hi)
                on(b1, xt_upper)
                on(b2, feats2_copy, 1)
                on(b3, project_copy, "q", q_t, bq_c)
                on(b3, project_copy, "k", k_t, bk_c)
                on(b1, feats_copy, 0, 0)
                on(b1, feats_copy, 0, 1)
                on(b2, coeff_parts, bank2, "f", 4, f2_hi, f2_tmp, g2_ready)
                on(b1, feats_copy, 1, 0)
                on(b1, feats_copy, 1, 1)
                on(b3, exp_3, 0)
                on(b1, coeff_parts, bank1, "f", P, f_hi, f_tmp, g_ready)
                on(b2, exp_2)
                on(b3, exp_3, 1)
                on(b3, probs_t_3, 0)
                on(b3, exp_3, 2)
                on(b1, exp_1, 0)
                on(b2, probs_t_2)
                on(b3, probs_t_3, 1)
                on(b3, exp_3, 3)
                on(b3, exp_3, 4)
                on(b2, elu_exp_2)
                on(b3, probs_t_3, 2)
                on(b1, probs_t_1, 0)
                on(b3, exp_3, 5)
                on(b3, probs_t_3, 3)
                on(b3, probs_t_3, 4)
                on(b1, elu_exp_1, 0)
                on(b2, hidden)
                on(b3, exp_3, 6)
                on(b3, probs_t_3, 5)
                on(b1, exp_1, 1)
                on(b3, att_copy, 0)
                on(b3, exp_3, 7)
                on(b3, probs_t_3, 6)
                on(b1, probs_t_1, 1)
                on(b3, probs_t_3, 7)
                on(b1, elu_exp_1, 1)
                on(b3, att_copy, 1)
                on(b1, exp_1, 2)
                on(b2, upper, bank2, "xt", x1t_h[:], bank2.filled("m1", b2 - 1) if b2 is not None else None, x1t_hi)
                on(b1, probs_t_1, 2)
                on(b2, mj_upper, bank2, 0, mj1_h, mj1_hi)
                on(b2, mj_upper, bank2, 1, mj1_h, mj1_hi)
                on(b1, elu_exp_1, 2)
                on(b3, upper, bank3, "x3t", x3t_h[:], bank3.filled("m1", b3 - 1) if b3 is not None else None, x3t_hi)
                on(b1, exp_1, 3)
                on(b3, mj_upper, bank3, 0, mj3_h, mj3_hi)
                on(b3, mj_upper, bank3, 1, mj3_h, mj3_hi)
                on(b1, probs_t_1, 3)
                on(b1, elu_exp_1, 3)

            pipeline(act, iteration)

        @block.vector
        def _(dve):
            count = [0]

            def setup(ins):
                count[0] += 1
                ins.then_inc(setup_step, 1)
                dve.wait_ge(setup_step, count[0])

            dve.wait_ge(loaded_adj, 16 * N_ADJ)
            nc.vector.tensor_copy(adj_f, adj_i).then_inc(setup_step, 1)
            count[0] += 1
            dve.wait_ge(setup_step, count[0])
            nc.vector.tensor_scalar(gat_mask[:], adj_f, 0.0, GAT_MASK, ALU.is_le, ALU.mult)
            nc.vector.tensor_scalar(att_mask[:], adj_f, 0.0, ATT_MASK, ALU.is_equal, ALU.mult)
            setup(nc.vector.tensor_reduce(deg[:], adj_f, AX.X, ALU.add))
            setup(nc.vector.memset(wa, 0.0))
            dve.wait_ge(loaded_rest, 16 * N_REST)
            for t in range(T):
                nc.vector.tensor_scalar(l1_db[:, t], rows[:, L1B], deg[:, t:t + 1], None, ALU.mult)
                last = nc.vector.tensor_scalar(l3_db[:, t], rows[:, L3B], deg[:, t:t + 1], None, ALU.mult)
            last.then_inc(setup_dve, 1)
            dve.wait_ge(loaded_stage, 16 * N_STAGE)
            for k in range(K):
                for h in range(H):
                    for half in range(2):
                        c = 32 * h + 2 * half
                        setup(nc.vector.tensor_tensor_reduce(junk[:, 0], stage_wh[:, k, h * D:(h + 1) * D],
                                                             stage_ah[:, h, half], 1.0, 0.0, ALU.mult, ALU.add,
                                                             wa[:, k, c:c + 1]))
            last = nc.vector.tensor_copy(wa.rearrange("p k (h c) -> p k h c", c=32)[:, :, :, 1:4:2],
                                         wa.rearrange("p k (h c) -> p k h c", c=32)[:, :, :, 0:4:2])
            last.then_inc(wa_ready, 1)
            for k in range(KH):
                for half in range(2):
                    c = D + 2 * half
                    setup(nc.vector.tensor_tensor_reduce(junk[:, 0], wout[:, k, 0:D], stage_ao[:, half], 1.0, 0.0,
                                                         ALU.mult, ALU.add, wout[:, k, c:c + 1]))
            nc.vector.tensor_copy(wout[:, :, D + 1:D + 4:2], wout[:, :, D:D + 4:2]).then_inc(setup_dve, 1)
            for n, (lo, src, hi) in enumerate(((wh_l, stage_wh, wh_h), (l1_l, stage_l1, l1_h), (l3_l, stage_l3, l3_h),
                                               (qkv_l, stage_qkv, qkv_h), (wa_l, wa, wa_h))):
                dve.wait_ge(split_hi, n + 1)
                last = nc.vector.tensor_tensor(lo[:], src, hi[:].bitcast(F32), ALU.subtract)
            last.then_inc(setup_dve, 1)
            dve.wait_ge(setup_dve, 3)

            steps = [0, 0, 0]

            def link(stage, b, ins, carried=True):
                steps[stage - 1] += 1
                ins.then_inc(dve_step[stage - 1], 1)
                done = dve_step[stage - 1], b * DVE_STEPS[stage - 1] + steps[stage - 1]
                wait(dve, done) if carried else wait_apart(done)

            def wait_apart(*sem_values):
                for sem_value in sem_values:
                    wait(dve, sem_value)
                nc.vector.memset(carrier[0:1, 0:1], 0.0)

            def xt_lower(b):
                dve.wait_ge(xt_hi_ready, b + 1)
                nc.vector.tensor_tensor(xt_l[:], xt_s[:], xt_h[:].bitcast(F32), ALU.subtract).then_inc(xt_lo_ready, 1)

            def coefficients(b, stage, bank, n, hi, tmp, sel, gq, gk, last_scores, ready):
                wait(dve, bank.was_read("f", b))
                wait(dve, bank.filled(last_scores, b - 1))
                link(stage, b, nc.vector.scalar_tensor_tensor(out=sel[:], in0=hi[:].bitcast(F32), scalar=select[0:n, 1:2],
                                                              in1=tmp[:], op0=ALU.mult, op1=ALU.add))
                nc.vector.tensor_scalar(gq[:], sel[:], select[0:n, 2:3], select[0:n, 3:4], ALU.mult, ALU.add)
                nc.vector.tensor_scalar(gk[:], sel[:], select[0:n, 3:4], select[0:n, 2:3], ALU.mult, ALU.add)\
                    .then_inc(ready, 1)

            def gat_logits(b, stage, bank, tile, e, mx, neg, nmax, e_free, done):
                wait_apart(bank.filled(tile, b), e_free)
                for t in range(T):
                    last = nc.vector.tensor_tensor_reduce(e[:, t], bank.half(tile)[:, t], gat_mask[:, t], 1.0, -3e38,
                                                          ALU.add, ALU.max, mx[:, t:t + 1])
                last.then_inc(bank.was_read(tile, b)[0], 1)
                wait(dve, bank.was_read(tile, b))
                link(stage, b, nc.vector.tensor_scalar(neg, mx, -1.0, None, ALU.mult))
                nc.vector.scalar_tensor_tensor(out=nmax, in0=neg, scalar=SLOPE, in1=neg, op0=ALU.mult, op1=ALU.min)
                nc.vector.scalar_tensor_tensor(out=e, in0=e, scalar=SLOPE, in1=e, op0=ALU.mult, op1=ALU.max)\
                    .then_inc(done, 1)

            def logits_1(b, h):
                gat_logits(b, 1, bank1, f"e{h}", e1[:, h % 2], max1[:, h % 2], neg1[:, h % 2], nmax1[:, h % 2],
                           (exp1_done, b * H + h - 1), logits1_ready)

            def logits_2(b):
                gat_logits(b, 2, bank2, "e", e2[:], max2[:], neg2[:], nmax2[:], (exp2_done, b), logits2_ready)

            def logits_3(b, h):
                tile = f"s{h}"
                wait_apart(bank3.filled(tile, b), (exp3_done, b * HM + h - 1))
                for t in range(T):
                    last = nc.vector.tensor_tensor_reduce(e3[:, h % 2, t], bank3.half(tile)[:, t], att_mask[:, t],
                                                          1.0, -3e38, ALU.add, ALU.max, max3[:, h % 2, t:t + 1])
                last.then_inc(bank3.was_read(tile, b)[0], 1)
                wait(dve, bank3.was_read(tile, b))
                nc.vector.tensor_scalar(nmax3[:, h % 2], max3[:, h % 2], -SCALE, None, ALU.mult).then_inc(logits3_ready, 1)

            def inverse(exp_done, inv_free, inv, sums, ready):
                wait(dve, exp_done)
                wait(dve, inv_free)
                nc.vector.reciprocal(inv, sums).then_inc(ready, 1)

            def inverse_1(b, h):
                inverse((exp1_done, b * H + h + 1), (probs1_ready, b * H + h - 1), inv1[:, h % 2], sum1[:, h % 2], inv1_ready)

            def inverse_2(b):
                inverse((exp2_done, b + 1), (probs2_ready, b), inv2[:], sum2[:], inv2_ready)

            def inverse_3(b, h):
                inverse((exp3_done, b * HM + h + 1), (probs3_ready, b * HM + h - 1), inv3[:, h % 2], sum3[:, h % 2], inv3_ready)

            def elu(b, stage, bank, tile, expd, exp_ready, dst, dst_free):
                wait(dve, exp_ready)
                wait(dve, dst_free)
                link(stage, b, nc.vector.tensor_scalar(expd, expd, 1.0, -1.0, ALU.min, ALU.add))
                nc.vector.tensor_tensor(dst, bank.half(tile), expd, ALU.max).then_inc(bank.was_read(tile, b)[0], 1)

            def elu_1(b, h):
                elu(b, 1, bank1, f"av{h}", elu1[:, h % 2], (elu1_exp, b * H + h + 1), heads_t[:, 2 * h:2 * h + 2],
                    bank2.filled("wh1", b - 1))

            def elu_2(b):
                elu(b, 2, bank2, "av", elu2[:], (elu2_exp, b + 1), out2_t[:], bank2.filled("y", b - 1))

            def statistics(b, stage, i, src):
                for t in range(T):
                    last = nc.vector.bn_stats(stats[:, i, t], src[:, t])
                link(stage, b, last, carried=False)
                for t in range(T):
                    last = nc.vector.bn_aggr(mean_var[:, i, t], stats[:, i, t])
                link(stage, b, last)
                nc.vector.tensor_scalar(var_eps[:, i], mean_var[:, i, :, 1], EPS, None, ALU.add).then_inc(var_ready[i], 1)

            def apply_norm(b, i, buf, done):
                dve.wait_ge(rstd_ready[i], b + 1)
                for t in range(T):
                    last = nc.vector.tensor_scalar(buf[:, t], buf[:, t], mean_var[:, i, t, 0:1], rstd[:, i, t:t + 1],
                                                   ALU.subtract, ALU.mult)
                last.then_inc(done, 1)

            def feed_forward_sum(b):
                wait(dve, bank2.filled("y", b))
                wait(dve, (res1_ready, b))
                nc.vector.tensor_tensor(y[:], bank2.half("y"), rows[:, B2, :].unsqueeze(1).broadcast_to([P, T, D]),
                                        ALU.add).then_inc(bank2.was_read("y", b)[0], 1)
                wait(dve, bank2.was_read("y", b))
                statistics(b, 2, 0, y)

            def norm_0(b):
                apply_norm(b, 0, y, yn_ready)

            def stats_1(b):
                dve.wait_ge(res1_ready, b + 1)
                statistics(b, 2, 1, x1)

            def norm_1(b):
                apply_norm(b, 1, x1, x1_ready)

            def lower(b, bank, tile, dst, hi, hi_ready):
                dve.wait_ge(hi_ready, b + 1)
                nc.vector.tensor_tensor(dst[:], bank.half(tile), hi[:].bitcast(F32), ALU.subtract)\
                    .then_inc(bank.was_read(tile, b)[0], 1)

            def messages(b, bank, t, lo, hi, hi_ready, base, base_ready, total, total_free):
                dve.wait_ge(hi_ready, b * T + t + 1)
                dve.wait_ge(base_ready, b + 1)
                for free in total_free:
                    wait(dve, free)
                nc.vector.tensor_tensor(lo[:, t], bank.ap(f"m{t}")[:, D:], hi[:, t].bitcast(F32), ALU.subtract)
                nc.vector.scalar_tensor_tensor(out=total[:, t], in0=bank.ap(f"m{t}")[:, 0:D], scalar=deg[:, t:t + 1],
                                               in1=base[:, t], op0=ALU.mult, op1=ALU.add)\
                    .then_inc(bank.was_read(f"m{t}", b)[0], 1)

            def aggregate(b, stage, bank, i, total):
                wait(dve, bank.filled("a", b))
                wait(dve, bank.was_read("m1", b))
                wait(dve, bank.was_read("m0", b))
                nc.vector.tensor_tensor(total[:], bank.half("a"), total[:], ALU.add).then_inc(bank.was_read("a", b)[0], 1)
                wait(dve, bank.was_read("a", b))
                statistics(b, stage, i, total)

            def norm_2(b):
                apply_norm(b, 2, x2, x2_ready)

            def messages_1(b, t):
                messages(b, bank2, t, mj1_l, mj1_h, mj1_hi, x1b, x1b_ready, x2, [bank3.filled("xt", b - 1), (x2b_ready, b)])

            def messages_3(b, t):
                messages(b, bank3, t, mj3_l, mj3_h, mj3_hi, x3b, x3b_ready, x4, [(stored, 16 * b)])

            def values(b):
                wait(dve, bank3.filled("v", b))
                wait(dve, bank3.filled("o1", b - 1))
                nc.vector.tensor_tensor(v_s[:], bank3.half("v"), rows[:, BV, :].unsqueeze(1).broadcast_to([P, T, D]),
                                        ALU.add).then_inc(bank3.was_read("v", b)[0], 1)

            def attention_sum(b):
                wait(dve, bank3.filled("o", b))
                dve.wait_ge(x2b_ready, b + 1)
                wait(dve, bank3.filled("x3t", b - 1))
                wait(dve, (x3b_ready, b))
                nc.vector.tensor_tensor(x3[:], bank3.half("o"), x2b[:], ALU.add).then_inc(bank3.was_read("o", b)[0], 1)
                wait(dve, bank3.was_read("o", b))
                statistics(b, 3, 3, x3)

            def norm_3(b):
                apply_norm(b, 3, x3, x3_ready)

            def norm_4(b):
                apply_norm(b, 4, x4, x4_ready)

            def iteration(b1, b2, b3):
                steps[:] = [0, 0, 0]
                on(b3, lower, bank3, "xt", x2t_l, x2t_h, x2t_hi)
                on(b1, xt_lower)
                on(b3, values)
                on(b2, coefficients, 2, bank2, 4, f2_hi, f2_tmp, f2_sel, g2_query, g2_key, "e", g2_ready)
                on(b3, logits_3, 0)
                on(b2, logits_2)
                on(b3, logits_3, 1)
                on(b3, inverse_3, 0)
                on(b1, coefficients, 1, bank1, P, f_hi, f_tmp, f_sel, g_query, g_key, "e3", g_ready)
                on(b2, inverse_2)
                on(b3, logits_3, 2)
                on(b3, inverse_3, 1)
                on(b1, logits_1, 0)
                on(b3, logits_3, 3)
                on(b3, inverse_3, 2)
                on(b3, logits_3, 4)
                on(b1, inverse_1, 0)
                on(b3, inverse_3, 3)
                on(b3, logits_3, 5)
                on(b3, inverse_3, 4)
                on(b2, elu_2)
                on(b3, logits_3, 6)
                on(b3, inverse_3, 5)
                on(b1, logits_1, 1)
                on(b1, elu_1, 0)
                on(b3, inverse_3, 6)
                on(b3, logits_3, 7)
                on(b1, inverse_1, 1)
                on(b2, feed_forward_sum)
                on(b3, inverse_3, 7)
                on(b2, norm_0)
                on(b1, logits_1, 2)
                on(b1, elu_1, 1)
                on(b1, inverse_1, 2)
                on(b2, stats_1)
                on(b2, norm_1)
                on(b3, attention_sum)
                on(b2, lower, bank2, "xt", x1t_l, x1t_h, x1t_hi)
                on(b3, norm_3)
                on(b1, logits_1, 3)
                on(b2, messages_1, 0)
                on(b2, messages_1, 1)
                on(b1, elu_1, 2)
                on(b3, lower, bank3, "x3t", x3t_l, x3t_h, x3t_hi)
                on(b1, inverse_1, 3)
                on(b2, aggregate, 2, bank2, 2, x2)
                on(b2, norm_2)
                on(b3, messages_3, 0)
                on(b3, messages_3, 1)
                on(b3, aggregate, 3, bank3, 4, x4)
                on(b1, elu_1, 3)
                on(b3, norm_4)
                for stage, b in enumerate((b1, b2, b3)):
                    assert b is None or steps[stage] == DVE_STEPS[stage], steps

            pipeline(dve, iteration)

        @block.tensor
        def _(pe):
            pe.wait_ge(loaded_rest, 16 * N_REST)
            pe.wait_ge(setup_act, 1)
            pe.wait_ge(setup_dve, 3)

            def product3(out_ap, stat, mov, first=True, last=True):
                n = 0
                for k in range(K):
                    for a, c in ((stat[0], mov[0]), (stat[0], mov[1]), (stat[1], mov[0])):
                        ins = nc.tensor.matmul(out_ap, a(k), c(k), start=first and n == 0, stop=last and n == 3 * K - 1)
                        n += 1
                return ins

            def parts(hi, lo, cut=slice(None)):
                return (lambda k: hi[:, k, cut]), (lambda k: lo[:, k, cut])

            def rows_cut(t):
                return slice(t * P, (t + 1) * P)

            def transposes(b, bank, tile, src):
                for t in range(2):
                    for k in range(2):
                        ins = nc.tensor.transpose(bank.half(tile)[:, k, rows_cut(t)], src[:, t, rows_cut(k)], ident[:])
                ins.then_inc(bank.filled(tile, b)[0], 1)

            def project_1(b, t, half):
                tile = f"wh{t}{half}"
                pe.wait_ge(xt_lo_ready, b + 1)
                wait(pe, bank1.vacant(tile, b))
                product3(bank1.ap(tile)[:], parts(xt_h, xt_l, rows_cut(t)),
                         parts(wh_h, wh_l, slice(half * 512, (half + 1) * 512))).then_inc(bank1.filled(tile, b)[0], 1)

            def coeff_rows_1(b):
                wait(pe, bank1.vacant("f", b))
                product3(bank1.ap("f")[:, 0:N], parts(wa_h, wa_l), parts(xt_h, xt_l)).then_inc(bank1.filled("f", b)[0], 1)

            def pair_sums(b, bank, tile, gq, gk, at, ready):
                pe.wait_ge(ready, b + 1)
                wait(pe, bank.vacant(tile, b))
                for t in range(T):
                    ins = nc.tensor.matmul(bank.half(tile)[:, t], gq[at:at + 4, rows_cut(t)], gk[at:at + 4, :],
                                           start=True, stop=True, tile_position=(at, 0))
                ins.then_inc(bank.filled(tile, b)[0], 1)

            def pairs_1(b, h):
                pair_sums(b, bank1, f"e{h}", g_query, g_key, 32 * h, g_ready)

            def pairs_2(b):
                pair_sums(b, bank2, "e", g2_query, g2_key, 0, g2_ready)

            def turn_probs(b, bank, tile, probs, ready):
                wait(pe, ready)
                wait(pe, bank.vacant(tile, b))
                transposes(b, bank, tile, probs)

            def turn_1(b, h):
                turn_probs(b, bank1, f"t{h}", p1[:, h % 2], (probs1_ready, b * H + h + 1))

            def turn_2(b):
                turn_probs(b, bank2, "t", p2, (probs2_ready, b + 1))

            def turn_3(b, h):
                turn_probs(b, bank3, f"t{h}", p3[:, h % 2], (probs3_ready, b * HM + h + 1))

            def attend_t(b, bank, tile, turned, feat, probs_t):
                bank.wait_read(pe, b, turned, into=tile)
                for m in range(K):
                    for k in range(T):
                        ins = nc.tensor.matmul(bank.half(tile)[:, m], feat(k, m), probs_t[:, k], start=(k == 0),
                                               stop=(k == T - 1))
                ins.then_inc(bank.filled(tile, b)[0], 1)

            def attend_1(b, h):
                attend_t(b, bank1, f"av{h}", f"t{h}",
                         lambda k, m: feats[:, k, h * D + m * P:h * D + (m + 1) * P], pt1[:, h % 2])

            def attend_2(b):
                attend_t(b, bank2, "av", "t", lambda k, m: feats2[:, k, rows_cut(m)], pt2)

            def project_2(b, t):
                wait(pe, bank1.was_read("av2", b))
                wait(pe, bank1.was_read("av3", b))
                wait(pe, bank2.vacant(f"wh{t}", b))
                for k in range(KH):
                    ins = nc.tensor.matmul(bank2.ap(f"wh{t}")[:, 0:D + 4], heads_t[:, k, rows_cut(t)], wout[:, k],
                                           start=(k == 0), stop=(k == KH - 1))
                ins.then_inc(bank2.filled(f"wh{t}", b)[0], 1)

            def coeff_rows_2(b):
                wait(pe, bank2.was_read("wh0", b))
                wait(pe, bank2.was_read("wh1", b))
                for t in range(T):
                    ins = nc.tensor.transpose(bank2.ap("f")[0:4, rows_cut(t)], feats2[:, t, D:D + 4], ident[:])
                ins.then_inc(bank2.filled("f", b)[0], 1)

            def feed_forward_1(b):
                bank2.wait_read(pe, b, "av", into="hid")
                for m in range(K):
                    for k in range(K):
                        ins = nc.tensor.matmul(bank2.half("hid")[:, m], w1_s[:, k, rows_cut(m)], out2_t[:, k],
                                               start=(k == 0), stop=(k == K - 1))
                ins.then_inc(bank2.filled("hid", b)[0], 1)

            def feed_forward_2(b):
                bank2.wait_read(pe, b, "hid", into="y")
                for t in range(T):
                    for c in range(K):
                        part = bank2.half("y")[:, t, rows_cut(c)]
                        for k in range(K):
                            nc.tensor.matmul(part, hid[:, k, rows_cut(t)], w2_s[:, k, rows_cut(c)],
                                             start=(k == 0), stop=False)
                        ins = nc.tensor.matmul(part, out2_t[:, c, rows_cut(t)], ident[:], start=False, stop=True)
                ins.then_inc(bank2.filled("y", b)[0], 1)

            def turn_rows(b, bank, tile, src, ready):
                wait(pe, ready)
                wait(pe, bank.vacant(tile, b))
                transposes(b, bank, tile, src)

            def own_and_messages(b, bank, t, rows_h, rows_l, turned, w_h, w_l):
                bank.wait_read(pe, b, turned, into=f"m{t}")
                product3(bank.ap(f"m{t}")[:], parts(rows_h, rows_l, rows_cut(t)), parts(w_h, w_l))\
                    .then_inc(bank.filled(f"m{t}", b)[0], 1)

            def aggregate(b, bank, mj_h, mj_l):
                bank.wait_read(pe, b, "m0", "m1", into="a")
                for t in range(T):
                    n = 0
                    for k in range(T):
                        for part in (mj_h, mj_l):
                            ins = nc.tensor.matmul(bank.half("a")[:, t], adjt_r[:, k, rows_cut(t)], part[:, k],
                                                   start=(n == 0), stop=(n == 2 * T - 1))
                            n += 1
                ins.then_inc(bank.filled("a", b)[0], 1)

            def project_qk(b, tile, which):
                bank3.wait_read(pe, b, "xt", into=tile)
                for m in range(K):
                    ins = product3(bank3.half(tile)[:, m],
                                   parts(qkv_h[:, which], qkv_l[:, which], rows_cut(m)), parts(x2t_h, x2t_l))
                ins.then_inc(bank3.filled(tile, b)[0], 1)

            def project_v(b):
                wait(pe, bank3.vacant("v", b))
                for t in range(T):
                    ins = product3(bank3.half("v")[:, t], parts(x2t_h, x2t_l, rows_cut(t)),
                                   parts(qkv_h[:, 2], qkv_l[:, 2]))
                ins.then_inc(bank3.filled("v", b)[0], 1)

            def scores(b, h):
                g, at = h // 4, 32 * (h % 4)
                bank3.wait_read(pe, b, "q", "k", into=f"s{h}")
                for t in range(T):
                    ins = nc.tensor.matmul(bank3.half(f"s{h}")[:, t], q_t[at:at + DH, g, rows_cut(t)],
                                           k_t[at:at + DH, g], start=True, stop=True, tile_position=(at, 0))
                ins.then_inc(bank3.filled(f"s{h}", b)[0], 1)

            def attend_3(b, g):
                bank3.wait_read(pe, b, "v", *(f"t{h}" for h in range(4 * g, 4 * g + 4)), into=f"o{g}")
                for k in range(T):
                    for j in range(4):
                        h = 4 * g + j
                        ins = nc.tensor.matmul(bank3.ap(f"o{g}")[32 * j:32 * j + 32, 0:N],
                                               v_s[:, k, h * DH:(h + 1) * DH], pt3[:, h % PT3, k],
                                               start=(k == 0), stop=(k == T - 1), tile_position=(0, 32 * j))
                ins.then_inc(bank3.filled(f"o{g}", b)[0], 1)

            def project_o(b):
                bank3.wait_read(pe, b, "o0", "o1", into="o")
                for t in range(T):
                    for k in range(K):
                        ins = nc.tensor.matmul(bank3.half("o")[:, t], att_t[:, k, rows_cut(t)], wo_s[:, k],
                                               start=(k == 0), stop=(k == K - 1))
                ins.then_inc(bank3.filled("o", b)[0], 1)

            def iteration(b1, b2, b3):
                on(b2, project_2, 0)
                on(b3, turn_rows, bank3, "xt", x2, (x2_ready, b3 + 1) if b3 is not None else None)
                on(b2, project_2, 1)
                on(b3, project_qk, "q", 0)
                on(b3, project_qk, "k", 1)
                on(b1, project_1, 0, 0)
                on(b1, project_1, 0, 1)
                on(b2, coeff_rows_2)
                on(b3, project_v)
                on(b3, scores, 0)
                on(b1, project_1, 1, 0)
                on(b1, project_1, 1, 1)
                on(b1, coeff_rows_1)
                on(b2, pairs_2)
                on(b3, scores, 1)
                on(b3, scores, 2)
                on(b3, turn_3, 0)
                on(b1, pairs_1, 0)
                on(b3, scores, 3)
                on(b3, scores, 4)
                on(b2, turn_2)
                on(b3, turn_3, 1)
                on(b2, attend_2)
                on(b3, scores, 5)
                on(b3, turn_3, 2)
                on(b1, turn_1, 0)
                on(b3, scores, 6)
                on(b3, turn_3, 3)
                on(b3, turn_3, 4)
                on(b1, pairs_1, 1)
                on(b1, attend_1, 0)
                on(b2, feed_forward_1)
                on(b3, scores, 7)
                on(b3, turn_3, 5)
                on(b3, attend_3, 0)
                on(b2, feed_forward_2)
                on(b3, turn_3, 6)
                on(b1, turn_1, 1)
                on(b1, pairs_1, 2)
                on(b1, attend_1, 1)
                on(b3, turn_3, 7)
                on(b3, attend_3, 1)
                on(b3, project_o)
                on(b1, turn_1, 2)
                on(b2, turn_rows, bank2, "xt", x1, (x1_ready, b2 + 1) if b2 is not None else None)
                on(b1, pairs_1, 3)
                on(b1, attend_1, 2)
                on(b2, own_and_messages, bank2, 0, x1t_h, x1t_l, "xt", l1_h, l1_l)
                on(b2, own_and_messages, bank2, 1, x1t_h, x1t_l, "xt", l1_h, l1_l)
                on(b3, turn_rows, bank3, "x3t", x3, (x3_ready, b3 + 1) if b3 is not None else None)
                on(b2, aggregate, bank2, mj1_h, mj1_l)
                on(b1, turn_1, 3)
                on(b3, own_and_messages, bank3, 0, x3t_h, x3t_l, "x3t", l3_h, l3_l)
                on(b3, own_and_messages, bank3, 1, x3t_h, x3t_l, "x3t", l3_h, l3_l)
                on(b3, aggregate, bank3, mj3_h, mj3_l)
                on(b1, attend_1, 3)

            pipeline(pe, iteration)


def kernel(**inputs):
    import numpy as _np
    import concourse.bacc as _bacc
    from concourse import mybir as _mybir
    from concourse.bass_utils import run_bass_kernel_spmd as _run

    x = _np.asarray(inputs["x"])
    adj = _np.asarray(inputs["adj"])
    row = _np.arange(P) % 32
    select = _np.stack([(row == 1) | (row == 3), _np.select([(row == 0) | (row == 2), (row == 1) | (row == 3)], [1, -1], 0),
                        (row == 0) | (row == 1), (row == 2) | (row == 3)], axis=1).astype(_np.float32)
    def columns(bias):
        return _np.asarray(bias).reshape(-1, P).T

    given = [
        ("x", x), ("xt", x.transpose(0, 2, 1)), ("adj", adj), ("adjt", adj.T),
        ("w_heads", inputs["L0_gnn_W_heads"]), ("a_heads", inputs["L0_gnn_a_heads"]),
        ("w_out", inputs["L0_gnn_W_out"]), ("a_out", inputs["L0_gnn_a_out"]),
        ("w1", inputs["L0_gnn_w1"]), ("b1", columns(inputs["L0_gnn_b1"])), ("w2", inputs["L0_gnn_w2"]), ("b2", inputs["L0_gnn_b2"]),
        ("gamma", inputs["L0_gnn_ln_gamma"]), ("beta", inputs["L0_gnn_ln_beta"]),
        ("l1_wt", _np.asarray(inputs["L1_gnn_W"]).T), ("l1_b", inputs["L1_gnn_b"]),
        ("wq_t", _np.asarray(inputs["L2_gnn_Wq"]).T), ("bq", columns(inputs["L2_gnn_bq"])),
        ("wk_t", _np.asarray(inputs["L2_gnn_Wk"]).T), ("bk", columns(inputs["L2_gnn_bk"])),
        ("wv_t", _np.asarray(inputs["L2_gnn_Wv"]).T), ("bv", inputs["L2_gnn_bv"]),
        ("wo_t", _np.asarray(inputs["L2_gnn_Wo"]).T), ("bo", inputs["L2_gnn_bo"]),
        ("l3_wt", _np.asarray(inputs["L3_gnn_W"]).T), ("l3_b", inputs["L3_gnn_b"]),
        ("ident", _np.eye(P, dtype=_np.float32)), ("select", select),
    ]
    nc = _bacc.Bacc("TRN2", target_bir_lowering=False, num_devices=1)
    arrays, args = {}, []
    for name, a in given:
        a = _np.ascontiguousarray(a)
        arrays[f"in_{name}_dram"] = a
        args.append(nc.dram_tensor(f"in_{name}_dram", a.shape, _mybir.dt.from_np(a.dtype), kind="ExternalInput").ap())
    args.append(nc.dram_tensor("out_dram", x.shape, _mybir.dt.from_np(x.dtype), kind="ExternalOutput").ap())
    build(nc, *args)
    r = _run(nc, [arrays], core_ids=[0])
    return r.results[0]["out_dram"]
```

```python
from contextlib import ExitStack

import numpy as np

import concourse.bass as bass
from concourse import mybir

P = 128
F32 = mybir.dt.float32
F32R = mybir.dt.float32r
I32 = mybir.dt.int32
ALU = mybir.AluOpType
ACT = mybir.ActivationFunctionType
AX = mybir.AxisListType

GAT_MASK = -1e11
ATT_MASK = -1e30
SLOPE = 0.01
EPS = 1e-5

TILES_1 = ["wh00", "wh01", "wh10", "wh11", "f",
           "e0", "t0", "e1", "av0", "t1", "e2", "av1", "t2", "e3", "av2", "t3", "av3"]
TILES_2 = ["wh0", "wh1", "f", "e", "t", "av", "hid", "y"]
TILES_3 = ["xt", "m0", "m1", "a", "x2t", "q", "k", "v"]
TILES_4 = ["s0", "s1", "s2", "t0", "s3", "s4", "t1", "s5", "t2", "s6", "t3", "t4",
           "s7", "t5", "o0", "t6", "t7", "o1", "o", "x3t", "m0", "m1", "a"]


class Banks:

    def __init__(self, ctx, nc, name, tiles, n):
        self.tiles, self.n = tiles, n
        self.bank = [ctx.enter_context(nc.psum_tensor(f"{name}_bank{r}", [P, 512], F32)) for r in range(n)]
        self.full = [ctx.enter_context(nc.semaphore(f"{name}_full{r}")) for r in range(n)]
        self.read = [ctx.enter_context(nc.semaphore(f"{name}_read{r}")) for r in range(n)]

    def ring(self, tile):
        i = self.tiles.index(tile)
        r = i % self.n
        return r, len(range(r, i, self.n)), len(range(r, len(self.tiles), self.n))

    def ap(self, tile):
        return self.bank[self.ring(tile)[0]]

    def half(self, tile):
        return self.ap(tile)[:].rearrange("p (t n) -> p t n", t=2)

    def filled(self, tile, b):
        r, use, per = self.ring(tile)
        return self.full[r], b * per + (use + 1)

    def was_read(self, tile, b):
        r, use, per = self.ring(tile)
        return self.read[r], b * per + (use + 1)

    def vacant(self, tile, b):
        r, use, per = self.ring(tile)
        return self.read[r], b * per + use

    def wait_read(self, eng, b, *tiles, into):
        r, use, _ = self.ring(into)
        counts = {r: use}
        for tile in tiles:
            r, use, _ = self.ring(tile)
            counts[r] = max(counts.get(r, 0), use + 1)
        for r, count in counts.items():
            wait(eng, (self.read[r], b * len(range(r, len(self.tiles), self.n)) + count))


def wait(eng, sem_value):
    sem, value = sem_value
    if not isinstance(value, int) or value > 0:
        eng.wait_ge(sem, value)


def build(nc, x, xt, adj, adjt, w_heads, a_heads, w_out, a_out, w1, b1, w2, b2, gamma, beta,
          l1_wt, l1_b, wq_t, bq, wk_t, bk, wv_t, bv, wo_t, bo, l3_wt, l3_b, ident_d, select_d, out):
    B, N, D = x.shape
    H = w_heads.shape[0]
    HM, DH = 8, 32
    PT3 = 6
    R3 = 3
    T = N // P
    K = D // P
    KH = H * D // P
    assert T == 2 and K == 2 and D == HM * DH and B >= 5
    SCALE = float(np.float32(1.0) / np.sqrt(np.float32(DH)))

    with ExitStack() as ctx:
        def sb(name, shape, dt=F32):
            return ctx.enter_context(nc.sbuf_tensor(name, shape, dt))

        def sem(name):
            return ctx.enter_context(nc.semaphore(name))

        wh_h, wh_l = sb("wh_h", [P, K, H * D], F32R), sb("wh_l", [P, K, H * D], F32R)
        wa_h, wa_l = sb("wa_h", [P, K, P], F32R), sb("wa_l", [P, K, P], F32R)
        l1_h, l1_l = sb("l1_h", [P, K, 2 * D], F32R), sb("l1_l", [P, K, 2 * D], F32R)
        l3_h, l3_l = sb("l3_h", [P, K, 2 * D], F32R), sb("l3_l", [P, K, 2 * D], F32R)
        qkv_h, qkv_l = sb("qkv_h", [P, 3, K, D], F32R), sb("qkv_l", [P, 3, K, D], F32R)
        wout_h, wout_l = sb("wout_h", [P, KH, D + 4], F32R), sb("wout_l", [P, KH, D + 4], F32R)
        w1_s, w2_s, wo_s = sb("w1_s", [P, K, D]), sb("w2_s", [P, K, D]), sb("wo_s", [P, K, D])
        ident = sb("ident_s", [P, P])
        select = sb("select_s", [P, 4])
        adjt_r = sb("adjt_r", [P, T, N], F32R)
        gat_mask, att_mask = sb("gat_mask", [P, T, N]), sb("att_mask", [P, T, N])
        deg = sb("deg", [P, T])
        rows = sb("rows", [P, 5, D])
        GAMMA, BETA, B2, BO, BV = range(5)
        l1_db, l3_db = sb("l1_db", [P, T, D]), sb("l3_db", [P, T, D])
        b1_c, bq_c, bk_c = sb("b1_c", [P, K]), sb("bq_c", [P, K]), sb("bk_c", [P, K])
        minus_half = sb("minus_half", [P, T])

        xt_s = sb("xt_s", [P, K, N])
        xt_h, xt_l = sb("xt_h", [P, K, N], F32R), sb("xt_l", [P, K, N], F32R)
        feats_h, feats_l = sb("feats_h", [P, T, H * D], F32R), sb("feats_l", [P, T, H * D], F32R)
        f_hi, f_sel = sb("f_hi", [P, N], F32R), sb("f_sel", [P, N])
        g_query, g_key = sb("g_query", [P, N], F32R), sb("g_key", [P, N], F32R)
        p1 = sb("p1", [P, 2, T, N])
        pt1_h, pt1_l = sb("pt1_h", [P, 2, T, N], F32R), sb("pt1_l", [P, 2, T, N], F32R)
        max1, neg1, nmax1 = sb("max1", [P, 2, T]), sb("neg1", [P, 2, T]), sb("nmax1", [P, 2, T])
        sum1, inv1 = sb("sum1", [P, 2, T]), sb("inv1", [P, 2, T])
        elu1 = sb("elu1", [P, 2, K, N])
        heads_h, heads_l = sb("heads_h", [P, KH, N], F32R), sb("heads_l", [P, KH, N], F32R)
        x_s = sb("x_s", [P, T, D])
        f2_hi, g2_query, g2_key = [heads_h[0:4, i] for i in range(3)]
        feats2_h, feats2_l = sb("feats2_h", [P, T, D], F32R), sb("feats2_l", [P, T, D], F32R)
        coeff2 = sb("coeff2", [P, T, 4])
        p2 = sb("p2", [P, T, N])
        f2_sel, hid = p2[0:4, 0], p2
        pt2_h, pt2_l = sb("pt2_h", [P, T, N], F32R), sb("pt2_l", [P, T, N], F32R)
        max2, neg2, nmax2 = sb("max2", [P, T]), sb("neg2", [P, T]), sb("nmax2", [P, T])
        sum2, inv2 = sb("sum2", [P, T]), sb("inv2", [P, T])
        out2_t = sb("out2_t", [P, K, N])
        x1, x2 = sb("x1", [P, T, D]), sb("x2", [P, T, D])
        y = x1
        xrt_h, xrt_l = sb("xrt_h", [P, K, N], F32R), sb("xrt_l", [P, K, N], F32R)
        mj1_h, mj1_l = sb("mj1_h", [P, T, D], F32R), sb("mj1_l", [P, T, D], F32R)
        q_s, k_s, v_s = sb("q_s", [P, K, N]), sb("k_s", [P, K, N]), sb("v_s", [P, T, D])
        x2b = sb("x2b", [P, T, D])
        p3, pt3 = sb("p3", [P, R3, T, N]), sb("pt3", [P, PT3, T, N])
        x3t_h, x3t_l = sb("x3t_h", [P, K, N], F32R), sb("x3t_l", [P, K, N], F32R)
        mj3_h, mj3_l = sb("mj3_h", [P, T, D], F32R), sb("mj3_l", [P, T, D], F32R)
        max3, nmax3 = sb("max3", [P, R3, T]), sb("nmax3", [P, R3, T])
        sum3, inv3 = sb("sum3", [P, R3, T]), sb("inv3", [P, R3, T])
        att_t, x3 = sb("att_t", [P, K, N]), sb("x3", [P, T, D])
        x4 = x3
        stats, mean_var = sb("stats", [P, 5, T, 6]), sb("mean_var", [P, 5, T, 2])
        var_eps, rstd = sb("var_eps", [P, 5, T]), sb("rstd", [P, 5, T])

        carrier = sb("carrier", [1, 1])

        wa2 = sb("wa2", [P, KH, 4])

        def wide(buf):
            return buf.rearrange("p a t n -> p (a t n)").rearrange("p (k n) -> p k n", k=K)

        stage_wh, stage_l1, stage_l3 = wide(pt3[:, 0:4]), wide(pt3[:, 4:6]), wide(p3[:, 0:2])
        stage_qkv = [x2b, x3, v_s]
        stage_wout = [x1, x2, out2_t, p2]
        stage_ah = [buf[:, i] for buf in (p1, elu1) for i in range(2)]
        stage_ao = att_t[:]
        adj_i, adjt_i = att_mask[:].bitcast(I32), p3[:, 2].bitcast(I32)
        wa = f_sel[:].rearrange("p (k n) -> p k n", k=K)

        bank1 = Banks(ctx, nc, "s1", TILES_1, 3)
        bank2 = Banks(ctx, nc, "s2", TILES_2, 1)
        bank3 = Banks(ctx, nc, "s3", TILES_3, 1)
        bank4 = Banks(ctx, nc, "s4", TILES_4, 3)

        junk = bank1.bank[2][:, 0:D]
        adj_f = bank1.bank[1][:].rearrange("p (t n) -> p t n", t=T)

        loaded_stage, loaded_adj, loaded_rest = sem("loaded_stage"), sem("loaded_adj"), sem("loaded_rest")
        split_hi, wa_ready, wout_ready = sem("split_hi"), sem("wa_ready"), sem("wout_ready")
        setup_step, setup_act, setup_dve = sem("setup_step"), sem("setup_act"), sem("setup_dve")
        xt_loaded, xt_hi_ready, xt_lo_ready = sem("xt_loaded"), sem("xt_hi_ready"), sem("xt_lo_ready")
        g_ready, logits1_ready, exp1_done = sem("g_ready"), sem("logits1_ready"), sem("exp1_done")
        inv1_ready, probs1_ready, elu1_exp = sem("inv1_ready"), sem("probs1_ready"), sem("elu1_exp")
        x_loaded, xb_ready = sem("x_loaded"), sem("xb_ready")
        g2_ready, logits2_ready, exp2_done = sem("g2_ready"), sem("logits2_ready"), sem("exp2_done")
        inv2_ready, probs2_ready, elu2_exp = sem("inv2_ready"), sem("probs2_ready"), sem("elu2_exp")
        yn_ready, res1_ready = sem("yn_ready"), sem("res1_ready")
        feats_hi, pt1_hi, heads_hi, heads_lo = sem("feats_hi"), sem("pt1_hi"), sem("heads_hi"), sem("heads_lo")
        feats2_hi, pt2_hi = sem("feats2_hi"), sem("pt2_hi")
        x1_ready, x1b_ready, x1t_hi, mj1_hi, x2_ready = (sem("x1_ready"), sem("x1b_ready"), sem("x1t_hi"),
                                                          sem("mj1_hi"), sem("x2_ready"))
        x2b_ready, x2t_hi, logits3_ready = sem("x2b_ready"), sem("x2t_hi"), sem("logits3_ready")
        exp3_done, inv3_ready, probs3_ready = sem("exp3_done"), sem("inv3_ready"), sem("probs3_ready")
        x3_ready, x3b_ready, x3t_hi, mj3_hi, x4_ready = (sem("x3_ready"), sem("x3b_ready"), sem("x3t_hi"),
                                                          sem("mj3_hi"), sem("x4_ready"))
        stored = sem("stored")
        var_ready = [sem(f"var_ready{i}") for i in range(5)]
        rstd_ready = [sem(f"rstd_ready{i}") for i in range(5)]
        dve_step = [sem(f"dve_step{i}") for i in (1, 2, 3, 4)]
        pool_step = sem("pool_step")
        DVE_STEPS = (9, 7, 2, 4)

        block = ctx.enter_context(nc.Block())

        def pipeline(eng, iteration):
            iteration(0, None, None, None)
            iteration(1, 0, None, None)
            iteration(2, 1, 0, None)
            iteration(3, 2, 1, 0)
            with eng.Fori(4, B) as i:
                iteration(i, i - 1, i - 2, i - 3)
            iteration(None, B - 1, B - 2, B - 3)
            iteration(None, None, B - 1, B - 2)
            iteration(None, None, None, B - 1)

        def on(b, step, *args):
            if b is not None:
                step(b, *args)

        def rows_of(dram, b):
            return dram[bass.ds(b, 1)].rearrange("b (t p) n -> p (b t) n", p=P)

        @block.sync
        def _(sp):
            tiled = "(k p) n -> p k n"
            for dst, src in ((stage_wh.rearrange("p k (h n) -> p k h n", h=H),
                              w_heads.rearrange("h (k p) n -> p k h n", p=P)),
                             (stage_l1[:, :, 0:D], l1_wt[0:D].rearrange(tiled, p=P)),
                             (stage_l1[:, :, D:], l1_wt[D:].rearrange(tiled, p=P)),
                             (stage_l3[:, :, 0:D], l3_wt[0:D].rearrange(tiled, p=P)),
                             (stage_l3[:, :, D:], l3_wt[D:].rearrange(tiled, p=P)),
                             *((stage_wout[i][:], w_out[i * K * P:(i + 1) * K * P].rearrange(tiled, p=P))
                               for i in range(KH // K)),
                             *((stage_qkv[i][:], (wq_t, wk_t, wv_t)[i].rearrange(tiled, p=P)) for i in range(3))):
                if len(dst.shape) == 4:
                    for k in range(K):
                        sp.dma_start(dst[:, k], src[:, k]).then_inc(loaded_stage, 16)
                else:
                    sp.dma_start(dst, src).then_inc(loaded_stage, 16)

            def load_xt(b):
                wait(sp, (xt_lo_ready, b))
                sp.dma_start(xt_s[:], rows_of(xt, b)).then_inc(xt_loaded, 16)

            def load_x(b):
                wait(sp, (res1_ready, b))
                sp.dma_start(x_s[:], rows_of(x, b)).then_inc(x_loaded, 16)

            def store(b):
                sp.wait_ge(x4_ready, b + 1)
                sp.dma_start(rows_of(out, b), x4[:]).then_inc(stored, 16)

            def iteration(b1, b2, b3, b4):
                on(b1, load_xt)
                on(b2, load_x)
                on(b4, store)

            pipeline(sp, iteration)
            sp.wait_ge(stored, 16 * B)

        N_STAGE = 2 + 4 + KH // K + 3
        N_ADJ = 2
        N_REST = 3 + 2 + 9 + 7 + 3

        @block.gpsimd
        def _(pool):
            nc.gpsimd.memset(minus_half[:], -0.5).then_inc(pool_step, 1)
            pool.wait_ge(pool_step, 1)
            pool.wait_ge(loaded_rest, 16 * N_REST)
            pool.wait_ge(setup_dve, 1)

            def both(row):
                return rows[:, row, :].unsqueeze(1).broadcast_to([P, T, D])

            def spread(small):
                return small.unsqueeze(2).broadcast_to([P, T, N])

            def normalise(probs, inv, ready, done):
                wait(pool, ready)
                nc.gpsimd.tensor_tensor(probs, probs, spread(inv), ALU.mult).then_inc(done, 1)

            def probs_1(b, h):
                normalise(p1[:, h % 2], inv1[:, h % 2], (inv1_ready, b * H + h + 1), probs1_ready)

            def probs_2(b):
                normalise(p2[:], inv2[:], (inv2_ready, b + 1), probs2_ready)

            def probs_3(b, h):
                normalise(p3[:, h % R3], inv3[:, h % R3], (inv3_ready, b * HM + h + 1), probs3_ready)

            def inverse_root(b, i):
                pool.wait_ge(var_ready[i], b + 1)
                nc.gpsimd.tensor_tensor(rstd[:, i], var_eps[:, i], minus_half[:], ALU.pow).then_inc(rstd_ready[i], 1)

            def add_beta(b):
                pool.wait_ge(x_loaded, 16 * (b + 1))
                nc.gpsimd.tensor_tensor(x_s[:], x_s[:], both(BETA), ALU.add).then_inc(xb_ready, 1)

            def residual_1(b):
                pool.wait_ge(yn_ready, b + 1)
                nc.gpsimd.tensor_tensor(x1[:], y[:], both(GAMMA), ALU.mult).then_inc(pool_step, 1)
                pool.wait_ge(pool_step, b + 2)
                pool.wait_ge(xb_ready, b + 1)
                nc.gpsimd.tensor_tensor(x1[:], x1[:], x_s[:], ALU.add).then_inc(res1_ready, 1)

            def heads_lower(b, h):
                pool.wait_ge(heads_hi, b * H + h + 1)
                nc.gpsimd.tensor_tensor(heads_l[:, 2 * h:2 * h + 2], elu1[:, h % 2],
                                        heads_h[:, 2 * h:2 * h + 2].bitcast(F32), ALU.subtract).then_inc(heads_lo, 1)

            def add_const(b, rows_in, turned, const, done):
                wait(pool, turned)
                nc.gpsimd.tensor_tensor(rows_in[:], rows_in[:], const, ALU.add).then_inc(done, 1)

            def x1_const(b):
                add_const(b, x1, bank3.filled("xt", b), l1_db[:], x1b_ready)

            def x2_const(b):
                pool.wait_ge(x2_ready, b + 1)
                wait(pool, bank4.was_read("o", b - 1))
                nc.gpsimd.tensor_tensor(x2b[:], x2[:], both(BO), ALU.add).then_inc(x2b_ready, 1)

            def x3_const(b):
                add_const(b, x3, bank4.filled("x3t", b), l3_db[:], x3b_ready)

            def iteration(b1, b2, b3, b4):
                on(b4, probs_3, 0)
                on(b4, probs_3, 1)
                on(b4, probs_3, 2)
                on(b1, probs_1, 0)
                on(b4, probs_3, 3)
                on(b4, probs_3, 4)
                on(b3, x1_const)
                on(b4, probs_3, 5)
                on(b2, add_beta)
                on(b4, probs_3, 6)
                on(b1, heads_lower, 0)
                on(b1, probs_1, 1)
                on(b4, probs_3, 7)
                on(b2, probs_2)
                on(b3, inverse_root, 2)
                on(b1, heads_lower, 1)
                on(b1, probs_1, 2)
                on(b4, inverse_root, 3)
                on(b4, x3_const)
                on(b1, heads_lower, 2)
                on(b1, probs_1, 3)
                on(b2, inverse_root, 0)
                on(b3, x2_const)
                on(b2, residual_1)
                on(b4, inverse_root, 4)
                on(b1, heads_lower, 3)
                on(b2, inverse_root, 1)

            pipeline(pool, iteration)

        @block.scalar
        def _(act):
            tiled = "(k p) n -> p k n"
            act.dma_start(adj_i, adj.rearrange("(t p) n -> p t n", p=P)).then_inc(loaded_adj, 16)
            act.dma_start(adjt_i, adjt.rearrange("(t p) n -> p t n", p=P)).then_inc(loaded_adj, 16)
            for dst, src in ((w1_s, w1), (w2_s, w2), (wo_s, wo_t)):
                act.dma_start(dst[:], src.rearrange(tiled, p=P)).then_inc(loaded_rest, 16)
            act.dma_start(ident[:], ident_d).then_inc(loaded_rest, 16)
            act.dma_start(select[:], select_d).then_inc(loaded_rest, 16)
            for h in range(H):
                for half in range(2):
                    act.dma_start(stage_ah[h][:, half], a_heads[h:h + 1, half * D:(half + 1) * D]
                                  .broadcast_to([P, D])).then_inc(loaded_rest, 16)
            act.dma_start(stage_ao, a_out.rearrange("(o t n) -> o t n", o=1, t=2)
                          .broadcast_to([P, 2, D])).then_inc(loaded_rest, 16)
            for r, src in enumerate((gamma, beta, b2, bo, bv)):
                act.dma_start(rows[:, r], src.rearrange("(o n) -> o n", o=1).broadcast_to([P, D])).then_inc(loaded_rest, 16)
            for dst, src in ((l1_db, l1_b), (l3_db, l3_b)):
                act.dma_start(dst[:, T - 1], src.rearrange("(o n) -> o n", o=1).broadcast_to([P, D])).then_inc(loaded_rest, 16)
            for dst, src in ((b1_c, b1), (bq_c, bq), (bk_c, bk)):
                act.dma_start(dst[:], src).then_inc(loaded_rest, 16)

            act.wait_ge(loaded_stage, 16 * N_STAGE)
            for dst, src in ((wh_h[:], stage_wh), (l1_h[:], stage_l1), (l3_h[:], stage_l3)):
                nc.scalar.activation(dst, src, ACT.Copy).then_inc(split_hi, 1)
            for i in range(3):
                nc.scalar.activation(qkv_h[:, i], stage_qkv[i][:], ACT.Copy).then_inc(split_hi, 1)
            for i in range(KH // K):
                nc.scalar.activation(wout_h[:, K * i:K * (i + 1), 0:D], stage_wout[i][:], ACT.Copy).then_inc(split_hi, 1)
            act.wait_ge(wa_ready, 1)
            nc.scalar.activation(wa_h[:], wa, ACT.Copy).then_inc(split_hi, 1)
            act.wait_ge(wa_ready, 2)
            nc.scalar.activation(wout_h[:, :, D:], wa2[:], ACT.Copy).then_inc(split_hi, 1)
            act.wait_ge(loaded_adj, 16 * N_ADJ)
            nc.scalar.activation(adjt_r[:], adjt_i, ACT.Copy).then_inc(setup_act, 1)
            act.wait_ge(loaded_rest, 16 * N_REST)
            act.wait_ge(setup_dve, 3)

            def xt_upper(b):
                act.wait_ge(xt_loaded, 16 * (b + 1))
                wait(act, bank1.filled("f", b - 1))
                nc.scalar.activation(xt_h[:], xt_s[:], ACT.Copy).then_inc(xt_hi_ready, 1)

            def feats_copy(b, t, half):
                tile = f"wh{t}{half}"
                wait(act, bank1.filled(tile, b))
                if (t, half) == (0, 0):
                    wait(act, bank1.filled("av3", b - 1))
                nc.scalar.activation(feats_h[:, t, half * 512:(half + 1) * 512], bank1.ap(tile)[:], ACT.Copy)\
                    .then_inc(feats_hi, 1)

            def coeff_parts(b, bank, tile, n, hi, sel, used):
                wait(act, bank.filled(tile, b))
                wait(act, (used, b))
                nc.scalar.activation(hi[:], bank.ap(tile)[0:n, 0:N], ACT.Copy)
                nc.scalar.activation(sel[:], bank.ap(tile)[0:n, 0:N], ACT.Copy, scale=select[0:n, 0:1])\
                    .then_inc(bank.was_read(tile, b)[0], 1)

            def softmax_exp(probs, nmax, sums, scale, ready, done):
                wait(act, ready)
                for t in range(T):
                    last = nc.scalar.activation(probs[:, t], probs[:, t], ACT.Exp, bias=nmax[:, t:t + 1], scale=scale,
                                                accum_out=sums[:, t:t + 1])
                last.then_inc(done, 1)

            def exp_1(b, h):
                softmax_exp(p1[:, h % 2], nmax1[:, h % 2], sum1[:, h % 2], 1.0, (logits1_ready, b * H + h + 1), exp1_done)

            def exp_2(b):
                softmax_exp(p2[:], nmax2[:], sum2[:], 1.0, (logits2_ready, b + 1), exp2_done)

            def exp_3(b, h):
                softmax_exp(p3[:, h % R3], nmax3[:, h % R3], sum3[:, h % R3], SCALE, (logits3_ready, b * HM + h + 1),
                            exp3_done)

            def probs_t_1(b, h):
                wait(act, bank1.filled(f"t{h}", b))
                wait(act, bank1.filled(f"av{h - 2}", b) if h >= 2 else bank1.filled(f"av{h + 2}", b - 1))
                nc.scalar.activation(pt1_h[:, h % 2], bank1.half(f"t{h}"), ACT.Copy).then_inc(pt1_hi, 1)

            def probs_t_2(b):
                wait(act, bank2.filled("t", b))
                wait(act, bank2.filled("av", b - 1))
                nc.scalar.activation(pt2_h[:], bank2.half("t"), ACT.Copy).then_inc(pt2_hi, 1)

            def probs_t_3(b, h):
                wait(act, bank4.filled(f"t{h}", b))
                wait(act, bank4.filled("o0", b) if h >= PT3 else bank4.filled("o1", b - 1))
                nc.scalar.activation(pt3[:, h % PT3], bank4.half(f"t{h}"), ACT.Copy)\
                    .then_inc(bank4.was_read(f"t{h}", b)[0], 1)

            def elu_exp_1(b, h):
                wait(act, bank1.filled(f"av{h}", b))
                wait(act, (heads_lo, b * H + h - 1))
                nc.scalar.activation(elu1[:, h % 2], bank1.half(f"av{h}"), ACT.Exp).then_inc(elu1_exp, 1)

            def heads_upper(b, h):
                wait(act, bank1.was_read(f"av{h}", b))
                wait(act, bank2.filled("e", b - 1))
                nc.scalar.activation(heads_h[:, 2 * h:2 * h + 2], elu1[:, h % 2], ACT.Copy).then_inc(heads_hi, 1)

            def elu_exp_2(b):
                wait(act, bank2.filled("av", b))
                wait(act, bank2.filled("y", b - 1))
                nc.scalar.activation(out2_t[:], bank2.half("av"), ACT.Exp).then_inc(elu2_exp, 1)

            def feats2_upper(b, t):
                wait(act, bank2.filled(f"wh{t}", b))
                if t == 0:
                    wait(act, bank2.filled("av", b - 1))
                nc.scalar.activation(feats2_h[:, t], bank2.ap(f"wh{t}")[:, 0:D], ACT.Copy).then_inc(feats2_hi, 1)

            def hidden(b):
                wait(act, bank2.filled("hid", b))
                wait(act, bank2.filled("y", b - 1))
                for m in range(K):
                    last = nc.scalar.activation(hid[:, m], bank2.half("hid")[:, m], ACT.Relu, bias=b1_c[:, m:m + 1])
                last.then_inc(bank2.was_read("hid", b)[0], 1)

            def upper(b, bank, tile, dst, used, done):
                wait(act, bank.filled(tile, b))
                wait(act, used)
                nc.scalar.activation(dst, bank.half(tile), ACT.Copy).then_inc(done, 1)

            def mj_upper(b, bank, t, dst, done):
                wait(act, bank.filled(f"m{t}", b))
                nc.scalar.activation(dst[:, t], bank.ap(f"m{t}")[:, D:], ACT.Copy).then_inc(done, 1)

            def qk_copy(b, tile, dst, bias):
                wait(act, bank3.filled(tile, b))
                wait(act, bank4.filled("s7", b - 1))
                for m in range(K):
                    last = nc.scalar.activation(dst[:, m], bank3.half(tile)[:, m], ACT.Identity, bias=bias[:, m:m + 1])
                last.then_inc(bank3.was_read(tile, b)[0], 1)

            def att_copy(b, g):
                wait(act, bank4.filled(f"o{g}", b))
                wait(act, bank4.filled("o", b - 1))
                nc.scalar.activation(att_t[:, g], bank4.ap(f"o{g}")[:, 0:N], ACT.Copy).then_inc(bank4.was_read(f"o{g}", b)[0], 1)

            def coeff_parts_1(b):
                coeff_parts(b, bank1, "f", P, f_hi, f_sel, g_ready)

            def coeff_parts_2(b):
                coeff_parts(b, bank2, "f", 4, f2_hi, f2_sel, g2_ready)

            def x1t_upper(b):
                upper(b, bank3, "xt", xrt_h[:], bank3.filled("v", b - 1), x1t_hi)

            def x2t_upper(b):
                upper(b, bank3, "x2t", xrt_h[:], bank3.filled("m1", b), x2t_hi)

            def x3t_upper(b):
                upper(b, bank4, "x3t", x3t_h[:], bank4.filled("m1", b - 1), x3t_hi)

            def mj1_upper(b, t):
                mj_upper(b, bank3, t, mj1_h, mj1_hi)

            def mj3_upper(b, t):
                mj_upper(b, bank4, t, mj3_h, mj3_hi)

            def queries(b):
                qk_copy(b, "q", q_s, bq_c)

            def keys(b):
                qk_copy(b, "k", k_s, bk_c)

            def iteration(b1, b2, b3, b4):
                on(b1, xt_upper)
                on(b1, feats_copy, 0, 0)
                on(b4, exp_3, 0)
                on(b2, feats2_upper, 0)
                on(b1, feats_copy, 0, 1)
                on(b4, exp_3, 1)
                on(b1, feats_copy, 1, 0)
                on(b1, feats_copy, 1, 1)
                on(b1, coeff_parts_1)
                on(b4, probs_t_3, 0)
                on(b4, exp_3, 2)
                on(b4, probs_t_3, 1)
                on(b4, exp_3, 3)
                on(b3, x1t_upper)
                on(b1, exp_1, 0)
                on(b2, feats2_upper, 1)
                on(b4, exp_3, 4)
                on(b4, probs_t_3, 2)
                on(b1, probs_t_1, 0)
                on(b4, exp_3, 5)
                on(b4, probs_t_3, 3)
                on(b2, coeff_parts_2)
                on(b4, probs_t_3, 4)
                on(b1, exp_1, 1)
                on(b1, elu_exp_1, 0)
                on(b4, exp_3, 6)
                on(b3, mj1_upper, 0)
                on(b1, heads_upper, 0)
                on(b4, probs_t_3, 5)
                on(b4, att_copy, 0)
                on(b4, exp_3, 7)
                on(b3, mj1_upper, 1)
                on(b2, exp_2)
                on(b1, probs_t_1, 1)
                on(b4, probs_t_3, 6)
                on(b2, probs_t_2)
                on(b4, probs_t_3, 7)
                on(b1, exp_1, 2)
                on(b1, elu_exp_1, 1)
                on(b4, att_copy, 1)
                on(b2, elu_exp_2)
                on(b1, heads_upper, 1)
                on(b3, x2t_upper)
                on(b1, probs_t_1, 2)
                on(b2, hidden)
                on(b4, x3t_upper)
                on(b1, exp_1, 3)
                on(b1, elu_exp_1, 2)
                on(b1, heads_upper, 2)
                on(b3, queries)
                on(b4, mj3_upper, 0)
                on(b4, mj3_upper, 1)
                on(b1, probs_t_1, 3)
                on(b3, keys)
                on(b1, elu_exp_1, 3)
                on(b1, heads_upper, 3)

            pipeline(act, iteration)

        @block.vector
        def _(dve):
            count = [0]

            def setup(ins):
                count[0] += 1
                ins.then_inc(setup_step, 1)
                dve.wait_ge(setup_step, count[0])

            dve.wait_ge(loaded_adj, 16 * N_ADJ)
            nc.vector.tensor_copy(adj_f, adj_i).then_inc(setup_step, 1)
            count[0] += 1
            dve.wait_ge(setup_step, count[0])
            nc.vector.tensor_scalar(gat_mask[:], adj_f, 0.0, GAT_MASK, ALU.is_le, ALU.mult)
            nc.vector.tensor_scalar(att_mask[:], adj_f, 0.0, ATT_MASK, ALU.is_equal, ALU.mult)
            setup(nc.vector.tensor_reduce(deg[:], adj_f, AX.X, ALU.add))
            setup(nc.vector.memset(wa, 0.0))
            dve.wait_ge(loaded_rest, 16 * N_REST)
            for t in range(T):
                nc.vector.tensor_scalar(l1_db[:, t], l1_db[:, T - 1], deg[:, t:t + 1], None, ALU.mult)
                last = nc.vector.tensor_scalar(l3_db[:, t], l3_db[:, T - 1], deg[:, t:t + 1], None, ALU.mult)
            last.then_inc(setup_dve, 1)
            dve.wait_ge(loaded_stage, 16 * N_STAGE)
            for k in range(K):
                for h in range(H):
                    for half in range(2):
                        c = 32 * h + 2 * half
                        setup(nc.vector.tensor_tensor_reduce(junk, stage_wh[:, k, h * D:(h + 1) * D],
                                                             stage_ah[h][:, half], 1.0, 0.0, ALU.mult, ALU.add,
                                                             wa[:, k, c:c + 1]))
            last = nc.vector.tensor_copy(wa.rearrange("p k (h c) -> p k h c", c=32)[:, :, :, 1:4:2],
                                         wa.rearrange("p k (h c) -> p k h c", c=32)[:, :, :, 0:4:2])
            last.then_inc(wa_ready, 1)
            for k in range(KH):
                for half in range(2):
                    setup(nc.vector.tensor_tensor_reduce(junk, stage_wout[k // K][:, k % K], stage_ao[:, half], 1.0, 0.0,
                                                         ALU.mult, ALU.add, wa2[:, k, 2 * half:2 * half + 1]))
            nc.vector.tensor_copy(wa2[:, :, 1:4:2], wa2[:, :, 0:4:2]).then_inc(wa_ready, 1)
            splits = [(wh_l[:], stage_wh, wh_h[:]), (l1_l[:], stage_l1, l1_h[:]), (l3_l[:], stage_l3, l3_h[:]),
                      *((qkv_l[:, i], stage_qkv[i][:], qkv_h[:, i]) for i in range(3)),
                      *((wout_l[:, K * i:K * (i + 1), 0:D], stage_wout[i][:], wout_h[:, K * i:K * (i + 1), 0:D])
                        for i in range(KH // K)),
                      (wa_l[:], wa, wa_h[:]), (wout_l[:, :, D:], wa2[:], wout_h[:, :, D:])]
            for n, (lo, src, hi) in enumerate(splits):
                dve.wait_ge(split_hi, n + 1)
                if n == len(splits) - 1:
                    dve.wait_ge(wa_ready, 2)
                last = nc.vector.tensor_tensor(lo, src, hi.bitcast(F32), ALU.subtract)
            last.then_inc(setup_dve, 2)
            dve.wait_ge(setup_dve, 3)

            steps = [0] * len(DVE_STEPS)

            def link(stage, b, ins, carried=True):
                steps[stage - 1] += 1
                ins.then_inc(dve_step[stage - 1], 1)
                done = dve_step[stage - 1], b * DVE_STEPS[stage - 1] + steps[stage - 1]
                wait(dve, done) if carried else wait_apart(done)

            def wait_apart(*sem_values):
                for sem_value in sem_values:
                    wait(dve, sem_value)
                nc.vector.memset(carrier[0:1, 0:1], 0.0)

            def xt_lower(b):
                dve.wait_ge(xt_hi_ready, b + 1)
                nc.vector.tensor_tensor(xt_l[:], xt_s[:], xt_h[:].bitcast(F32), ALU.subtract).then_inc(xt_lo_ready, 1)

            def feats_lower(b, t, half):
                tile, cut = f"wh{t}{half}", slice(half * 512, (half + 1) * 512)
                dve.wait_ge(feats_hi, b * 2 * T + 2 * t + half + 1)
                nc.vector.tensor_tensor(feats_l[:, t, cut], bank1.ap(tile)[:], feats_h[:, t, cut].bitcast(F32),
                                        ALU.subtract).then_inc(bank1.was_read(tile, b)[0], 1)

            def feats2_lower(b, t):
                dve.wait_ge(feats2_hi, b * T + t + 1)
                nc.vector.tensor_copy(coeff2[:, t], bank2.ap(f"wh{t}")[:, D:D + 4])
                nc.vector.tensor_tensor(feats2_l[:, t], bank2.ap(f"wh{t}")[:, 0:D], feats2_h[:, t].bitcast(F32),
                                        ALU.subtract).then_inc(bank2.was_read(f"wh{t}", b)[0], 1)

            def lower(b, bank, tile, dst, hi, hi_ready):
                wait(dve, hi_ready)
                nc.vector.tensor_tensor(dst, bank.half(tile), hi.bitcast(F32), ALU.subtract)\
                    .then_inc(bank.was_read(tile, b)[0], 1)

            def turned_lower(b, bank, tile, dst, hi, hi_ready):
                lower(b, bank, tile, dst, hi, (hi_ready, b + 1))

            def probs_t_lower_1(b, h):
                lower(b, bank1, f"t{h}", pt1_l[:, h % 2], pt1_h[:, h % 2], (pt1_hi, b * H + h + 1))

            def probs_t_lower_2(b):
                lower(b, bank2, "t", pt2_l[:], pt2_h[:], (pt2_hi, b + 1))

            def coefficients(b, stage, bank, n, hi, sel, gq, gk, last_scores, ready):
                wait(dve, bank.was_read("f", b))
                wait(dve, bank.filled(last_scores, b - 1))
                link(stage, b, nc.vector.scalar_tensor_tensor(out=sel[:], in0=hi[:].bitcast(F32), scalar=select[0:n, 1:2],
                                                              in1=sel[:], op0=ALU.mult, op1=ALU.add))
                nc.vector.tensor_scalar(gq[:], sel[:], select[0:n, 2:3], select[0:n, 3:4], ALU.mult, ALU.add)
                nc.vector.tensor_scalar(gk[:], sel[:], select[0:n, 3:4], select[0:n, 2:3], ALU.mult, ALU.add)\
                    .then_inc(ready, 1)

            def gat_logits(b, stage, bank, tile, e, mx, neg, nmax, e_free, done):
                wait_apart(bank.filled(tile, b), e_free)
                for t in range(T):
                    last = nc.vector.tensor_tensor_reduce(e[:, t], bank.half(tile)[:, t], gat_mask[:, t], 1.0, -3e38,
                                                          ALU.add, ALU.max, mx[:, t:t + 1])
                last.then_inc(bank.was_read(tile, b)[0], 1)
                wait(dve, bank.was_read(tile, b))
                link(stage, b, nc.vector.tensor_scalar(neg, mx, -1.0, None, ALU.mult))
                nc.vector.scalar_tensor_tensor(out=nmax, in0=neg, scalar=SLOPE, in1=neg, op0=ALU.mult, op1=ALU.min)
                nc.vector.scalar_tensor_tensor(out=e, in0=e, scalar=SLOPE, in1=e, op0=ALU.mult, op1=ALU.max)\
                    .then_inc(done, 1)

            def logits_1(b, h):
                gat_logits(b, 1, bank1, f"e{h}", p1[:, h % 2], max1[:, h % 2], neg1[:, h % 2], nmax1[:, h % 2],
                           bank1.filled(f"t{h - 2}", b) if h >= 2 else bank1.filled(f"t{h + 2}", b - 1), logits1_ready)

            def logits_2(b):
                gat_logits(b, 2, bank2, "e", p2[:], max2[:], neg2[:], nmax2[:], bank2.filled("t", b - 1), logits2_ready)

            def logits_3(b, h):
                tile = f"s{h}"
                if h < R3:
                    wait_apart(bank4.filled(tile, b))
                else:
                    wait_apart(bank4.filled(tile, b), bank4.filled(f"t{h - R3}", b))
                for t in range(T):
                    last = nc.vector.tensor_tensor_reduce(p3[:, h % R3, t], bank4.half(tile)[:, t], att_mask[:, t],
                                                          1.0, -3e38, ALU.add, ALU.max, max3[:, h % R3, t:t + 1])
                last.then_inc(bank4.was_read(tile, b)[0], 1)
                wait(dve, bank4.was_read(tile, b))
                nc.vector.tensor_scalar(nmax3[:, h % R3], max3[:, h % R3], -SCALE, None, ALU.mult).then_inc(logits3_ready, 1)

            def inverse(exp_done, inv_free, inv, sums, ready):
                wait(dve, exp_done)
                wait(dve, inv_free)
                nc.vector.reciprocal(inv, sums).then_inc(ready, 1)

            def inverse_1(b, h):
                inverse((exp1_done, b * H + h + 1), (probs1_ready, b * H + h - 1), inv1[:, h % 2], sum1[:, h % 2], inv1_ready)

            def inverse_2(b):
                inverse((exp2_done, b + 1), (probs2_ready, b), inv2[:], sum2[:], inv2_ready)

            def inverse_3(b, h):
                inverse((exp3_done, b * HM + h + 1), (probs3_ready, b * HM + h - 2), inv3[:, h % R3], sum3[:, h % R3], inv3_ready)

            def elu(b, stage, bank, tile, expd, exp_ready, dst):
                wait(dve, exp_ready)
                link(stage, b, nc.vector.tensor_scalar(expd, expd, 1.0, -1.0, ALU.min, ALU.add))
                nc.vector.tensor_tensor(dst, bank.half(tile), expd, ALU.max).then_inc(bank.was_read(tile, b)[0], 1)

            def elu_1(b, h):
                elu(b, 1, bank1, f"av{h}", elu1[:, h % 2], (elu1_exp, b * H + h + 1), elu1[:, h % 2])

            def elu_2(b):
                elu(b, 2, bank2, "av", out2_t[:], (elu2_exp, b + 1), out2_t[:])

            def statistics(b, stage, i, src):
                for t in range(T):
                    last = nc.vector.bn_stats(stats[:, i, t], src[:, t])
                link(stage, b, last, carried=False)
                for t in range(T):
                    last = nc.vector.bn_aggr(mean_var[:, i, t], stats[:, i, t])
                link(stage, b, last)
                nc.vector.tensor_scalar(var_eps[:, i], mean_var[:, i, :, 1], EPS, None, ALU.add).then_inc(var_ready[i], 1)

            def apply_norm(b, i, buf, done):
                dve.wait_ge(rstd_ready[i], b + 1)
                for t in range(T):
                    last = nc.vector.tensor_scalar(buf[:, t], buf[:, t], mean_var[:, i, t, 0:1], rstd[:, i, t:t + 1],
                                                   ALU.subtract, ALU.mult)
                last.then_inc(done, 1)

            def feed_forward_sum(b):
                wait(dve, bank2.filled("y", b))
                wait(dve, bank3.was_read("m1", b - 1))
                nc.vector.tensor_tensor(y[:], bank2.half("y"), rows[:, B2, :].unsqueeze(1).broadcast_to([P, T, D]),
                                        ALU.add).then_inc(bank2.was_read("y", b)[0], 1)
                wait(dve, bank2.was_read("y", b))
                statistics(b, 2, 0, y)

            def norm_0(b):
                apply_norm(b, 0, y, yn_ready)

            def stats_1(b):
                dve.wait_ge(res1_ready, b + 1)
                statistics(b, 2, 1, x1)

            def norm_1(b):
                apply_norm(b, 1, x1, x1_ready)

            def messages(b, bank, t, lo, hi, hi_ready, base, base_ready, total):
                dve.wait_ge(hi_ready, b * T + t + 1)
                dve.wait_ge(base_ready, b + 1)
                nc.vector.tensor_tensor(lo[:, t], bank.ap(f"m{t}")[:, D:], hi[:, t].bitcast(F32), ALU.subtract)
                nc.vector.scalar_tensor_tensor(out=total[:, t], in0=bank.ap(f"m{t}")[:, 0:D], scalar=deg[:, t:t + 1],
                                               in1=base[:, t], op0=ALU.mult, op1=ALU.add)\
                    .then_inc(bank.was_read(f"m{t}", b)[0], 1)

            def aggregate(b, stage, bank, i, total):
                wait(dve, bank.filled("a", b))
                wait(dve, bank.was_read("m1", b))
                wait(dve, bank.was_read("m0", b))
                nc.vector.tensor_tensor(total[:], bank.half("a"), total[:], ALU.add).then_inc(bank.was_read("a", b)[0], 1)
                wait(dve, bank.was_read("a", b))
                statistics(b, stage, i, total)

            def norm_2(b):
                apply_norm(b, 2, x2, x2_ready)

            def messages_1(b, t):
                wait(dve, (x2b_ready, b))
                messages(b, bank3, t, mj1_l, mj1_h, mj1_hi, x1, x1b_ready, x2)

            def messages_3(b, t):
                messages(b, bank4, t, mj3_l, mj3_h, mj3_hi, x3, x3b_ready, x4)

            def values(b):
                wait(dve, bank3.filled("v", b))
                wait(dve, bank4.filled("o1", b - 1))
                nc.vector.tensor_tensor(v_s[:], bank3.half("v"), rows[:, BV, :].unsqueeze(1).broadcast_to([P, T, D]),
                                        ALU.add).then_inc(bank3.was_read("v", b)[0], 1)

            def attention_sum(b):
                wait(dve, bank4.filled("o", b))
                dve.wait_ge(x2b_ready, b + 1)
                wait(dve, (stored, 16 * b))
                nc.vector.tensor_tensor(x3[:], bank4.half("o"), x2b[:], ALU.add).then_inc(bank4.was_read("o", b)[0], 1)
                wait(dve, bank4.was_read("o", b))
                statistics(b, 4, 3, x3)

            def norm_3(b):
                apply_norm(b, 3, x3, x3_ready)

            def norm_4(b):
                apply_norm(b, 4, x4, x4_ready)

            def coefficients_1(b):
                coefficients(b, 1, bank1, P, f_hi, f_sel, g_query, g_key, "e3", g_ready)

            def coefficients_2(b):
                coefficients(b, 2, bank2, 4, f2_hi, f2_sel, g2_query, g2_key, "e", g2_ready)

            def x1t_lower(b):
                turned_lower(b, bank3, "xt", xrt_l[:], xrt_h[:], x1t_hi)

            def x2t_lower(b):
                turned_lower(b, bank3, "x2t", xrt_l[:], xrt_h[:], x2t_hi)

            def x3t_lower(b):
                turned_lower(b, bank4, "x3t", x3t_l[:], x3t_h[:], x3t_hi)

            def aggregate_1(b):
                aggregate(b, 3, bank3, 2, x2)

            def aggregate_3(b):
                aggregate(b, 4, bank4, 4, x4)

            def iteration(b1, b2, b3, b4):
                steps[:] = [0] * len(steps)
                on(b1, xt_lower)
                on(b4, logits_3, 0)
                on(b4, logits_3, 1)
                on(b1, feats_lower, 0, 0)
                on(b4, inverse_3, 0)
                on(b4, logits_3, 2)
                on(b1, feats_lower, 0, 1)
                on(b4, inverse_3, 1)
                on(b2, feats2_lower, 0)
                on(b1, feats_lower, 1, 0)
                on(b1, feats_lower, 1, 1)
                on(b1, coefficients_1)
                on(b4, logits_3, 3)
                on(b1, logits_1, 0)
                on(b4, inverse_3, 2)
                on(b4, logits_3, 4)
                on(b1, inverse_1, 0)
                on(b4, inverse_3, 3)
                on(b3, x1t_lower)
                on(b2, feats2_lower, 1)
                on(b4, logits_3, 5)
                on(b4, inverse_3, 4)
                on(b1, probs_t_lower_1, 0)
                on(b1, logits_1, 1)
                on(b4, logits_3, 6)
                on(b4, inverse_3, 5)
                on(b2, coefficients_2)
                on(b1, elu_1, 0)
                on(b4, inverse_3, 6)
                on(b3, messages_1, 0)
                on(b1, inverse_1, 1)
                on(b4, logits_3, 7)
                on(b2, logits_2)
                on(b4, inverse_3, 7)
                on(b3, messages_1, 1)
                on(b2, inverse_2)
                on(b1, probs_t_lower_1, 1)
                on(b1, logits_1, 2)
                on(b2, probs_t_lower_2)
                on(b3, aggregate_1)
                on(b1, elu_1, 1)
                on(b3, norm_2)
                on(b2, elu_2)
                on(b1, inverse_1, 2)
                on(b4, attention_sum)
                on(b3, x2t_lower)
                on(b4, norm_3)
                on(b1, probs_t_lower_1, 2)
                on(b1, logits_1, 3)
                on(b4, x3t_lower)
                on(b1, elu_1, 2)
                on(b1, inverse_1, 3)
                on(b2, feed_forward_sum)
                on(b4, messages_3, 0)
                on(b4, messages_3, 1)
                on(b2, norm_0)
                on(b1, probs_t_lower_1, 3)
                on(b4, aggregate_3)
                on(b1, elu_1, 3)
                on(b4, norm_4)
                on(b2, stats_1)
                on(b3, values)
                on(b2, norm_1)
                for stage, b in enumerate((b1, b2, b3, b4)):
                    assert b is None or steps[stage] == DVE_STEPS[stage], steps

            pipeline(dve, iteration)

        @block.tensor
        def _(pe):
            pe.wait_ge(loaded_rest, 16 * N_REST)
            pe.wait_ge(setup_act, 1)
            pe.wait_ge(setup_dve, 3)

            def product3(out_ap, stat, mov, tiles=K):
                n = 0
                for k in range(tiles):
                    for a, c in ((stat[0], mov[0]), (stat[0], mov[1]), (stat[1], mov[0])):
                        ins = nc.tensor.matmul(out_ap, a(k), c(k), start=(n == 0), stop=(n == 3 * tiles - 1))
                        n += 1
                return ins

            def parts(hi, lo, cut=slice(None)):
                return (lambda k: hi[:, k, cut]), (lambda k: lo[:, k, cut])

            def rows_cut(t):
                return slice(t * P, (t + 1) * P)

            def transposes(b, bank, tile, src):
                for t in range(2):
                    for k in range(2):
                        ins = nc.tensor.transpose(bank.half(tile)[:, k, rows_cut(t)], src[:, t, rows_cut(k)], ident[:])
                ins.then_inc(bank.filled(tile, b)[0], 1)

            def project_1(b, t, half):
                tile = f"wh{t}{half}"
                pe.wait_ge(xt_lo_ready, b + 1)
                wait(pe, bank1.vacant(tile, b))
                product3(bank1.ap(tile)[:], parts(xt_h, xt_l, rows_cut(t)),
                         parts(wh_h, wh_l, slice(half * 512, (half + 1) * 512))).then_inc(bank1.filled(tile, b)[0], 1)

            def coeff_rows_1(b):
                wait(pe, bank1.vacant("f", b))
                product3(bank1.ap("f")[:, 0:N], parts(wa_h, wa_l), parts(xt_h, xt_l)).then_inc(bank1.filled("f", b)[0], 1)

            def pair_sums(b, bank, tile, gq, gk, at, ready):
                pe.wait_ge(ready, b + 1)
                wait(pe, bank.vacant(tile, b))
                for t in range(T):
                    ins = nc.tensor.matmul(bank.half(tile)[:, t], gq[at:at + 4, rows_cut(t)], gk[at:at + 4, :],
                                           start=True, stop=True, tile_position=(at, 0))
                ins.then_inc(bank.filled(tile, b)[0], 1)

            def pairs_1(b, h):
                pair_sums(b, bank1, f"e{h}", g_query, g_key, 32 * h, g_ready)

            def pairs_2(b):
                pair_sums(b, bank2, "e", g2_query, g2_key, 0, g2_ready)

            def turn_probs(b, bank, tile, probs, ready):
                wait(pe, ready)
                wait(pe, bank.vacant(tile, b))
                transposes(b, bank, tile, probs)

            def turn_1(b, h):
                turn_probs(b, bank1, f"t{h}", p1[:, h % 2], (probs1_ready, b * H + h + 1))

            def turn_2(b):
                turn_probs(b, bank2, "t", p2, (probs2_ready, b + 1))

            def turn_3(b, h):
                turn_probs(b, bank4, f"t{h}", p3[:, h % R3], (probs3_ready, b * HM + h + 1))

            def attend_t(b, bank, tile, turned, feats_of, probs_of):
                bank.wait_read(pe, b, turned, into=tile)
                for m in range(K):
                    ins = product3(bank.half(tile)[:, m], feats_of(m), probs_of)
                ins.then_inc(bank.filled(tile, b)[0], 1)

            def attend_1(b, h):
                attend_t(b, bank1, f"av{h}", f"t{h}",
                         lambda m: parts(feats_h, feats_l, slice(h * D + m * P, h * D + (m + 1) * P)),
                         parts(pt1_h[:, h % 2], pt1_l[:, h % 2]))

            def attend_2(b):
                attend_t(b, bank2, "av", "t", lambda m: parts(feats2_h, feats2_l, rows_cut(m)), parts(pt2_h, pt2_l))

            def project_2(b, t):
                pe.wait_ge(heads_lo, (b + 1) * H)
                wait(pe, bank2.vacant(f"wh{t}", b))
                product3(bank2.ap(f"wh{t}")[:, 0:D + 4], parts(heads_h, heads_l, rows_cut(t)), parts(wout_h, wout_l),
                         tiles=KH).then_inc(bank2.filled(f"wh{t}", b)[0], 1)

            def coeff_rows_2(b):
                wait(pe, bank2.was_read("wh0", b))
                wait(pe, bank2.was_read("wh1", b))
                for t in range(T):
                    ins = nc.tensor.transpose(bank2.ap("f")[0:4, rows_cut(t)], coeff2[:, t], ident[:])
                ins.then_inc(bank2.filled("f", b)[0], 1)

            def feed_forward_1(b):
                bank2.wait_read(pe, b, "av", into="hid")
                for m in range(K):
                    for k in range(K):
                        ins = nc.tensor.matmul(bank2.half("hid")[:, m], w1_s[:, k, rows_cut(m)], out2_t[:, k],
                                               start=(k == 0), stop=(k == K - 1))
                ins.then_inc(bank2.filled("hid", b)[0], 1)

            def feed_forward_2(b):
                bank2.wait_read(pe, b, "hid", into="y")
                for t in range(T):
                    for c in range(K):
                        part = bank2.half("y")[:, t, rows_cut(c)]
                        for k in range(K):
                            nc.tensor.matmul(part, hid[:, k, rows_cut(t)], w2_s[:, k, rows_cut(c)],
                                             start=(k == 0), stop=False)
                        ins = nc.tensor.matmul(part, out2_t[:, c, rows_cut(t)], ident[:], start=False, stop=True)
                ins.then_inc(bank2.filled("y", b)[0], 1)

            def turn_rows(b, bank, tile, src, ready):
                wait(pe, ready)
                wait(pe, bank.vacant(tile, b))
                transposes(b, bank, tile, src)

            def own_and_messages(b, bank, t, rows_h, rows_l, turned, w_h, w_l):
                bank.wait_read(pe, b, turned, into=f"m{t}")
                product3(bank.ap(f"m{t}")[:], parts(rows_h, rows_l, rows_cut(t)), parts(w_h, w_l))\
                    .then_inc(bank.filled(f"m{t}", b)[0], 1)

            def aggregate(b, bank, mj_h, mj_l):
                bank.wait_read(pe, b, "m0", "m1", into="a")
                for t in range(T):
                    n = 0
                    for k in range(T):
                        for part in (mj_h, mj_l):
                            ins = nc.tensor.matmul(bank.half("a")[:, t], adjt_r[:, k, rows_cut(t)], part[:, k],
                                                   start=(n == 0), stop=(n == 2 * T - 1))
                            n += 1
                ins.then_inc(bank.filled("a", b)[0], 1)

            def project_qk(b, tile, which):
                bank3.wait_read(pe, b, "x2t", into=tile)
                for m in range(K):
                    ins = product3(bank3.half(tile)[:, m],
                                   parts(qkv_h[:, which], qkv_l[:, which], rows_cut(m)), parts(xrt_h, xrt_l))
                ins.then_inc(bank3.filled(tile, b)[0], 1)

            def project_v(b):
                wait(pe, bank3.vacant("v", b))
                for t in range(T):
                    ins = product3(bank3.half("v")[:, t], parts(xrt_h, xrt_l, rows_cut(t)),
                                   parts(qkv_h[:, 2], qkv_l[:, 2]))
                ins.then_inc(bank3.filled("v", b)[0], 1)

            def scores(b, h):
                if h == 0:
                    wait(pe, bank3.was_read("q", b))
                    wait(pe, bank3.was_read("k", b))
                wait(pe, bank4.vacant(f"s{h}", b))
                j, at = h // (P // DH), DH * (h % (P // DH))
                for t in range(T):
                    ins = nc.tensor.matmul(bank4.half(f"s{h}")[:, t], q_s[at:at + DH, j, rows_cut(t)],
                                           k_s[at:at + DH, j], start=True, stop=True, tile_position=(at, 0))
                ins.then_inc(bank4.filled(f"s{h}", b)[0], 1)

            def attend_3(b, g):
                if g == 0:
                    wait(pe, bank3.was_read("v", b))
                bank4.wait_read(pe, b, *(f"t{h}" for h in range(4 * g, 4 * g + 4)), into=f"o{g}")
                for k in range(T):
                    for j in range(4):
                        h = 4 * g + j
                        ins = nc.tensor.matmul(bank4.ap(f"o{g}")[32 * j:32 * j + 32, 0:N],
                                               v_s[:, k, h * DH:(h + 1) * DH], pt3[:, h % PT3, k],
                                               start=(k == 0), stop=(k == T - 1), tile_position=(0, 32 * j))
                ins.then_inc(bank4.filled(f"o{g}", b)[0], 1)

            def project_o(b):
                bank4.wait_read(pe, b, "o0", "o1", into="o")
                for t in range(T):
                    for k in range(K):
                        ins = nc.tensor.matmul(bank4.half("o")[:, t], att_t[:, k, rows_cut(t)], wo_s[:, k],
                                               start=(k == 0), stop=(k == K - 1))
                ins.then_inc(bank4.filled("o", b)[0], 1)

            def turn_x1(b):
                turn_rows(b, bank3, "xt", x1, (x1_ready, b + 1))

            def turn_x2(b):
                turn_rows(b, bank3, "x2t", x2, (x2_ready, b + 1))

            def turn_x3(b):
                turn_rows(b, bank4, "x3t", x3, (x3_ready, b + 1))

            def own_and_messages_1(b, t):
                own_and_messages(b, bank3, t, xrt_h, xrt_l, "xt", l1_h, l1_l)

            def own_and_messages_3(b, t):
                own_and_messages(b, bank4, t, x3t_h, x3t_l, "x3t", l3_h, l3_l)

            def aggregate_1(b):
                aggregate(b, bank3, mj1_h, mj1_l)

            def aggregate_3(b):
                aggregate(b, bank4, mj3_h, mj3_l)

            def iteration(b1, b2, b3, b4):
                on(b4, scores, 0)
                on(b4, scores, 1)
                on(b4, scores, 2)
                on(b2, project_2, 0)
                on(b1, project_1, 0, 0)
                on(b1, project_1, 0, 1)
                on(b1, project_1, 1, 0)
                on(b1, project_1, 1, 1)
                on(b1, coeff_rows_1)
                on(b4, turn_3, 0)
                on(b4, scores, 3)
                on(b4, scores, 4)
                on(b4, turn_3, 1)
                on(b1, pairs_1, 0)
                on(b3, turn_x1)
                on(b2, project_2, 1)
                on(b4, scores, 5)
                on(b4, turn_3, 2)
                on(b1, turn_1, 0)
                on(b1, pairs_1, 1)
                on(b4, scores, 6)
                on(b4, turn_3, 3)
                on(b2, coeff_rows_2)
                on(b4, turn_3, 4)
                on(b1, attend_1, 0)
                on(b3, own_and_messages_1, 0)
                on(b4, scores, 7)
                on(b2, pairs_2)
                on(b4, turn_3, 5)
                on(b4, attend_3, 0)
                on(b3, own_and_messages_1, 1)
                on(b1, turn_1, 1)
                on(b4, turn_3, 6)
                on(b1, pairs_1, 2)
                on(b4, turn_3, 7)
                on(b3, aggregate_1)
                on(b2, turn_2)
                on(b1, attend_1, 1)
                on(b4, attend_3, 1)
                on(b2, attend_2)
                on(b4, project_o)
                on(b3, turn_x2)
                on(b2, feed_forward_1)
                on(b1, turn_1, 2)
                on(b1, pairs_1, 3)
                on(b3, project_qk, "q", 0)
                on(b4, turn_x3)
                on(b1, attend_1, 2)
                on(b2, feed_forward_2)
                on(b4, own_and_messages_3, 0)
                on(b4, own_and_messages_3, 1)
                on(b3, project_qk, "k", 1)
                on(b1, turn_1, 3)
                on(b4, aggregate_3)
                on(b1, attend_1, 3)
                on(b3, project_v)

            pipeline(pe, iteration)


def kernel(**inputs):
    import numpy as _np
    import concourse.bacc as _bacc
    from concourse import mybir as _mybir
    from concourse.bass_utils import run_bass_kernel_spmd as _run

    x = _np.asarray(inputs["x"])
    adj = _np.asarray(inputs["adj"])
    row = _np.arange(P) % 32
    select = _np.stack([(row == 1) | (row == 3), _np.select([(row == 0) | (row == 2), (row == 1) | (row == 3)], [1, -1], 0),
                        (row == 0) | (row == 1), (row == 2) | (row == 3)], axis=1).astype(_np.float32)
    def columns(bias):
        return _np.asarray(bias).reshape(-1, P).T

    given = [
        ("x", x), ("xt", x.transpose(0, 2, 1)), ("adj", adj), ("adjt", adj.T),
        ("w_heads", inputs["L0_gnn_W_heads"]), ("a_heads", inputs["L0_gnn_a_heads"]),
        ("w_out", inputs["L0_gnn_W_out"]), ("a_out", inputs["L0_gnn_a_out"]),
        ("w1", inputs["L0_gnn_w1"]), ("b1", columns(inputs["L0_gnn_b1"])), ("w2", inputs["L0_gnn_w2"]), ("b2", inputs["L0_gnn_b2"]),
        ("gamma", inputs["L0_gnn_ln_gamma"]), ("beta", inputs["L0_gnn_ln_beta"]),
        ("l1_wt", _np.asarray(inputs["L1_gnn_W"]).T), ("l1_b", inputs["L1_gnn_b"]),
        ("wq_t", _np.asarray(inputs["L2_gnn_Wq"]).T), ("bq", columns(inputs["L2_gnn_bq"])),
        ("wk_t", _np.asarray(inputs["L2_gnn_Wk"]).T), ("bk", columns(inputs["L2_gnn_bk"])),
        ("wv_t", _np.asarray(inputs["L2_gnn_Wv"]).T), ("bv", inputs["L2_gnn_bv"]),
        ("wo_t", _np.asarray(inputs["L2_gnn_Wo"]).T), ("bo", inputs["L2_gnn_bo"]),
        ("l3_wt", _np.asarray(inputs["L3_gnn_W"]).T), ("l3_b", inputs["L3_gnn_b"]),
        ("ident", _np.eye(P, dtype=_np.float32)), ("select", select),
    ]
    nc = _bacc.Bacc("TRN2", target_bir_lowering=False, num_devices=1)
    arrays, args = {}, []
    for name, a in given:
        a = _np.ascontiguousarray(a)
        arrays[f"in_{name}_dram"] = a
        args.append(nc.dram_tensor(f"in_{name}_dram", a.shape, _mybir.dt.from_np(a.dtype), kind="ExternalInput").ap())
    args.append(nc.dram_tensor("out_dram", x.shape, _mybir.dt.from_np(x.dtype), kind="ExternalOutput").ap())
    build(nc, *args)
    r = _run(nc, [arrays], core_ids=[0])
    return r.results[0]["out_dram"]
```

```python
from contextlib import ExitStack

import numpy as np

import concourse.bass as bass
from concourse import mybir

P = 128
F32 = mybir.dt.float32
F32R = mybir.dt.float32r
I32 = mybir.dt.int32
ALU = mybir.AluOpType
ACT = mybir.ActivationFunctionType
AX = mybir.AxisListType

GAT_MASK = -1e11
ATT_MASK = -1e30
SLOPE = 0.01
EPS = 1e-5

TILES_1 = ["wh00", "wh01", "wh10", "wh11", "f",
           "e0", "e1", "t0", "e2", "av0", "t1", "e3", "av1", "t2", "av2", "t3", "av3"]
TILES_2 = ["wh0", "wh1", "f", "e", "t", "av", "hid", "y"]
TILES_3 = ["xt", "m0", "m1", "a", "x2t", "q", "k", "v"]
TILES_4 = ["s0", "s1", "s2", "t0", "s3", "s4", "t1", "s5", "t2", "s6", "t3", "t4",
           "s7", "t5", "o0", "t6", "t7", "o1", "o", "x3t", "m0", "m1", "a"]


class Banks:

    def __init__(self, ctx, nc, name, tiles, n):
        self.tiles, self.n = tiles, n
        self.bank = [ctx.enter_context(nc.psum_tensor(f"{name}_bank{r}", [P, 512], F32)) for r in range(n)]
        self.full = [ctx.enter_context(nc.semaphore(f"{name}_full{r}")) for r in range(n)]
        self.read = [ctx.enter_context(nc.semaphore(f"{name}_read{r}")) for r in range(n)]

    def ring(self, tile):
        i = self.tiles.index(tile)
        r = i % self.n
        return r, len(range(r, i, self.n)), len(range(r, len(self.tiles), self.n))

    def ap(self, tile):
        return self.bank[self.ring(tile)[0]]

    def half(self, tile):
        return self.ap(tile)[:].rearrange("p (t n) -> p t n", t=2)

    def filled(self, tile, b):
        r, use, per = self.ring(tile)
        return self.full[r], b * per + (use + 1)

    def was_read(self, tile, b):
        r, use, per = self.ring(tile)
        return self.read[r], b * per + (use + 1)

    def vacant(self, tile, b):
        r, use, per = self.ring(tile)
        return self.read[r], b * per + use

    def wait_read(self, eng, b, *tiles, into):
        r, use, _ = self.ring(into)
        counts = {r: use}
        for tile in tiles:
            r, use, _ = self.ring(tile)
            counts[r] = max(counts.get(r, 0), use + 1)
        for r, count in counts.items():
            wait(eng, (self.read[r], b * len(range(r, len(self.tiles), self.n)) + count))


def wait(eng, sem_value):
    sem, value = sem_value
    if not isinstance(value, int) or value > 0:
        eng.wait_ge(sem, value)


def build(nc, x, xt, adj, adjt, w_heads, a_heads, w_out, a_out, w1, w2, l1_wt, wq_t, wk_t, wv_t, wo_t,
          l3_wt, row_vectors, l1_b, l3_b, column_vectors, ident_d, select_d, out):
    B, N, D = x.shape
    H = w_heads.shape[0]
    HM, DH = 8, 32
    PT3 = 6
    R3 = 3
    T = N // P
    K = D // P
    KH = H * D // P
    assert T == 2 and K == 2 and D == HM * DH and B >= 5
    SCALE = float(np.float32(1.0) / np.sqrt(np.float32(DH)))

    with ExitStack() as ctx:
        def sb(name, shape, dt=F32):
            return ctx.enter_context(nc.sbuf_tensor(name, shape, dt))

        def sem(name):
            return ctx.enter_context(nc.semaphore(name))

        wh_h, wh_l = sb("wh_h", [P, K, H * D], F32R), sb("wh_l", [P, K, H * D], F32R)
        wa_h, wa_l = sb("wa_h", [P, K, P], F32R), sb("wa_l", [P, K, P], F32R)
        l1_h, l1_l = sb("l1_h", [P, K, 2 * D], F32R), sb("l1_l", [P, K, 2 * D], F32R)
        l3_h, l3_l = sb("l3_h", [P, K, 2 * D], F32R), sb("l3_l", [P, K, 2 * D], F32R)
        qkv_h, qkv_l = sb("qkv_h", [P, 3, K, D], F32R), sb("qkv_l", [P, 3, K, D], F32R)
        wout_h, wout_l = sb("wout_h", [P, KH, D + 4], F32R), sb("wout_l", [P, KH, D + 4], F32R)
        w1_s, w2_s, wo_s = sb("w1_s", [P, K, D]), sb("w2_s", [P, K, D]), sb("wo_s", [P, K, D])
        ident = sb("ident_s", [P, P])
        select = sb("select_s", [P, 4])
        adjt_r = sb("adjt_r", [P, T, N], F32R)
        gat_mask, att_mask = sb("gat_mask", [P, T, N]), sb("att_mask", [P, T, N])
        deg = sb("deg", [P, T])
        rows = sb("rows", [P, 5, D])
        GAMMA, BETA, B2, BO, BV = range(5)
        l1_db, l3_db = sb("l1_db", [P, T, D]), sb("l3_db", [P, T, D])
        columns = sb("columns", [P, 3, K])
        b1_c, bq_c, bk_c = [columns[:, i] for i in range(3)]
        minus_half = sb("minus_half", [P, T])

        xt_s = sb("xt_s", [P, K, N])
        xt_h, xt_l = sb("xt_h", [P, K, N], F32R), sb("xt_l", [P, K, N], F32R)
        feats_h, feats_l = sb("feats_h", [P, T, H * D], F32R), sb("feats_l", [P, T, H * D], F32R)
        f_hi, f_sel = sb("f_hi", [P, N], F32R), sb("f_sel", [P, N])
        g_query, g_key = sb("g_query", [P, N], F32R), sb("g_key", [P, N], F32R)
        p1 = sb("p1", [P, 2, T, N])
        pt1_h, pt1_l = sb("pt1_h", [P, 2, T, N], F32R), sb("pt1_l", [P, 2, T, N], F32R)
        max1, neg1, nmax1 = sb("max1", [P, 2, T]), sb("neg1", [P, 2, T]), sb("nmax1", [P, 2, T])
        sum1, inv1 = sb("sum1", [P, 2, T]), sb("inv1", [P, 2, T])
        elu1 = sb("elu1", [P, 2, K, N])
        heads_h, heads_l = sb("heads_h", [P, KH, N], F32R), sb("heads_l", [P, KH, N], F32R)
        x_s = sb("x_s", [P, T, D])
        f2_hi, g2_query, g2_key = [heads_h[0:4, i] for i in range(3)]
        feats2_h, feats2_l = sb("feats2_h", [P, T, D], F32R), sb("feats2_l", [P, T, D], F32R)
        coeff2 = sb("coeff2", [P, T, 4])
        p2 = sb("p2", [P, T, N])
        f2_sel, hid = p2[0:4, 0], p2
        max2, neg2, nmax2 = sb("max2", [P, T]), sb("neg2", [P, T]), sb("nmax2", [P, T])
        sum2, inv2 = sb("sum2", [P, T]), sb("inv2", [P, T])
        out2_t = sb("out2_t", [P, K, N])
        x1, x2 = sb("x1", [P, T, D]), sb("x2", [P, T, D])
        y = x1
        xrt_h, xrt_l = sb("xrt_h", [P, K, N], F32R), sb("xrt_l", [P, K, N], F32R)
        mj1_h, mj1_l = sb("mj1_h", [P, T, D], F32R), sb("mj1_l", [P, T, D], F32R)
        pt2_h, pt2_l = mj1_h, mj1_l
        q_h, q_l = sb("q_h", [P, K, N], F32R), sb("q_l", [P, K, N], F32R)
        k_h, k_l = sb("k_h", [P, K, N], F32R), sb("k_l", [P, K, N], F32R)
        v_s = sb("v_s", [P, T, D])
        x2b = sb("x2b", [P, T, D])
        p3, pt3 = sb("p3", [P, R3, T, N]), sb("pt3", [P, PT3, T, N])
        x3t_h, x3t_l = sb("x3t_h", [P, K, N], F32R), sb("x3t_l", [P, K, N], F32R)
        mj3_h, mj3_l = sb("mj3_h", [P, T, D], F32R), sb("mj3_l", [P, T, D], F32R)
        max3, nmax3 = sb("max3", [P, R3, T]), sb("nmax3", [P, R3, T])
        sum3, inv3 = sb("sum3", [P, R3, T]), sb("inv3", [P, R3, T])
        att_t, x3 = sb("att_t", [P, K, N]), sb("x3", [P, T, D])
        x4 = x3
        stats, mean_var = sb("stats", [P, 5, T, 6]), sb("mean_var", [P, 5, T, 2])
        var_eps, rstd = sb("var_eps", [P, 5, T]), sb("rstd", [P, 5, T])

        carrier = sb("carrier", [1, 1])
        wa2 = sb("wa2", [P, KH, 4])

        def wide(buf):
            return buf.rearrange("p a t n -> p (a t n)").rearrange("p (k n) -> p k n", k=K)

        stage_wh, stage_l1, stage_l3 = wide(pt3[:, 0:4]), wide(pt3[:, 4:6]), wide(p3[:, 0:2])
        stage_qkv = [x2b, x3, v_s]
        stage_wout = [x1, x2, out2_t, p2]
        stage_ah = [buf[:, i] for buf in (p1, elu1) for i in range(2)]
        stage_ao = att_t[:]
        adj_i, adjt_i = att_mask[:].bitcast(I32), p3[:, 2].bitcast(I32)
        wa = f_sel[:].rearrange("p (k n) -> p k n", k=K)

        bank1 = Banks(ctx, nc, "s1", TILES_1, 3)
        bank2 = Banks(ctx, nc, "s2", TILES_2, 1)
        bank3 = Banks(ctx, nc, "s3", TILES_3, 1)
        bank4 = Banks(ctx, nc, "s4", TILES_4, 3)

        junk = [bank4.bank[0][:, i * D:(i + 1) * D] for i in range(2)]
        adj_f = bank4.bank[1][:].rearrange("p (t n) -> p t n", t=T)

        loaded_wh, loaded_adj, loaded_small = sem("loaded_wh"), sem("loaded_adj"), sem("loaded_small")
        loaded_2, loaded_3, loaded_4 = sem("loaded_2"), sem("loaded_3"), sem("loaded_4")
        wh_hi, wh_lo, wa_ready = sem("wh_hi"), sem("wh_lo"), sem("wa_ready")
        hi_2, lo_2, wa2_ready, hi_3, lo_3, hi_4, lo_4 = (sem(n) for n in ("hi_2", "lo_2", "wa2_ready", "hi_3", "lo_3",
                                                                         "hi_4", "lo_4"))
        deg_ready, l1_lo, setup_step = sem("deg_ready"), sem("l1_lo"), sem("setup_step")
        xt_loaded, xt_hi, xt_lo = sem("xt_loaded"), sem("xt_hi"), sem("xt_lo")
        g_ready, logits1_ready, exp1_done = sem("g_ready"), sem("logits1_ready"), sem("exp1_done")
        inv1_ready, probs1_ready, elu1_exp = sem("inv1_ready"), sem("probs1_ready"), sem("elu1_exp")
        x_loaded, x_beta_ready = sem("x_loaded"), sem("x_beta_ready")
        g2_ready, logits2_ready, exp2_done = sem("g2_ready"), sem("logits2_ready"), sem("exp2_done")
        inv2_ready, probs2_ready, elu2_exp = sem("inv2_ready"), sem("probs2_ready"), sem("elu2_exp")
        yn_ready, res1_ready = sem("yn_ready"), sem("res1_ready")
        feats_hi, pt1_hi, heads_hi, heads_lo = sem("feats_hi"), sem("pt1_hi"), sem("heads_hi"), sem("heads_lo")
        feats2_hi, pt2_hi = sem("feats2_hi"), sem("pt2_hi")
        x1_ready, x1b_ready, x1t_hi, mj1_hi, x2_ready = (sem("x1_ready"), sem("x1b_ready"), sem("x1t_hi"),
                                                          sem("mj1_hi"), sem("x2_ready"))
        x2b_ready, x2t_hi, logits3_ready = sem("x2b_ready"), sem("x2t_hi"), sem("logits3_ready")
        exp3_done, inv3_ready, probs3_ready = sem("exp3_done"), sem("inv3_ready"), sem("probs3_ready")
        x3_ready, x3b_ready, x3t_hi, mj3_hi, x4_ready = (sem("x3_ready"), sem("x3b_ready"), sem("x3t_hi"),
                                                          sem("mj3_hi"), sem("x4_ready"))
        q_hi, k_hi = sem("q_hi"), sem("k_hi")
        stored = sem("stored")
        var_ready = [sem(f"var_ready{i}") for i in range(5)]
        rstd_ready = [sem(f"rstd_ready{i}") for i in range(5)]
        dve_step = [sem(f"dve_step{i}") for i in (1, 2, 3, 4)]
        pool_step = sem("pool_step")
        DVE_STEPS = (9, 7, 2, 4)

        block = ctx.enter_context(nc.Block())

        def pipeline(eng, iteration, before=lambda stage: None):
            before(1)
            iteration(0, None, None, None)
            before(2)
            iteration(1, 0, None, None)
            before(3)
            iteration(2, 1, 0, None)
            before(4)
            iteration(3, 2, 1, 0)
            with eng.Fori(4, B) as i:
                iteration(i, i - 1, i - 2, i - 3)
            iteration(None, B - 1, B - 2, B - 3)
            iteration(None, None, B - 1, B - 2)
            iteration(None, None, None, B - 1)

        def on(b, step, *args):
            if b is not None:
                step(b, *args)

        def rows_of(dram, b):
            return dram[bass.ds(b, 1)].rearrange("b (t p) n -> p (b t) n", p=P)

        @block.sync
        def _(sp):
            tiled = "(k p) n -> p k n"

            def before(stage):
                if stage == 1:
                    for part in range(2):
                        heads = slice(part * H // 2, (part + 1) * H // 2)
                        for k in range(K):
                            sp.dma_start(stage_wh[:, k, part * KH * P // 2:(part + 1) * KH * P // 2].rearrange("p (h n) -> p h n", n=D),
                                         w_heads[heads, k * P:(k + 1) * P].rearrange("h p n -> p h n")).then_inc(loaded_wh, 16)
                if stage == 2:
                    for i in range(KH // K):
                        sp.dma_start(stage_wout[i][:], w_out[i * K * P:(i + 1) * K * P].rearrange(tiled, p=P))\
                            .then_inc(loaded_2, 16)
                    for i in range(2):
                        sp.dma_start(stage_l1[:, :, i * D:(i + 1) * D], l1_wt[i * D:(i + 1) * D].rearrange(tiled, p=P))\
                            .then_inc(loaded_3, 16)
                    for i, src in enumerate((wq_t, wk_t, wv_t)):
                        sp.dma_start(stage_qkv[i][:], src.rearrange(tiled, p=P)).then_inc(loaded_3, 16)
                    for i in range(2):
                        sp.dma_start(stage_l3[:, :, i * D:(i + 1) * D], l3_wt[i * D:(i + 1) * D].rearrange(tiled, p=P))\
                            .then_inc(loaded_4, 16)

            def load_xt(b):
                wait(sp, (xt_lo, b))
                sp.dma_start(xt_s[:], rows_of(xt, b)).then_inc(xt_loaded, 16)

            def load_x(b):
                wait(sp, (res1_ready, b))
                sp.dma_start(x_s[:], rows_of(x, b)).then_inc(x_loaded, 16)

            def store(b):
                sp.wait_ge(x4_ready, b + 1)
                sp.dma_start(rows_of(out, b), x4[:]).then_inc(stored, 16)

            def store_previous(b):
                if not isinstance(b, int) or b > 0:
                    store(b - 1)

            def iteration(b1, b2, b3, b4):
                on(b1, load_xt)
                on(b4, store_previous)
                on(b2, load_x)

            pipeline(sp, iteration, before)
            store(B - 1)
            sp.wait_ge(stored, 16 * B)

        N_WH, N_ADJ, N_SMALL, N_2, N_3, N_4 = 2 * K, 1, 8, KH // K + 3, 6, 3

        @block.gpsimd
        def _(pool):
            def before(stage):
                if stage == 1:
                    nc.gpsimd.memset(minus_half[:], -0.5).then_inc(pool_step, 1)
                    pool.wait_ge(pool_step, 1)
                    pool.wait_ge(loaded_small, 16 * N_SMALL)
                if stage == 2:
                    for i in range(KH // K):
                        pool.wait_ge(hi_2, i + 1)
                        cut = wout_h[:, K * i:K * (i + 1), 0:D]
                        nc.gpsimd.tensor_tensor(wout_l[:, K * i:K * (i + 1), 0:D], stage_wout[i][:], cut.bitcast(F32),
                                                ALU.subtract).then_inc(lo_2, 1)
                if stage == 3:
                    for i in range(3):
                        pool.wait_ge(hi_3, i + 2)
                        nc.gpsimd.tensor_tensor(qkv_l[:, i], stage_qkv[i][:], qkv_h[:, i].bitcast(F32), ALU.subtract)\
                            .then_inc(lo_3, 1)
                    pool.wait_ge(deg_ready, 1)

            def xt_lower(b):
                pool.wait_ge(xt_hi, b + 1)
                nc.gpsimd.tensor_tensor(xt_l[:], xt_s[:], xt_h[:].bitcast(F32), ALU.subtract).then_inc(xt_lo, 1)

            def both(row):
                return rows[:, row, :].unsqueeze(1).broadcast_to([P, T, D])

            def spread(small):
                return small.unsqueeze(2).broadcast_to([P, T, N])

            def normalise(probs, inv, ready, done):
                wait(pool, ready)
                nc.gpsimd.tensor_tensor(probs, probs, spread(inv), ALU.mult).then_inc(done, 1)

            def probs_1(b, h):
                normalise(p1[:, h % 2], inv1[:, h % 2], (inv1_ready, b * H + h + 1), probs1_ready)

            def probs_2(b):
                normalise(p2[:], inv2[:], (inv2_ready, b + 1), probs2_ready)

            def probs_3(b, h):
                normalise(p3[:, h % R3], inv3[:, h % R3], (inv3_ready, b * HM + h + 1), probs3_ready)

            def inverse_root(b, i):
                pool.wait_ge(var_ready[i], b + 1)
                nc.gpsimd.tensor_tensor(rstd[:, i], var_eps[:, i], minus_half[:], ALU.pow).then_inc(rstd_ready[i], 1)

            def add_beta(b):
                pool.wait_ge(x_loaded, 16 * (b + 1))
                nc.gpsimd.tensor_tensor(x_s[:], x_s[:], both(BETA), ALU.add).then_inc(x_beta_ready, 1)

            def residual_1(b):
                pool.wait_ge(yn_ready, b + 1)
                nc.gpsimd.tensor_tensor(x1[:], y[:], both(GAMMA), ALU.mult).then_inc(pool_step, 1)
                pool.wait_ge(pool_step, b + 2)
                pool.wait_ge(x_beta_ready, b + 1)
                nc.gpsimd.tensor_tensor(x1[:], x1[:], x_s[:], ALU.add).then_inc(res1_ready, 1)

            def heads_lower(b, h):
                pool.wait_ge(heads_hi, b * H + h + 1)
                nc.gpsimd.tensor_tensor(heads_l[:, 2 * h:2 * h + 2], elu1[:, h % 2],
                                        heads_h[:, 2 * h:2 * h + 2].bitcast(F32), ALU.subtract).then_inc(heads_lo, 1)

            def add_const(b, rows_in, turned, const, done):
                wait(pool, turned)
                nc.gpsimd.tensor_tensor(rows_in[:], rows_in[:], const, ALU.add).then_inc(done, 1)

            def x1_const(b):
                add_const(b, x1, bank3.filled("xt", b), l1_db[:], x1b_ready)

            def x2_const(b):
                pool.wait_ge(x2_ready, b + 1)
                wait(pool, bank4.was_read("o", b - 1))
                nc.gpsimd.tensor_tensor(x2b[:], x2[:], both(BO), ALU.add).then_inc(x2b_ready, 1)

            def x3_const(b):
                add_const(b, x3, bank4.filled("x3t", b), l3_db[:], x3b_ready)

            def iteration(b1, b2, b3, b4):
                on(b1, xt_lower)
                on(b4, probs_3, 0)
                on(b4, probs_3, 1)
                on(b3, x1_const)
                on(b2, add_beta)
                on(b4, probs_3, 2)
                on(b4, probs_3, 3)
                on(b1, probs_1, 0)
                on(b4, probs_3, 4)
                on(b4, probs_3, 5)
                on(b4, probs_3, 6)
                on(b1, probs_1, 1)
                on(b2, probs_2)
                on(b4, probs_3, 7)
                on(b3, inverse_root, 2)
                on(b1, probs_1, 2)
                on(b1, heads_lower, 0)
                on(b4, inverse_root, 3)
                on(b1, probs_1, 3)
                on(b1, heads_lower, 1)
                on(b4, x3_const)
                on(b3, x2_const)
                on(b2, inverse_root, 0)
                on(b1, heads_lower, 2)
                on(b2, residual_1)
                on(b1, heads_lower, 3)
                on(b4, inverse_root, 4)
                on(b2, inverse_root, 1)

            pipeline(pool, iteration, before)

        @block.scalar
        def _(act):
            tiled = "(k p) n -> p k n"
            for i, buf in enumerate((p1, elu1)):
                act.dma_start(buf[:].rearrange("p a t n -> p (a t n)"), a_heads[i * H // 2:(i + 1) * H // 2]
                              .rearrange("(o h) n -> o (h n)", o=1).broadcast_to([P, H * D])).then_inc(loaded_small, 16)
            act.dma_start(select[:], select_d).then_inc(loaded_small, 16)
            act.dma_start(ident[:], ident_d).then_inc(loaded_small, 16)
            act.dma_start(adj_i, adj.rearrange("(t p) n -> p t n", p=P)).then_inc(loaded_adj, 16)
            act.dma_start(columns[:], column_vectors).then_inc(loaded_small, 16)
            act.dma_start(rows[:], row_vectors.rearrange("(o r) n -> o r n", o=1).broadcast_to([P, 5, D]))\
                .then_inc(loaded_small, 16)
            for dst, src in ((l1_db, l1_b), (l3_db, l3_b)):
                act.dma_start(dst[:, T - 1], src.rearrange("(o n) -> o n", o=1).broadcast_to([P, D])).then_inc(loaded_small, 16)
            act.dma_start(stage_ao, a_out.rearrange("(o t n) -> o t n", o=1, t=2).broadcast_to([P, 2, D])).then_inc(loaded_2, 16)
            for dst, src in ((w1_s, w1), (w2_s, w2)):
                act.dma_start(dst[:], src.rearrange(tiled, p=P)).then_inc(loaded_2, 16)
            act.dma_start(adjt_i, adjt.rearrange("(t p) n -> p t n", p=P)).then_inc(loaded_3, 16)
            act.dma_start(wo_s[:], wo_t.rearrange(tiled, p=P)).then_inc(loaded_4, 16)

            def before(stage):
                if stage == 1:
                    for part in range(2):
                        act.wait_ge(loaded_wh, 16 * N_WH)
                        cut = slice(part * H * D // 2, (part + 1) * H * D // 2)
                        nc.scalar.activation(wh_h[:, :, cut], stage_wh[:, :, cut], ACT.Copy).then_inc(wh_hi, 1)
                    act.wait_ge(loaded_small, 16 * N_SMALL)
                if stage == 2:
                    act.wait_ge(loaded_2, 16 * N_2)
                    for i in range(KH // K):
                        nc.scalar.activation(wout_h[:, K * i:K * (i + 1), 0:D], stage_wout[i][:], ACT.Copy).then_inc(hi_2, 1)
                if stage == 3:
                    act.wait_ge(loaded_3, 16 * N_3)
                    nc.scalar.activation(l1_h[:], stage_l1, ACT.Copy).then_inc(hi_3, 1)
                    for i in range(3):
                        nc.scalar.activation(qkv_h[:, i], stage_qkv[i][:], ACT.Copy).then_inc(hi_3, 1)
                    nc.scalar.activation(adjt_r[:], adjt_i, ACT.Copy).then_inc(hi_3, 1)
                if stage == 4:
                    act.wait_ge(loaded_4, 16 * N_4)
                    nc.scalar.activation(l3_h[:], stage_l3, ACT.Copy).then_inc(hi_4, 1)

            def xt_upper(b):
                act.wait_ge(xt_loaded, 16 * (b + 1))
                wait(act, bank1.filled("f", b - 1))
                nc.scalar.activation(xt_h[:], xt_s[:], ACT.Copy).then_inc(xt_hi, 1)

            def feats_copy(b, t, half):
                tile = f"wh{t}{half}"
                wait(act, bank1.filled(tile, b))
                if (t, half) == (0, 0):
                    wait(act, bank1.filled("av3", b - 1))
                nc.scalar.activation(feats_h[:, t, half * 512:(half + 1) * 512], bank1.ap(tile)[:], ACT.Copy)\
                    .then_inc(feats_hi, 1)

            def coeff_parts(b, bank, tile, n, hi, sel, used):
                wait(act, bank.filled(tile, b))
                wait(act, (used, b))
                nc.scalar.activation(hi[:], bank.ap(tile)[0:n, 0:N], ACT.Copy)
                nc.scalar.activation(sel[:], bank.ap(tile)[0:n, 0:N], ACT.Copy, scale=select[0:n, 0:1])\
                    .then_inc(bank.was_read(tile, b)[0], 1)

            def softmax_exp(probs, nmax, sums, scale, ready, done):
                wait(act, ready)
                for t in range(T):
                    last = nc.scalar.activation(probs[:, t], probs[:, t], ACT.Exp, bias=nmax[:, t:t + 1], scale=scale,
                                                accum_out=sums[:, t:t + 1])
                last.then_inc(done, 1)

            def exp_1(b, h):
                softmax_exp(p1[:, h % 2], nmax1[:, h % 2], sum1[:, h % 2], 1.0, (logits1_ready, b * H + h + 1), exp1_done)

            def exp_2(b):
                softmax_exp(p2[:], nmax2[:], sum2[:], 1.0, (logits2_ready, b + 1), exp2_done)

            def exp_3(b, h):
                softmax_exp(p3[:, h % R3], nmax3[:, h % R3], sum3[:, h % R3], SCALE, (logits3_ready, b * HM + h + 1),
                            exp3_done)

            def probs_t_1(b, h):
                wait(act, bank1.filled(f"t{h}", b))
                wait(act, bank1.filled(f"av{h - 2}", b) if h >= 2 else bank1.filled(f"av{h + 2}", b - 1))
                nc.scalar.activation(pt1_h[:, h % 2], bank1.half(f"t{h}"), ACT.Copy).then_inc(pt1_hi, 1)

            def probs_t_2(b):
                wait(act, bank2.filled("t", b))
                wait(act, bank3.filled("a", b - 1))
                nc.scalar.activation(pt2_h[:], bank2.half("t"), ACT.Copy).then_inc(pt2_hi, 1)

            def probs_t_3(b, h):
                wait(act, bank4.filled(f"t{h}", b))
                wait(act, bank4.filled("o0", b) if h >= PT3 else bank4.filled("o1", b - 1))
                nc.scalar.activation(pt3[:, h % PT3], bank4.half(f"t{h}"), ACT.Copy)\
                    .then_inc(bank4.was_read(f"t{h}", b)[0], 1)

            def elu_exp_1(b, h):
                wait(act, bank1.filled(f"av{h}", b))
                wait(act, (heads_lo, b * H + h - 1))
                nc.scalar.activation(elu1[:, h % 2], bank1.half(f"av{h}"), ACT.Exp).then_inc(elu1_exp, 1)

            def heads_upper(b, h):
                wait(act, bank1.was_read(f"av{h}", b))
                wait(act, bank2.filled("e", b - 1))
                nc.scalar.activation(heads_h[:, 2 * h:2 * h + 2], elu1[:, h % 2], ACT.Copy).then_inc(heads_hi, 1)

            def elu_exp_2(b):
                wait(act, bank2.filled("av", b))
                wait(act, bank2.filled("y", b - 1))
                nc.scalar.activation(out2_t[:], bank2.half("av"), ACT.Exp).then_inc(elu2_exp, 1)

            def feats2_upper(b, t):
                wait(act, bank2.filled(f"wh{t}", b))
                if t == 0:
                    wait(act, bank2.filled("av", b - 1))
                nc.scalar.activation(feats2_h[:, t], bank2.ap(f"wh{t}")[:, 0:D], ACT.Copy).then_inc(feats2_hi, 1)

            def hidden(b):
                wait(act, bank2.filled("hid", b))
                wait(act, bank2.filled("y", b - 1))
                for m in range(K):
                    last = nc.scalar.activation(hid[:, m], bank2.half("hid")[:, m], ACT.Relu, bias=b1_c[:, m:m + 1])
                last.then_inc(bank2.was_read("hid", b)[0], 1)

            def upper(b, bank, tile, dst, used, done):
                wait(act, bank.filled(tile, b))
                wait(act, used)
                nc.scalar.activation(dst, bank.half(tile), ACT.Copy).then_inc(done, 1)

            def mj_upper(b, bank, t, dst, done):
                wait(act, bank.filled(f"m{t}", b))
                nc.scalar.activation(dst[:, t], bank.ap(f"m{t}")[:, D:], ACT.Copy).then_inc(done, 1)

            def qk_upper(b, tile, dst, bias, done):
                wait(act, bank3.filled(tile, b))
                wait(act, bank4.filled("s7", b - 1))
                for m in range(K):
                    last = nc.scalar.activation(dst[:, m], bank3.half(tile)[:, m], ACT.Identity, bias=bias[:, m:m + 1])
                last.then_inc(done, 1)

            def att_copy(b, g):
                wait(act, bank4.filled(f"o{g}", b))
                wait(act, bank4.filled("o", b - 1))
                nc.scalar.activation(att_t[:, g], bank4.ap(f"o{g}")[:, 0:N], ACT.Copy).then_inc(bank4.was_read(f"o{g}", b)[0], 1)

            def coeff_parts_1(b):
                coeff_parts(b, bank1, "f", P, f_hi, f_sel, g_ready)

            def coeff_parts_2(b):
                coeff_parts(b, bank2, "f", 4, f2_hi, f2_sel, g2_ready)

            def x1t_upper(b):
                upper(b, bank3, "xt", xrt_h[:], bank3.filled("v", b - 1), x1t_hi)

            def x2t_upper(b):
                upper(b, bank3, "x2t", xrt_h[:], bank3.filled("m1", b), x2t_hi)

            def x3t_upper(b):
                upper(b, bank4, "x3t", x3t_h[:], bank4.filled("m1", b - 1), x3t_hi)

            def mj1_upper(b, t):
                mj_upper(b, bank3, t, mj1_h, mj1_hi)

            def mj3_upper(b, t):
                mj_upper(b, bank4, t, mj3_h, mj3_hi)

            def queries(b):
                qk_upper(b, "q", q_h, bq_c, q_hi)

            def keys(b):
                qk_upper(b, "k", k_h, bk_c, k_hi)

            def iteration(b1, b2, b3, b4):
                on(b1, xt_upper)
                on(b2, feats2_upper, 0)
                on(b3, x1t_upper)
                on(b4, exp_3, 0)
                on(b1, feats_copy, 0, 0)
                on(b1, feats_copy, 0, 1)
                on(b4, exp_3, 1)
                on(b1, feats_copy, 1, 0)
                on(b1, feats_copy, 1, 1)
                on(b1, coeff_parts_1)
                on(b4, probs_t_3, 0)
                on(b4, exp_3, 2)
                on(b4, probs_t_3, 1)
                on(b4, exp_3, 3)
                on(b2, feats2_upper, 1)
                on(b1, exp_1, 0)
                on(b4, exp_3, 4)
                on(b2, coeff_parts_2)
                on(b3, mj1_upper, 0)
                on(b4, probs_t_3, 2)
                on(b4, exp_3, 5)
                on(b1, exp_1, 1)
                on(b4, probs_t_3, 3)
                on(b4, probs_t_3, 4)
                on(b4, exp_3, 6)
                on(b1, probs_t_1, 0)
                on(b3, mj1_upper, 1)
                on(b2, exp_2)
                on(b4, probs_t_3, 5)
                on(b4, att_copy, 0)
                on(b4, exp_3, 7)
                on(b2, probs_t_2)
                on(b4, probs_t_3, 6)
                on(b4, probs_t_3, 7)
                on(b1, exp_1, 2)
                on(b1, elu_exp_1, 0)
                on(b4, att_copy, 1)
                on(b2, elu_exp_2)
                on(b1, heads_upper, 0)
                on(b1, probs_t_1, 1)
                on(b2, hidden)
                on(b1, exp_1, 3)
                on(b1, elu_exp_1, 1)
                on(b3, x2t_upper)
                on(b1, heads_upper, 1)
                on(b1, probs_t_1, 2)
                on(b4, x3t_upper)
                on(b3, queries)
                on(b1, elu_exp_1, 2)
                on(b4, mj3_upper, 0)
                on(b1, heads_upper, 2)
                on(b1, probs_t_1, 3)
                on(b4, mj3_upper, 1)
                on(b3, keys)
                on(b1, elu_exp_1, 3)
                on(b1, heads_upper, 3)

            pipeline(act, iteration, before)

        @block.vector
        def _(dve):
            count = [0]

            def step(ins, back=0):
                count[0] += 1
                ins.then_inc(setup_step, 1)
                wait(dve, (setup_step, count[0] - back))

            def coefficient_weights(src, k, a, cols):
                for half in range(2):
                    step(nc.vector.tensor_tensor_reduce(junk[half], src, a[half], 1.0, 0.0, ALU.mult, ALU.add,
                                                        cols[:, k, 2 * half:2 * half + 1]), back=1)

            def before(stage):
                if stage == 1:
                    nc.vector.memset(wa, 0.0).then_inc(setup_step, 1)
                    count[0] += 1
                    for part in range(2):
                        cut = slice(part * H * D // 2, (part + 1) * H * D // 2)
                        dve.wait_ge(wh_hi, part + 1)
                        nc.vector.tensor_tensor(wh_l[:, :, cut], stage_wh[:, :, cut], wh_h[:, :, cut].bitcast(F32),
                                                ALU.subtract).then_inc(wh_lo, 1)
                    dve.wait_ge(setup_step, 1)
                    dve.wait_ge(loaded_small, 16 * N_SMALL)
                    for k in range(K):
                        for h in range(H):
                            coefficient_weights(stage_wh[:, k, h * D:(h + 1) * D], k, [stage_ah[h][:, i] for i in range(2)],
                                                wa[:, :, 32 * h:32 * h + 4])
                    wait(dve, (setup_step, count[0]))
                    pairs = wa.rearrange("p k (h c) -> p k h c", c=32)
                    step(nc.vector.tensor_copy(pairs[:, :, :, 1:4:2], pairs[:, :, :, 0:4:2]))
                    step(nc.vector.tensor_copy(wa_h[:], wa))
                    nc.vector.tensor_tensor(wa_l[:], wa, wa_h[:].bitcast(F32), ALU.subtract).then_inc(wa_ready, 1)
                    dve.wait_ge(loaded_adj, 16 * N_ADJ)
                    step(nc.vector.tensor_copy(adj_f, adj_i))
                    nc.vector.tensor_scalar(gat_mask[:], adj_f, 0.0, GAT_MASK, ALU.is_le, ALU.mult)
                    step(nc.vector.tensor_scalar(att_mask[:], adj_f, 0.0, ATT_MASK, ALU.is_equal, ALU.mult))
                if stage == 2:
                    dve.wait_ge(loaded_2, 16 * N_2)
                    for k in range(KH):
                        coefficient_weights(stage_wout[k // K][:, k % K], k, [stage_ao[:, i] for i in range(2)], wa2)
                    wait(dve, (setup_step, count[0]))
                    step(nc.vector.tensor_copy(wa2[:, :, 1:4:2], wa2[:, :, 0:4:2]))
                    step(nc.vector.tensor_copy(wout_h[:, :, D:], wa2[:]))
                    nc.vector.tensor_tensor(wout_l[:, :, D:], wa2[:], wout_h[:, :, D:].bitcast(F32), ALU.subtract)\
                        .then_inc(wa2_ready, 1)
                if stage == 3:
                    step(nc.vector.tensor_reduce(deg[:], adj_f, AX.X, ALU.add))
                    for t in range(T):
                        nc.vector.tensor_scalar(l1_db[:, t], l1_db[:, T - 1], deg[:, t:t + 1], None, ALU.mult)
                        last = nc.vector.tensor_scalar(l3_db[:, t], l3_db[:, T - 1], deg[:, t:t + 1], None, ALU.mult)
                    last.then_inc(deg_ready, 1)
                    dve.wait_ge(hi_3, 1)
                    nc.vector.tensor_tensor(l1_l[:], stage_l1, l1_h[:].bitcast(F32), ALU.subtract).then_inc(l1_lo, 1)
                if stage == 4:
                    dve.wait_ge(hi_4, 1)
                    nc.vector.tensor_tensor(l3_l[:], stage_l3, l3_h[:].bitcast(F32), ALU.subtract).then_inc(lo_4, 1)

            steps = [0] * len(DVE_STEPS)

            def link(stage, b, ins, carried=True):
                steps[stage - 1] += 1
                ins.then_inc(dve_step[stage - 1], 1)
                done = dve_step[stage - 1], b * DVE_STEPS[stage - 1] + steps[stage - 1]
                wait(dve, done) if carried else wait_apart(done)

            def wait_apart(*sem_values):
                for sem_value in sem_values:
                    wait(dve, sem_value)
                nc.vector.memset(carrier[0:1, 0:1], 0.0)

            def feats_lower(b, t, half):
                tile, cut = f"wh{t}{half}", slice(half * 512, (half + 1) * 512)
                dve.wait_ge(feats_hi, b * 2 * T + 2 * t + half + 1)
                nc.vector.tensor_tensor(feats_l[:, t, cut], bank1.ap(tile)[:], feats_h[:, t, cut].bitcast(F32),
                                        ALU.subtract).then_inc(bank1.was_read(tile, b)[0], 1)

            def feats2_lower(b, t):
                dve.wait_ge(feats2_hi, b * T + t + 1)
                nc.vector.tensor_copy(coeff2[:, t], bank2.ap(f"wh{t}")[:, D:D + 4])
                nc.vector.tensor_tensor(feats2_l[:, t], bank2.ap(f"wh{t}")[:, 0:D], feats2_h[:, t].bitcast(F32),
                                        ALU.subtract).then_inc(bank2.was_read(f"wh{t}", b)[0], 1)

            def lower(b, bank, tile, dst, hi, hi_ready):
                wait(dve, hi_ready)
                nc.vector.tensor_tensor(dst, bank.half(tile), hi.bitcast(F32), ALU.subtract)\
                    .then_inc(bank.was_read(tile, b)[0], 1)

            def turned_lower(b, bank, tile, dst, hi, hi_ready):
                lower(b, bank, tile, dst, hi, (hi_ready, b + 1))

            def probs_t_lower_1(b, h):
                lower(b, bank1, f"t{h}", pt1_l[:, h % 2], pt1_h[:, h % 2], (pt1_hi, b * H + h + 1))

            def probs_t_lower_2(b):
                lower(b, bank2, "t", pt2_l[:], pt2_h[:], (pt2_hi, b + 1))

            def coefficients(b, stage, bank, n, hi, sel, gq, gk, last_scores, ready):
                wait(dve, bank.was_read("f", b))
                wait(dve, bank.filled(last_scores, b - 1))
                link(stage, b, nc.vector.scalar_tensor_tensor(out=sel[:], in0=hi[:].bitcast(F32), scalar=select[0:n, 1:2],
                                                              in1=sel[:], op0=ALU.mult, op1=ALU.add))
                nc.vector.tensor_scalar(gq[:], sel[:], select[0:n, 2:3], select[0:n, 3:4], ALU.mult, ALU.add)
                nc.vector.tensor_scalar(gk[:], sel[:], select[0:n, 3:4], select[0:n, 2:3], ALU.mult, ALU.add)\
                    .then_inc(ready, 1)

            def gat_logits(b, stage, bank, tile, e, mx, neg, nmax, e_free, done):
                wait_apart(bank.filled(tile, b), e_free)
                for t in range(T):
                    last = nc.vector.tensor_tensor_reduce(e[:, t], bank.half(tile)[:, t], gat_mask[:, t], 1.0, -3e38,
                                                          ALU.add, ALU.max, mx[:, t:t + 1])
                last.then_inc(bank.was_read(tile, b)[0], 1)
                wait(dve, bank.was_read(tile, b))
                link(stage, b, nc.vector.tensor_scalar(neg, mx, -1.0, None, ALU.mult))
                nc.vector.scalar_tensor_tensor(out=nmax, in0=neg, scalar=SLOPE, in1=neg, op0=ALU.mult, op1=ALU.min)
                nc.vector.scalar_tensor_tensor(out=e, in0=e, scalar=SLOPE, in1=e, op0=ALU.mult, op1=ALU.max)\
                    .then_inc(done, 1)

            def logits_1(b, h):
                gat_logits(b, 1, bank1, f"e{h}", p1[:, h % 2], max1[:, h % 2], neg1[:, h % 2], nmax1[:, h % 2],
                           bank1.filled(f"t{h - 2}", b) if h >= 2 else bank1.filled(f"t{h + 2}", b - 1), logits1_ready)

            def logits_2(b):
                gat_logits(b, 2, bank2, "e", p2[:], max2[:], neg2[:], nmax2[:], bank2.filled("t", b - 1), logits2_ready)

            def logits_3(b, h):
                tile = f"s{h}"
                if h < R3:
                    wait_apart(bank4.filled(tile, b))
                else:
                    wait_apart(bank4.filled(tile, b), bank4.filled(f"t{h - R3}", b))
                for t in range(T):
                    last = nc.vector.tensor_tensor_reduce(p3[:, h % R3, t], bank4.half(tile)[:, t], att_mask[:, t],
                                                          1.0, -3e38, ALU.add, ALU.max, max3[:, h % R3, t:t + 1])
                last.then_inc(bank4.was_read(tile, b)[0], 1)
                wait(dve, bank4.was_read(tile, b))
                nc.vector.tensor_scalar(nmax3[:, h % R3], max3[:, h % R3], -SCALE, None, ALU.mult).then_inc(logits3_ready, 1)

            def inverse(exp_done, inv_free, inv, sums, ready):
                wait(dve, exp_done)
                wait(dve, inv_free)
                nc.vector.reciprocal(inv, sums).then_inc(ready, 1)

            def inverse_1(b, h):
                inverse((exp1_done, b * H + h + 1), (probs1_ready, b * H + h - 1), inv1[:, h % 2], sum1[:, h % 2], inv1_ready)

            def inverse_2(b):
                inverse((exp2_done, b + 1), (probs2_ready, b), inv2[:], sum2[:], inv2_ready)

            def inverse_3(b, h):
                inverse((exp3_done, b * HM + h + 1), (probs3_ready, b * HM + h - 2), inv3[:, h % R3], sum3[:, h % R3], inv3_ready)

            def elu(b, stage, bank, tile, expd, exp_ready, dst):
                wait(dve, exp_ready)
                link(stage, b, nc.vector.tensor_scalar(expd, expd, 1.0, -1.0, ALU.min, ALU.add))
                nc.vector.tensor_tensor(dst, bank.half(tile), expd, ALU.max).then_inc(bank.was_read(tile, b)[0], 1)

            def elu_1(b, h):
                elu(b, 1, bank1, f"av{h}", elu1[:, h % 2], (elu1_exp, b * H + h + 1), elu1[:, h % 2])

            def elu_2(b):
                elu(b, 2, bank2, "av", out2_t[:], (elu2_exp, b + 1), out2_t[:])

            def statistics(b, stage, i, src):
                for t in range(T):
                    last = nc.vector.bn_stats(stats[:, i, t], src[:, t])
                link(stage, b, last, carried=False)
                for t in range(T):
                    last = nc.vector.bn_aggr(mean_var[:, i, t], stats[:, i, t])
                link(stage, b, last)
                nc.vector.tensor_scalar(var_eps[:, i], mean_var[:, i, :, 1], EPS, None, ALU.add).then_inc(var_ready[i], 1)

            def apply_norm(b, i, buf, done):
                dve.wait_ge(rstd_ready[i], b + 1)
                for t in range(T):
                    last = nc.vector.tensor_scalar(buf[:, t], buf[:, t], mean_var[:, i, t, 0:1], rstd[:, i, t:t + 1],
                                                   ALU.subtract, ALU.mult)
                last.then_inc(done, 1)

            def feed_forward_sum(b):
                wait(dve, bank2.filled("y", b))
                wait(dve, bank3.was_read("m1", b - 1))
                nc.vector.tensor_tensor(y[:], bank2.half("y"), rows[:, B2, :].unsqueeze(1).broadcast_to([P, T, D]),
                                        ALU.add).then_inc(bank2.was_read("y", b)[0], 1)
                wait(dve, bank2.was_read("y", b))
                statistics(b, 2, 0, y)

            def norm_0(b):
                apply_norm(b, 0, y, yn_ready)

            def stats_1(b):
                dve.wait_ge(res1_ready, b + 1)
                statistics(b, 2, 1, x1)

            def norm_1(b):
                apply_norm(b, 1, x1, x1_ready)

            def messages(b, bank, t, lo, hi, hi_ready, base, base_ready, total):
                dve.wait_ge(hi_ready, b * T + t + 1)
                dve.wait_ge(base_ready, b + 1)
                nc.vector.tensor_tensor(lo[:, t], bank.ap(f"m{t}")[:, D:], hi[:, t].bitcast(F32), ALU.subtract)
                nc.vector.scalar_tensor_tensor(out=total[:, t], in0=bank.ap(f"m{t}")[:, 0:D], scalar=deg[:, t:t + 1],
                                               in1=base[:, t], op0=ALU.mult, op1=ALU.add)\
                    .then_inc(bank.was_read(f"m{t}", b)[0], 1)

            def aggregate(b, stage, bank, i, total):
                wait(dve, bank.filled("a", b))
                wait(dve, bank.was_read("m1", b))
                wait(dve, bank.was_read("m0", b))
                nc.vector.tensor_tensor(total[:], bank.half("a"), total[:], ALU.add).then_inc(bank.was_read("a", b)[0], 1)
                wait(dve, bank.was_read("a", b))
                statistics(b, stage, i, total)

            def norm_2(b):
                apply_norm(b, 2, x2, x2_ready)

            def messages_1(b, t):
                wait(dve, (x2b_ready, b))
                messages(b, bank3, t, mj1_l, mj1_h, mj1_hi, x1, x1b_ready, x2)

            def messages_3(b, t):
                messages(b, bank4, t, mj3_l, mj3_h, mj3_hi, x3, x3b_ready, x4)

            def values(b):
                wait(dve, bank3.filled("v", b))
                wait(dve, bank4.filled("o1", b - 1))
                nc.vector.tensor_tensor(v_s[:], bank3.half("v"), rows[:, BV, :].unsqueeze(1).broadcast_to([P, T, D]),
                                        ALU.add).then_inc(bank3.was_read("v", b)[0], 1)

            def attention_sum(b):
                wait(dve, bank4.filled("o", b))
                dve.wait_ge(x2b_ready, b + 1)
                wait(dve, (stored, 16 * b))
                nc.vector.tensor_tensor(x3[:], bank4.half("o"), x2b[:], ALU.add).then_inc(bank4.was_read("o", b)[0], 1)
                wait(dve, bank4.was_read("o", b))
                statistics(b, 4, 3, x3)

            def norm_3(b):
                apply_norm(b, 3, x3, x3_ready)

            def norm_4(b):
                apply_norm(b, 4, x4, x4_ready)

            def coefficients_1(b):
                coefficients(b, 1, bank1, P, f_hi, f_sel, g_query, g_key, "e3", g_ready)

            def coefficients_2(b):
                coefficients(b, 2, bank2, 4, f2_hi, f2_sel, g2_query, g2_key, "e", g2_ready)

            def x1t_lower(b):
                turned_lower(b, bank3, "xt", xrt_l[:], xrt_h[:], x1t_hi)

            def x2t_lower(b):
                turned_lower(b, bank3, "x2t", xrt_l[:], xrt_h[:], x2t_hi)

            def x3t_lower(b):
                turned_lower(b, bank4, "x3t", x3t_l[:], x3t_h[:], x3t_hi)

            def aggregate_1(b):
                aggregate(b, 3, bank3, 2, x2)

            def aggregate_3(b):
                aggregate(b, 4, bank4, 4, x4)

            def qk_lower(b, tile, dst, hi, bias, hi_ready):
                dve.wait_ge(hi_ready, b + 1)
                for m in range(K):
                    last = nc.vector.scalar_tensor_tensor(out=dst[:, m], in0=bank3.half(tile)[:, m], scalar=bias[:, m:m + 1],
                                                          in1=hi[:, m].bitcast(F32), op0=ALU.add, op1=ALU.subtract)
                last.then_inc(bank3.was_read(tile, b)[0], 1)

            def queries_lower(b):
                qk_lower(b, "q", q_l, q_h, bq_c, q_hi)

            def keys_lower(b):
                qk_lower(b, "k", k_l, k_h, bk_c, k_hi)

            def iteration(b1, b2, b3, b4):
                steps[:] = [0] * len(steps)
                on(b4, logits_3, 0)
                on(b4, logits_3, 1)
                on(b4, inverse_3, 0)
                on(b2, feats2_lower, 0)
                on(b1, feats_lower, 0, 0)
                on(b4, logits_3, 2)
                on(b1, feats_lower, 0, 1)
                on(b4, inverse_3, 1)
                on(b3, x1t_lower)
                on(b1, feats_lower, 1, 0)
                on(b1, feats_lower, 1, 1)
                on(b1, coefficients_1)
                on(b4, logits_3, 3)
                on(b4, inverse_3, 2)
                on(b1, logits_1, 0)
                on(b4, logits_3, 4)
                on(b4, inverse_3, 3)
                on(b2, feats2_lower, 1)
                on(b1, logits_1, 1)
                on(b1, inverse_1, 0)
                on(b4, logits_3, 5)
                on(b4, inverse_3, 4)
                on(b2, coefficients_2)
                on(b3, messages_1, 0)
                on(b4, logits_3, 6)
                on(b4, inverse_3, 5)
                on(b2, logits_2)
                on(b4, inverse_3, 6)
                on(b1, inverse_1, 1)
                on(b1, probs_t_lower_1, 0)
                on(b4, logits_3, 7)
                on(b2, inverse_2)
                on(b3, messages_1, 1)
                on(b4, inverse_3, 7)
                on(b1, logits_1, 2)
                on(b2, probs_t_lower_2)
                on(b3, aggregate_1)
                on(b1, elu_1, 0)
                on(b3, norm_2)
                on(b2, elu_2)
                on(b1, probs_t_lower_1, 1)
                on(b1, inverse_1, 2)
                on(b1, logits_1, 3)
                on(b4, attention_sum)
                on(b1, elu_1, 1)
                on(b4, norm_3)
                on(b3, x2t_lower)
                on(b1, probs_t_lower_1, 2)
                on(b1, inverse_1, 3)
                on(b4, x3t_lower)
                on(b2, feed_forward_sum)
                on(b1, elu_1, 2)
                on(b3, queries_lower)
                on(b4, messages_3, 0)
                on(b1, probs_t_lower_1, 3)
                on(b4, messages_3, 1)
                on(b2, norm_0)
                on(b3, keys_lower)
                on(b1, elu_1, 3)
                on(b4, aggregate_3)
                on(b2, stats_1)
                on(b3, values)
                on(b2, norm_1)
                on(b4, norm_4)
                for stage, b in enumerate((b1, b2, b3, b4)):
                    assert b is None or steps[stage] == DVE_STEPS[stage], steps

            pipeline(dve, iteration, before)

        @block.tensor
        def _(pe):
            def before(stage):
                if stage == 1:
                    pe.wait_ge(wh_lo, 2)
                    pe.wait_ge(loaded_small, 16 * N_SMALL)
                if stage == 2:
                    pe.wait_ge(loaded_2, 16 * N_2)
                    pe.wait_ge(lo_2, KH // K)
                    pe.wait_ge(wa2_ready, 1)
                if stage == 3:
                    pe.wait_ge(hi_3, 5)
                    pe.wait_ge(lo_3, 3)
                    pe.wait_ge(l1_lo, 1)
                if stage == 4:
                    pe.wait_ge(loaded_4, 16 * N_4)
                    pe.wait_ge(lo_4, 1)
                    pe.wait_ge(deg_ready, 1)

            def product3(out_ap, stat, mov, tiles=K):
                n = 0
                for k in range(tiles):
                    for a, c in ((stat[0], mov[0]), (stat[0], mov[1]), (stat[1], mov[0])):
                        ins = nc.tensor.matmul(out_ap, a(k), c(k), start=(n == 0), stop=(n == 3 * tiles - 1))
                        n += 1
                return ins

            def parts(hi, lo, cut=slice(None)):
                return (lambda k: hi[:, k, cut]), (lambda k: lo[:, k, cut])

            def rows_cut(t):
                return slice(t * P, (t + 1) * P)

            def transposes(b, bank, tile, src):
                for t in range(2):
                    for k in range(2):
                        ins = nc.tensor.transpose(bank.half(tile)[:, k, rows_cut(t)], src[:, t, rows_cut(k)], ident[:])
                ins.then_inc(bank.filled(tile, b)[0], 1)

            def project_1(b, t, half):
                tile = f"wh{t}{half}"
                pe.wait_ge(xt_lo, b + 1)
                wait(pe, bank1.vacant(tile, b))
                product3(bank1.ap(tile)[:], parts(xt_h, xt_l, rows_cut(t)),
                         parts(wh_h, wh_l, slice(half * 512, (half + 1) * 512))).then_inc(bank1.filled(tile, b)[0], 1)

            def coeff_rows_1(b):
                pe.wait_ge(wa_ready, 1)
                wait(pe, bank1.vacant("f", b))
                product3(bank1.ap("f")[:, 0:N], parts(wa_h, wa_l), parts(xt_h, xt_l)).then_inc(bank1.filled("f", b)[0], 1)

            def pair_sums(b, bank, tile, gq, gk, at, ready):
                pe.wait_ge(ready, b + 1)
                wait(pe, bank.vacant(tile, b))
                for t in range(T):
                    ins = nc.tensor.matmul(bank.half(tile)[:, t], gq[at:at + 4, rows_cut(t)], gk[at:at + 4, :],
                                           start=True, stop=True, tile_position=(at, 0))
                ins.then_inc(bank.filled(tile, b)[0], 1)

            def pairs_1(b, h):
                pair_sums(b, bank1, f"e{h}", g_query, g_key, 32 * h, g_ready)

            def pairs_2(b):
                pair_sums(b, bank2, "e", g2_query, g2_key, 0, g2_ready)

            def turn_probs(b, bank, tile, probs, ready):
                wait(pe, ready)
                wait(pe, bank.vacant(tile, b))
                transposes(b, bank, tile, probs)

            def turn_1(b, h):
                turn_probs(b, bank1, f"t{h}", p1[:, h % 2], (probs1_ready, b * H + h + 1))

            def turn_2(b):
                turn_probs(b, bank2, "t", p2, (probs2_ready, b + 1))

            def turn_3(b, h):
                turn_probs(b, bank4, f"t{h}", p3[:, h % R3], (probs3_ready, b * HM + h + 1))

            def attend_t(b, bank, tile, turned, feats_of, probs_of):
                bank.wait_read(pe, b, turned, into=tile)
                for m in range(K):
                    ins = product3(bank.half(tile)[:, m], feats_of(m), probs_of)
                ins.then_inc(bank.filled(tile, b)[0], 1)

            def attend_1(b, h):
                attend_t(b, bank1, f"av{h}", f"t{h}",
                         lambda m: parts(feats_h, feats_l, slice(h * D + m * P, h * D + (m + 1) * P)),
                         parts(pt1_h[:, h % 2], pt1_l[:, h % 2]))

            def attend_2(b):
                attend_t(b, bank2, "av", "t", lambda m: parts(feats2_h, feats2_l, rows_cut(m)), parts(pt2_h, pt2_l))

            def project_2(b, t):
                pe.wait_ge(heads_lo, (b + 1) * H)
                wait(pe, bank2.vacant(f"wh{t}", b))
                product3(bank2.ap(f"wh{t}")[:, 0:D + 4], parts(heads_h, heads_l, rows_cut(t)), parts(wout_h, wout_l),
                         tiles=KH).then_inc(bank2.filled(f"wh{t}", b)[0], 1)

            def coeff_rows_2(b):
                wait(pe, bank2.was_read("wh0", b))
                wait(pe, bank2.was_read("wh1", b))
                for t in range(T):
                    ins = nc.tensor.transpose(bank2.ap("f")[0:4, rows_cut(t)], coeff2[:, t], ident[:])
                ins.then_inc(bank2.filled("f", b)[0], 1)

            def feed_forward_1(b):
                bank2.wait_read(pe, b, "av", into="hid")
                for m in range(K):
                    for k in range(K):
                        ins = nc.tensor.matmul(bank2.half("hid")[:, m], w1_s[:, k, rows_cut(m)], out2_t[:, k],
                                               start=(k == 0), stop=(k == K - 1))
                ins.then_inc(bank2.filled("hid", b)[0], 1)

            def feed_forward_2(b):
                bank2.wait_read(pe, b, "hid", into="y")
                for t in range(T):
                    for c in range(K):
                        part = bank2.half("y")[:, t, rows_cut(c)]
                        for k in range(K):
                            nc.tensor.matmul(part, hid[:, k, rows_cut(t)], w2_s[:, k, rows_cut(c)],
                                             start=(k == 0), stop=False)
                        ins = nc.tensor.matmul(part, out2_t[:, c, rows_cut(t)], ident[:], start=False, stop=True)
                ins.then_inc(bank2.filled("y", b)[0], 1)

            def turn_rows(b, bank, tile, src, ready):
                wait(pe, ready)
                wait(pe, bank.vacant(tile, b))
                transposes(b, bank, tile, src)

            def own_and_messages(b, bank, t, rows_h, rows_l, turned, w_h, w_l):
                bank.wait_read(pe, b, turned, into=f"m{t}")
                product3(bank.ap(f"m{t}")[:], parts(rows_h, rows_l, rows_cut(t)), parts(w_h, w_l))\
                    .then_inc(bank.filled(f"m{t}", b)[0], 1)

            def aggregate(b, bank, mj_h, mj_l):
                bank.wait_read(pe, b, "m0", "m1", into="a")
                for t in range(T):
                    n = 0
                    for k in range(T):
                        for part in (mj_h, mj_l):
                            ins = nc.tensor.matmul(bank.half("a")[:, t], adjt_r[:, k, rows_cut(t)], part[:, k],
                                                   start=(n == 0), stop=(n == 2 * T - 1))
                            n += 1
                ins.then_inc(bank.filled("a", b)[0], 1)

            def project_qk(b, tile, which):
                bank3.wait_read(pe, b, "x2t", into=tile)
                for m in range(K):
                    ins = product3(bank3.half(tile)[:, m],
                                   parts(qkv_h[:, which], qkv_l[:, which], rows_cut(m)), parts(xrt_h, xrt_l))
                ins.then_inc(bank3.filled(tile, b)[0], 1)

            def project_v(b):
                wait(pe, bank3.vacant("v", b))
                for t in range(T):
                    ins = product3(bank3.half("v")[:, t], parts(xrt_h, xrt_l, rows_cut(t)),
                                   parts(qkv_h[:, 2], qkv_l[:, 2]))
                ins.then_inc(bank3.filled("v", b)[0], 1)

            def scores(b, h):
                if h == 0:
                    wait(pe, bank3.was_read("q", b))
                    wait(pe, bank3.was_read("k", b))
                wait(pe, bank4.vacant(f"s{h}", b))
                j, at = h // (P // DH), DH * (h % (P // DH))
                for t in range(T):
                    for n, (q, k) in enumerate(((q_h, k_h), (q_h, k_l), (q_l, k_h))):
                        ins = nc.tensor.matmul(bank4.half(f"s{h}")[:, t], q[at:at + DH, j, rows_cut(t)],
                                               k[at:at + DH, j], start=(n == 0), stop=(n == 2), tile_position=(at, 0))
                ins.then_inc(bank4.filled(f"s{h}", b)[0], 1)

            def attend_3(b, g):
                if g == 0:
                    wait(pe, bank3.was_read("v", b))
                bank4.wait_read(pe, b, *(f"t{h}" for h in range(4 * g, 4 * g + 4)), into=f"o{g}")
                for k in range(T):
                    for j in range(4):
                        h = 4 * g + j
                        ins = nc.tensor.matmul(bank4.ap(f"o{g}")[32 * j:32 * j + 32, 0:N],
                                               v_s[:, k, h * DH:(h + 1) * DH], pt3[:, h % PT3, k],
                                               start=(k == 0), stop=(k == T - 1), tile_position=(0, 32 * j))
                ins.then_inc(bank4.filled(f"o{g}", b)[0], 1)

            def project_o(b):
                bank4.wait_read(pe, b, "o0", "o1", into="o")
                for t in range(T):
                    for k in range(K):
                        ins = nc.tensor.matmul(bank4.half("o")[:, t], att_t[:, k, rows_cut(t)], wo_s[:, k],
                                               start=(k == 0), stop=(k == K - 1))
                ins.then_inc(bank4.filled("o", b)[0], 1)

            def turn_x1(b):
                turn_rows(b, bank3, "xt", x1, (x1_ready, b + 1))

            def turn_x2(b):
                turn_rows(b, bank3, "x2t", x2, (x2_ready, b + 1))

            def turn_x3(b):
                turn_rows(b, bank4, "x3t", x3, (x3_ready, b + 1))

            def own_and_messages_1(b, t):
                own_and_messages(b, bank3, t, xrt_h, xrt_l, "xt", l1_h, l1_l)

            def own_and_messages_3(b, t):
                own_and_messages(b, bank4, t, x3t_h, x3t_l, "x3t", l3_h, l3_l)

            def aggregate_1(b):
                aggregate(b, bank3, mj1_h, mj1_l)

            def aggregate_3(b):
                aggregate(b, bank4, mj3_h, mj3_l)

            def iteration(b1, b2, b3, b4):
                on(b4, scores, 0)
                on(b4, scores, 1)
                on(b4, scores, 2)
                on(b2, project_2, 0)
                on(b3, turn_x1)
                on(b1, project_1, 0, 0)
                on(b1, project_1, 0, 1)
                on(b1, project_1, 1, 0)
                on(b1, project_1, 1, 1)
                on(b1, coeff_rows_1)
                on(b4, turn_3, 0)
                on(b4, scores, 3)
                on(b4, scores, 4)
                on(b4, turn_3, 1)
                on(b1, pairs_1, 0)
                on(b2, project_2, 1)
                on(b1, pairs_1, 1)
                on(b4, scores, 5)
                on(b4, turn_3, 2)
                on(b2, coeff_rows_2)
                on(b3, own_and_messages_1, 0)
                on(b4, scores, 6)
                on(b4, turn_3, 3)
                on(b1, turn_1, 0)
                on(b2, pairs_2)
                on(b4, turn_3, 4)
                on(b3, own_and_messages_1, 1)
                on(b4, scores, 7)
                on(b4, turn_3, 5)
                on(b1, pairs_1, 2)
                on(b4, attend_3, 0)
                on(b1, attend_1, 0)
                on(b3, aggregate_1)
                on(b2, turn_2)
                on(b4, turn_3, 6)
                on(b4, turn_3, 7)
                on(b1, turn_1, 1)
                on(b1, pairs_1, 3)
                on(b4, attend_3, 1)
                on(b2, attend_2)
                on(b4, project_o)
                on(b3, turn_x2)
                on(b2, feed_forward_1)
                on(b1, attend_1, 1)
                on(b1, turn_1, 2)
                on(b2, feed_forward_2)
                on(b4, turn_x3)
                on(b3, project_qk, "q", 0)
                on(b1, attend_1, 2)
                on(b4, own_and_messages_3, 0)
                on(b1, turn_1, 3)
                on(b4, own_and_messages_3, 1)
                on(b3, project_qk, "k", 1)
                on(b1, attend_1, 3)
                on(b4, aggregate_3)
                on(b3, project_v)

            pipeline(pe, iteration, before)


def kernel(**inputs):
    import numpy as _np
    import concourse.bacc as _bacc
    from concourse import mybir as _mybir
    from concourse.bass_utils import run_bass_kernel_spmd as _run

    x = _np.asarray(inputs["x"])
    adj = _np.asarray(inputs["adj"])
    row = _np.arange(P) % 32
    select = _np.stack([(row == 1) | (row == 3), _np.select([(row == 0) | (row == 2), (row == 1) | (row == 3)], [1, -1], 0),
                        (row == 0) | (row == 1), (row == 2) | (row == 3)], axis=1).astype(_np.float32)
    def vectors(names, shape):
        return _np.stack([_np.asarray(inputs[n]).reshape(shape) for n in names])

    given = [
        ("x", x), ("xt", x.transpose(0, 2, 1)), ("adj", adj), ("adjt", adj.T),
        ("w_heads", inputs["L0_gnn_W_heads"]), ("a_heads", inputs["L0_gnn_a_heads"]),
        ("w_out", inputs["L0_gnn_W_out"]), ("a_out", inputs["L0_gnn_a_out"]),
        ("w1", inputs["L0_gnn_w1"]), ("w2", inputs["L0_gnn_w2"]), ("l1_wt", _np.asarray(inputs["L1_gnn_W"]).T),
        ("wq_t", _np.asarray(inputs["L2_gnn_Wq"]).T), ("wk_t", _np.asarray(inputs["L2_gnn_Wk"]).T),
        ("wv_t", _np.asarray(inputs["L2_gnn_Wv"]).T), ("wo_t", _np.asarray(inputs["L2_gnn_Wo"]).T),
        ("l3_wt", _np.asarray(inputs["L3_gnn_W"]).T),
        ("row_vectors", vectors(("L0_gnn_ln_gamma", "L0_gnn_ln_beta", "L0_gnn_b2", "L2_gnn_bo", "L2_gnn_bv"), (-1,))),
        ("l1_b", inputs["L1_gnn_b"]), ("l3_b", inputs["L3_gnn_b"]),
        ("column_vectors", vectors(("L0_gnn_b1", "L2_gnn_bq", "L2_gnn_bk"), (-1, P)).transpose(2, 0, 1)),
        ("ident", _np.eye(P, dtype=_np.float32)), ("select", select),
    ]
    nc = _bacc.Bacc("TRN2", target_bir_lowering=False, num_devices=1)
    arrays, args = {}, []
    for name, a in given:
        a = _np.ascontiguousarray(a)
        arrays[f"in_{name}_dram"] = a
        args.append(nc.dram_tensor(f"in_{name}_dram", a.shape, _mybir.dt.from_np(a.dtype), kind="ExternalInput").ap())
    args.append(nc.dram_tensor("out_dram", x.shape, _mybir.dt.from_np(x.dtype), kind="ExternalOutput").ap())
    build(nc, *args)
    r = _run(nc, [arrays], core_ids=[0])
    return r.results[0]["out_dram"]
```
